# Optimizing a Trainium2 kernel written in Bass

```python
import numpy as np
import jax
import jax.numpy as jnp

def _softmax(x, axis=-1):
    return jax.nn.softmax(x, axis=axis)

def _gelu(x):
    return jax.nn.gelu(x, approximate=True)

def _silu(x):
    return jax.nn.silu(x)

def _sigmoid(x):
    return jax.nn.sigmoid(x)

def _layernorm(x, axis=-1, eps=1e-05):
    m = jnp.mean(x, axis=axis, keepdims=True)
    v = jnp.var(x, axis=axis, keepdims=True)
    return (x - m) / jnp.sqrt(v + eps)

def _scatter_add(tgt, idx, src, axis=0):
    return tgt.at[idx].add(src)

def _segment_sum(src, seg, n):
    return jax.ops.segment_sum(src, seg, n)
kernel_name = 'mk_perceiver_d2_seqx_r4_d8636a'

def setup_inputs(seed: int=0):
    np.random.seed(seed)
    _w = jnp.asarray

    def _rec_inputs():
        import jax
        import jax.numpy as jnp
        _rk = jax.random.key(seed)
        x = -0.0002928 + 1 * jax.random.normal(jax.random.fold_in(_rk, 1), (4, 256, 256), jnp.float32)
        _lenS = 256 - jax.random.randint(jax.random.fold_in(_rk, 7), (4,), 0, max(1, 256 // 4) + 1, jnp.int32)
        _lenS2 = 4096 - jax.random.randint(jax.random.fold_in(_rk, 8), (4,), 0, max(1, 4096 // 4) + 1, jnp.int32)
        _ctx_1024P = jax.random.normal(jax.random.fold_in(_rk, 11), (4, 16, 256), jnp.float32)
        _ctx_1024c = jax.random.dirichlet(jax.random.fold_in(_rk, 511), 0.3 * jnp.ones((16,), jnp.float32), (4, 4096))
        _ctx_1024t = jnp.einsum('bsk,bkd->bsd', _ctx_1024c, _ctx_1024P)
        _ctx_1024t = _ctx_1024t * jax.lax.rsqrt(jnp.mean(jnp.square(_ctx_1024t)) + 1e-12) * 0.953939
        ctx_1024 = -1.39393e-06 + 0.999914 * (_ctx_1024t + 0.3 * jax.random.normal(jax.random.fold_in(_rk, 611), (4, 4096, 256), jnp.float32))
        _validS = jnp.arange(256)[None, :] < _lenS[:, None]
        _validS2 = jnp.arange(4096)[None, :] < _lenS2[:, None]
        _causal = jnp.tril(jnp.ones((256, 256), dtype=bool))
        mask_BxS2_bk0 = jnp.logical_not(jnp.broadcast_to(_validS2[:, :], (4, 4096)))
        return (x, ctx_1024, mask_BxS2_bk0)
    x, ctx_1024, mask_BxS2_bk0 = _rec_inputs()

    def _L0_xattn_setup():
        import jax, jax.numpy as jnp
        import numpy as np
        import math
        H = 16
        DH = 64
        NV = 256
        B, S = (2, 512)

        def _trans_qkv(x, num_heads):
            b, s, hd = x.shape
            x = x.reshape(b, s, num_heads, hd // num_heads)
            x = jnp.transpose(x, (0, 2, 1, 3))
            return x.reshape(b * num_heads, s, hd // num_heads)

        def _re_trans_qkv(x, num_heads):
            bh, s, d = x.shape
            x = x.reshape(bh // num_heads, num_heads, s, d)
            x = jnp.transpose(x, (0, 2, 1, 3))
            return x.reshape(bh // num_heads, s, num_heads * d)
        key = jax.random.key(seed)
        ks = jax.random.split(key, 7)
        sc = 1.0 / math.sqrt(NV)
        return {'Sq': jax.random.normal(ks[0], (B, S, NV), jnp.float32), 'Sk': jax.random.normal(ks[1], (B, S, NV), jnp.float32), 'Sv': jax.random.normal(ks[2], (B, S, NV), jnp.float32), 'Wq_w': jax.random.normal(ks[3], (H * DH, NV), jnp.float32) * sc, 'Wq_b': jax.random.normal(ks[4], (H * DH,), jnp.float32) * sc, 'out_w': jax.random.normal(ks[5], (NV, H * DH), jnp.float32) * sc, 'out_b': jax.random.normal(ks[6], (NV,), jnp.float32) * sc}
    _L0_xattn_all = _L0_xattn_setup()
    _L0_xattn_in = {k: v for k, v in _L0_xattn_all.items() if k in ('Wq_w', 'Wq_b', 'out_w', 'out_b')}
    del _L0_xattn_all

    def _L0_attn_setup():
        import jax, jax.numpy as jnp
        import numpy as np
        T, B, E, H = (256, 2, 256, 16)
        D = E // H
        R = 2 * T - 1

        def _rel_shift(x):
            b, h, q, r = x.shape
            zp = jnp.zeros((b, h, q, 1), x.dtype)
            xp = jnp.concatenate([zp, x], axis=3)
            xp = xp.reshape(b, h, r + 1, q)[:, :, 1:, :]
            return xp.reshape(b, h, q, r)
        key = jax.random.key(seed)
        ks = jax.random.split(key, 8)
        std = (2.0 / (E + E)) ** 0.5
        return {'x': jax.random.normal(ks[0], (T, B, E), jnp.float32), 'pos': jax.random.normal(ks[1], (R, 1, E), jnp.float32), 'in_proj_weight': jax.random.normal(ks[2], (3 * E, E), jnp.float32) * std, 'in_proj_bias': jnp.zeros((3 * E,), jnp.float32), 'pos_proj_weight': jax.random.normal(ks[3], (E, E), jnp.float32) * std, 'pos_proj_bias': jnp.zeros((E,), jnp.float32), 'out_proj_weight': jax.random.normal(ks[4], (E, E), jnp.float32) * std, 'out_proj_bias': jnp.zeros((E,), jnp.float32), 'r_w_bias': jax.random.normal(ks[5], (H, D), jnp.float32) * 0.02, 'r_r_bias': jax.random.normal(ks[6], (H, D), jnp.float32) * 0.02}
    _L0_attn_all = _L0_attn_setup()
    _L0_attn_in = {k: v for k, v in _L0_attn_all.items() if k in ('pos', 'in_proj_weight', 'in_proj_bias', 'pos_proj_weight', 'pos_proj_bias', 'out_proj_weight', 'out_proj_bias', 'r_w_bias', 'r_r_bias')}
    del _L0_attn_all

    def _L0_ffn_setup():
        import jax, jax.numpy as jnp
        import numpy as np
        B, T, C = (2, 256, 256)
        H = 1024
        E_R, E_S, K = (8, 2, 2)

        def _rmsnorm(x, g):
            eps = jnp.finfo(x.dtype).eps
            return x * jax.lax.rsqrt(jnp.mean(x * x, axis=-1, keepdims=True) + eps) * g

        def _experts_mlp(x, g, W1, b1, W2, b2):
            xn = _rmsnorm(x, g)
            h = jnp.einsum('btc,ech->bteh', xn, W1) + b1
            h = jax.nn.gelu(h, approximate=False)
            return jnp.einsum('bteh,ehc->btec', h, W2) + b2
        key = jax.random.key(seed)
        ks = jax.random.split(key, 12)
        s = 0.02
        return {'u': jax.random.normal(ks[0], (B, T, C), dtype=jnp.float32), 'g_shared': jnp.ones((C,), jnp.float32), 'W1_s': jax.random.normal(ks[1], (E_S, C, H), jnp.float32) * s, 'b1_s': jax.random.normal(ks[2], (E_S, H), jnp.float32) * s, 'W2_s': jax.random.normal(ks[3], (E_S, H, C), jnp.float32) * s, 'b2_s': jax.random.normal(ks[4], (E_S, C), jnp.float32) * s, 'g_routed': jnp.ones((C,), jnp.float32), 'W1_r': jax.random.normal(ks[5], (E_R, C, H), jnp.float32) * s, 'b1_r': jax.random.normal(ks[6], (E_R, H), jnp.float32) * s, 'W2_r': jax.random.normal(ks[7], (E_R, H, C), jnp.float32) * s, 'b2_r': jax.random.normal(ks[8], (E_R, C), jnp.float32) * s, 'centroids': jax.random.normal(ks[9], (C, E_R), jnp.float32) * s}
    _L0_ffn_all = _L0_ffn_setup()
    _L0_ffn_in = {k: v for k, v in _L0_ffn_all.items() if k in ('g_shared', 'W1_s', 'b1_s', 'W2_s', 'b2_s', 'g_routed', 'W1_r', 'b1_r', 'W2_r', 'b2_r', 'centroids')}
    del _L0_ffn_all

    def _L1_xattn_setup():
        import jax, jax.numpy as jnp
        import numpy as np
        B, TQ, TK, D, H = (2, 512, 512, 256, 16)
        HD = D // H
        NUM_PAD = 64
        key = jax.random.key(seed)
        ks = jax.random.split(key, 8)
        s = 0.02
        q = jax.random.normal(ks[0], (B, TQ, D), dtype=jnp.float32)
        kv = jax.random.normal(ks[1], (B, TK, D), dtype=jnp.float32)
        key_padding_mask = jnp.broadcast_to(jnp.arange(TK) >= TK - NUM_PAD, (B, TK))
        Wq = jax.random.normal(ks[2], (D, D), dtype=jnp.float32) * s
        bq = jax.random.normal(ks[3], (D,), dtype=jnp.float32) * s
        Wkv = jax.random.normal(ks[4], (D, 2 * D), dtype=jnp.float32) * s
        bkv = jax.random.normal(ks[5], (2 * D,), dtype=jnp.float32) * s
        Wo = jax.random.normal(ks[6], (D, D), dtype=jnp.float32) * s
        bo = jax.random.normal(ks[7], (D,), dtype=jnp.float32) * s
        return {'q': q, 'kv': kv, 'key_padding_mask': key_padding_mask, 'Wq': Wq, 'bq': bq, 'Wkv': Wkv, 'bkv': bkv, 'Wo': Wo, 'bo': bo}
    _L1_xattn_all = _L1_xattn_setup()
    _L1_xattn_in = {k: v for k, v in _L1_xattn_all.items() if k in ('Wq', 'bq', 'Wkv', 'bkv', 'Wo', 'bo')}
    del _L1_xattn_all

    def _L1_attn_setup():
        import jax, jax.numpy as jnp
        import numpy as np
        D_MODEL = 256
        NUM_HEADS = 16
        HEAD_DIM = D_MODEL // NUM_HEADS
        D_FF = 1024
        EPS = 1e-05

        def layer_norm(x, gamma, beta):
            mu = jnp.mean(x, axis=-1, keepdims=True)
            var = jnp.mean((x - mu) ** 2, axis=-1, keepdims=True)
            return (x - mu) * jax.lax.rsqrt(var + EPS) * gamma + beta

        def apply_rope(t):
            S, d = (t.shape[-2], t.shape[-1])
            inv_freq = 1.0 / 10000.0 ** (jnp.arange(0, d, 2, dtype=jnp.float32) / d)
            angles = jnp.arange(S, dtype=jnp.float32)[:, None] * inv_freq[None, :]
            sin, cos = (jnp.sin(angles), jnp.cos(angles))
            tp = t.reshape(*t.shape[:-1], d // 2, 2)
            t0, t1 = (tp[..., 0], tp[..., 1])
            rot = jnp.stack([t0 * cos - t1 * sin, t0 * sin + t1 * cos], axis=-1)
            return rot.reshape(t.shape)
        key = jax.random.key(seed)
        ks = jax.random.split(key, 18)
        s = 0.02
        d, f = (D_MODEL, D_FF)
        return {'x': jax.random.normal(ks[0], (2, 512, d), dtype=jnp.float32), 'Wq': jax.random.normal(ks[1], (d, d), dtype=jnp.float32) * s, 'bq': jnp.zeros((d,), jnp.float32), 'Wk': jax.random.normal(ks[2], (d, d), dtype=jnp.float32) * s, 'bk': jnp.zeros((d,), jnp.float32), 'Wv': jax.random.normal(ks[3], (d, d), dtype=jnp.float32) * s, 'bv': jnp.zeros((d,), jnp.float32), 'Wo': jax.random.normal(ks[4], (d, d), dtype=jnp.float32) * s, 'bo': jnp.zeros((d,), jnp.float32), 'W1': jax.random.normal(ks[5], (d, f), dtype=jnp.float32) * s, 'b1': jnp.zeros((f,), jnp.float32), 'W2': jax.random.normal(ks[6], (f, d), dtype=jnp.float32) * s, 'b2': jnp.zeros((d,), jnp.float32), 'g1': jnp.ones((d,), jnp.float32), 'beta1': jnp.zeros((d,), jnp.float32), 'g2': jnp.ones((d,), jnp.float32), 'beta2': jnp.zeros((d,), jnp.float32)}
    _L1_attn_all = _L1_attn_setup()
    _L1_attn_in = {k: v for k, v in _L1_attn_all.items() if k in ('Wq', 'bq', 'Wk', 'bk', 'Wv', 'bv', 'Wo', 'bo', 'W1', 'b1', 'W2', 'b2', 'g1', 'beta1', 'g2', 'beta2')}
    del _L1_attn_all

    def _L1_ffn_setup():
        import jax, jax.numpy as jnp
        import numpy as np
        H = 16
        EPS = 1e-05

        def layernorm(x, g, b):
            m = jnp.mean(x, axis=-1, keepdims=True)
            v = jnp.mean((x - m) ** 2, axis=-1, keepdims=True)
            return (x - m) * jax.lax.rsqrt(v + EPS) * g + b
        key = jax.random.key(seed)
        B, S, D, E = (4, 512, 256, 8)
        ks = jax.random.split(key, 16)
        s = 0.02
        inp = {'x': jax.random.normal(ks[0], (B, S, D), jnp.float32), 'Wq': jax.random.normal(ks[1], (D, D), jnp.float32) * s, 'bq': jnp.zeros((D,), jnp.float32), 'Wk': jax.random.normal(ks[2], (D, D), jnp.float32) * s, 'bk': jnp.zeros((D,), jnp.float32), 'Wv': jax.random.normal(ks[3], (D, D), jnp.float32) * s, 'bv': jnp.zeros((D,), jnp.float32), 'Wo': jax.random.normal(ks[4], (D, D), jnp.float32) * s, 'bo': jnp.zeros((D,), jnp.float32), 'g1': jnp.ones((D,), jnp.float32), 'be1': jnp.zeros((D,), jnp.float32), 'g2': jnp.ones((D,), jnp.float32), 'be2': jnp.zeros((D,), jnp.float32), 'Wg': jax.random.normal(ks[5], (D, E), jnp.float32) * s, 'bg': jnp.zeros((E,), jnp.float32), 'We': jax.random.normal(ks[6], (E, D, D), jnp.float32) * s, 'bexp': jnp.zeros((E, D), jnp.float32)}
        return inp
    _L1_ffn_all = _L1_ffn_setup()
    _L1_ffn_in = {k: v for k, v in _L1_ffn_all.items() if k in ('Wq', 'bq', 'Wk', 'bk', 'Wv', 'bv', 'Wo', 'bo', 'g1', 'be1', 'g2', 'be2', 'Wg', 'bg', 'We', 'bexp')}
    del _L1_ffn_all
    return {'x': x, 'ctx_1024': ctx_1024, 'mask_BxS2_bk0': mask_BxS2_bk0, 'L0_xattn_Wq_w': _L0_xattn_in['Wq_w'], 'L0_xattn_Wq_b': _L0_xattn_in['Wq_b'], 'L0_xattn_out_w': _L0_xattn_in['out_w'], 'L0_xattn_out_b': _L0_xattn_in['out_b'], 'L0_attn_pos': _L0_attn_in['pos'], 'L0_attn_in_proj_weight': _L0_attn_in['in_proj_weight'], 'L0_attn_in_proj_bias': _L0_attn_in['in_proj_bias'], 'L0_attn_pos_proj_weight': _L0_attn_in['pos_proj_weight'], 'L0_attn_pos_proj_bias': _L0_attn_in['pos_proj_bias'], 'L0_attn_out_proj_weight': _L0_attn_in['out_proj_weight'], 'L0_attn_out_proj_bias': _L0_attn_in['out_proj_bias'], 'L0_attn_r_w_bias': _L0_attn_in['r_w_bias'], 'L0_attn_r_r_bias': _L0_attn_in['r_r_bias'], 'L0_ffn_g_shared': _L0_ffn_in['g_shared'], 'L0_ffn_W1_s': _L0_ffn_in['W1_s'], 'L0_ffn_b1_s': _L0_ffn_in['b1_s'], 'L0_ffn_W2_s': _L0_ffn_in['W2_s'], 'L0_ffn_b2_s': _L0_ffn_in['b2_s'], 'L0_ffn_g_routed': _L0_ffn_in['g_routed'], 'L0_ffn_W1_r': _L0_ffn_in['W1_r'], 'L0_ffn_b1_r': _L0_ffn_in['b1_r'], 'L0_ffn_W2_r': _L0_ffn_in['W2_r'], 'L0_ffn_b2_r': _L0_ffn_in['b2_r'], 'L0_ffn_centroids': _L0_ffn_in['centroids'], 'L1_xattn_Wq': _L1_xattn_in['Wq'], 'L1_xattn_bq': _L1_xattn_in['bq'], 'L1_xattn_Wkv': _L1_xattn_in['Wkv'], 'L1_xattn_bkv': _L1_xattn_in['bkv'], 'L1_xattn_Wo': _L1_xattn_in['Wo'], 'L1_xattn_bo': _L1_xattn_in['bo'], 'L1_attn_Wq': _L1_attn_in['Wq'], 'L1_attn_bq': _L1_attn_in['bq'], 'L1_attn_Wk': _L1_attn_in['Wk'], 'L1_attn_bk': _L1_attn_in['bk'], 'L1_attn_Wv': _L1_attn_in['Wv'], 'L1_attn_bv': _L1_attn_in['bv'], 'L1_attn_Wo': _L1_attn_in['Wo'], 'L1_attn_bo': _L1_attn_in['bo'], 'L1_attn_W1': _L1_attn_in['W1'], 'L1_attn_b1': _L1_attn_in['b1'], 'L1_attn_W2': _L1_attn_in['W2'], 'L1_attn_b2': _L1_attn_in['b2'], 'L1_attn_g1': _L1_attn_in['g1'], 'L1_attn_beta1': _L1_attn_in['beta1'], 'L1_attn_g2': _L1_attn_in['g2'], 'L1_attn_beta2': _L1_attn_in['beta2'], 'L1_ffn_Wq': _L1_ffn_in['Wq'], 'L1_ffn_bq': _L1_ffn_in['bq'], 'L1_ffn_Wk': _L1_ffn_in['Wk'], 'L1_ffn_bk': _L1_ffn_in['bk'], 'L1_ffn_Wv': _L1_ffn_in['Wv'], 'L1_ffn_bv': _L1_ffn_in['bv'], 'L1_ffn_Wo': _L1_ffn_in['Wo'], 'L1_ffn_bo': _L1_ffn_in['bo'], 'L1_ffn_g1': _L1_ffn_in['g1'], 'L1_ffn_be1': _L1_ffn_in['be1'], 'L1_ffn_g2': _L1_ffn_in['g2'], 'L1_ffn_be2': _L1_ffn_in['be2'], 'L1_ffn_Wg': _L1_ffn_in['Wg'], 'L1_ffn_bg': _L1_ffn_in['bg'], 'L1_ffn_We': _L1_ffn_in['We'], 'L1_ffn_bexp': _L1_ffn_in['bexp']}

def reference(x, ctx_1024, mask_BxS2_bk0, L0_xattn_Wq_w, L0_xattn_Wq_b, L0_xattn_out_w, L0_xattn_out_b, L0_attn_pos, L0_attn_in_proj_weight, L0_attn_in_proj_bias, L0_attn_pos_proj_weight, L0_attn_pos_proj_bias, L0_attn_out_proj_weight, L0_attn_out_proj_bias, L0_attn_r_w_bias, L0_attn_r_r_bias, L0_ffn_g_shared, L0_ffn_W1_s, L0_ffn_b1_s, L0_ffn_W2_s, L0_ffn_b2_s, L0_ffn_g_routed, L0_ffn_W1_r, L0_ffn_b1_r, L0_ffn_W2_r, L0_ffn_b2_r, L0_ffn_centroids, L1_xattn_Wq, L1_xattn_bq, L1_xattn_Wkv, L1_xattn_bkv, L1_xattn_Wo, L1_xattn_bo, L1_attn_Wq, L1_attn_bq, L1_attn_Wk, L1_attn_bk, L1_attn_Wv, L1_attn_bv, L1_attn_Wo, L1_attn_bo, L1_attn_W1, L1_attn_b1, L1_attn_W2, L1_attn_b2, L1_attn_g1, L1_attn_beta1, L1_attn_g2, L1_attn_beta2, L1_ffn_Wq, L1_ffn_bq, L1_ffn_Wk, L1_ffn_bk, L1_ffn_Wv, L1_ffn_bv, L1_ffn_Wo, L1_ffn_bo, L1_ffn_g1, L1_ffn_be1, L1_ffn_g2, L1_ffn_be2, L1_ffn_Wg, L1_ffn_bg, L1_ffn_We, L1_ffn_bexp):
    import jax
    import jax.numpy as jnp

    def _L0_xattn_ref(Sq, Sk, Sv, Wq_w, Wq_b, out_w, out_b):
        import jax, jax.numpy as jnp
        import numpy as np
        import math
        H = 16
        DH = 64
        NV = 256
        B, S = (2, 512)

        def _trans_qkv(x, num_heads):
            b, s, hd = x.shape
            x = x.reshape(b, s, num_heads, hd // num_heads)
            x = jnp.transpose(x, (0, 2, 1, 3))
            return x.reshape(b * num_heads, s, hd // num_heads)

        def _re_trans_qkv(x, num_heads):
            bh, s, d = x.shape
            x = x.reshape(bh // num_heads, num_heads, s, d)
            x = jnp.transpose(x, (0, 2, 1, 3))
            return x.reshape(bh // num_heads, s, num_heads * d)
        Q = Sq @ Wq_w.T + Wq_b
        K = Sk @ Wq_w.T + Wq_b
        V = Sv @ Wq_w.T + Wq_b
        Q1 = _trans_qkv(Q, H)
        K1 = _trans_qkv(K, H)
        V1 = _trans_qkv(V, H)
        d = Q1.shape[-1]
        qk = jnp.einsum('bqd,bkd->bqk', Q1, K1) / jnp.sqrt(jnp.float32(d))
        X1 = jax.nn.softmax(jnp.einsum('bqk,bkd->bqd', qk, V1), axis=-1)
        X = _re_trans_qkv(X1, H)
        return X @ out_w.T + out_b

    def _L0_attn_ref(x, pos, in_proj_weight, in_proj_bias, pos_proj_weight, pos_proj_bias, out_proj_weight, out_proj_bias, r_w_bias, r_r_bias):
        import jax, jax.numpy as jnp
        import numpy as np
        T, B, E, H = (256, 2, 256, 16)
        D = E // H
        R = 2 * T - 1

        def _rel_shift(x):
            b, h, q, r = x.shape
            zp = jnp.zeros((b, h, q, 1), x.dtype)
            xp = jnp.concatenate([zp, x], axis=3)
            xp = xp.reshape(b, h, r + 1, q)[:, :, 1:, :]
            return xp.reshape(b, h, q, r)
        t, b, e = x.shape
        h, d = r_w_bias.shape
        qkv = x @ in_proj_weight.T + in_proj_bias
        q, k, v = jnp.split(qkv, 3, axis=-1)
        q = q.reshape(t, b, h, d)
        k = k.reshape(t, b, h, d)
        v = v.reshape(t, b, h, d)
        p = (pos @ pos_proj_weight.T + pos_proj_bias).reshape(-1, h, d)
        scale = 1.0 / jnp.sqrt(jnp.asarray(d, x.dtype))
        ac = jnp.einsum('tbhd,sbhd->bhts', q + r_w_bias, k)
        bd = jnp.einsum('tbhd,rhd->bhtr', q + r_r_bias, p)
        bd = _rel_shift(bd)[..., :t]
        attn = jax.nn.softmax((ac + bd) * scale, axis=-1)
        ctx = jnp.einsum('bhts,sbhd->tbhd', attn, v).reshape(t, b, e)
        return ctx @ out_proj_weight.T + out_proj_bias

    def _L0_ffn_ref(u, g_shared, W1_s, b1_s, W2_s, b2_s, g_routed, W1_r, b1_r, W2_r, b2_r, centroids):
        import jax, jax.numpy as jnp
        import numpy as np
        B, T, C = (2, 256, 256)
        H = 1024
        E_R, E_S, K = (8, 2, 2)

        def _rmsnorm(x, g):
            eps = jnp.finfo(x.dtype).eps
            return x * jax.lax.rsqrt(jnp.mean(x * x, axis=-1, keepdims=True) + eps) * g

        def _experts_mlp(x, g, W1, b1, W2, b2):
            xn = _rmsnorm(x, g)
            h = jnp.einsum('btc,ech->bteh', xn, W1) + b1
            h = jax.nn.gelu(h, approximate=False)
            return jnp.einsum('bteh,ehc->btec', h, W2) + b2
        h_s = _experts_mlp(u, g_shared, W1_s, b1_s, W2_s, b2_s).sum(axis=-2)
        scores = jax.nn.sigmoid(u @ centroids)
        gpk, i_topk = jax.lax.top_k(scores, K)
        gk = gpk / scores.sum(axis=-1, keepdims=True)
        routed_all = _experts_mlp(u, g_routed, W1_r, b1_r, W2_r, b2_r)
        routed_topk = jnp.take_along_axis(routed_all, i_topk[..., None], axis=2)
        h_r = (gk[..., None] * routed_topk).sum(axis=-2)
        return u + h_s + h_r

    def _L1_xattn_ref(q, kv, key_padding_mask, Wq, bq, Wkv, bkv, Wo, bo):
        import jax, jax.numpy as jnp
        import numpy as np
        B, TQ, TK, D, H = (2, 512, 512, 256, 16)
        HD = D // H
        NUM_PAD = 64
        Bc, Tq, Dm = q.shape
        Tk = kv.shape[1]
        scale = HD ** (-0.5)
        Q = (q @ Wq + bq).reshape(Bc, Tq, H, HD).transpose(0, 2, 1, 3)
        KV = (kv @ Wkv + bkv).reshape(Bc, Tk, 2, H, HD).transpose(2, 0, 3, 1, 4)
        K, V = (KV[0], KV[1])
        attn = jnp.einsum('bhqd,bhkd->bhqk', Q, K) * scale
        attn = jnp.where(key_padding_mask[:, None, None, :], -jnp.inf, attn)
        attn = jax.nn.softmax(attn, axis=-1)
        out = jnp.einsum('bhqk,bhkd->bhqd', attn, V)
        out = out.transpose(0, 2, 1, 3).reshape(Bc, Tq, Dm)
        return out @ Wo + bo

    def _L1_attn_ref(x, Wq, bq, Wk, bk, Wv, bv, Wo, bo, W1, b1, W2, b2, g1, beta1, g2, beta2):
        import jax, jax.numpy as jnp
        import numpy as np
        D_MODEL = 256
        NUM_HEADS = 16
        HEAD_DIM = D_MODEL // NUM_HEADS
        D_FF = 1024
        EPS = 1e-05

        def layer_norm(x, gamma, beta):
            mu = jnp.mean(x, axis=-1, keepdims=True)
            var = jnp.mean((x - mu) ** 2, axis=-1, keepdims=True)
            return (x - mu) * jax.lax.rsqrt(var + EPS) * gamma + beta

        def apply_rope(t):
            S, d = (t.shape[-2], t.shape[-1])
            inv_freq = 1.0 / 10000.0 ** (jnp.arange(0, d, 2, dtype=jnp.float32) / d)
            angles = jnp.arange(S, dtype=jnp.float32)[:, None] * inv_freq[None, :]
            sin, cos = (jnp.sin(angles), jnp.cos(angles))
            tp = t.reshape(*t.shape[:-1], d // 2, 2)
            t0, t1 = (tp[..., 0], tp[..., 1])
            rot = jnp.stack([t0 * cos - t1 * sin, t0 * sin + t1 * cos], axis=-1)
            return rot.reshape(t.shape)
        B, S, d = x.shape
        H, hd = (NUM_HEADS, HEAD_DIM)
        x_norm = layer_norm(x, g1, beta1)
        q = (x_norm @ Wq + bq).reshape(B, S, H, hd).transpose(0, 2, 1, 3)
        k = (x_norm @ Wk + bk).reshape(B, S, H, hd).transpose(0, 2, 1, 3)
        v = (x_norm @ Wv + bv).reshape(B, S, H, hd).transpose(0, 2, 1, 3)
        q = apply_rope(q)
        k = apply_rope(k)
        q = q * (1.0 / jnp.sqrt(jnp.float32(hd)))
        scores = jnp.einsum('bhqd,bhkd->bhqk', q, k)
        attn = jax.nn.softmax(scores, axis=-1)
        out = jnp.einsum('bhqk,bhkd->bhqd', attn, v)
        out = out.transpose(0, 2, 1, 3).reshape(B, S, d)
        attn_out = out @ Wo + bo
        x = x + attn_out
        x_norm2 = layer_norm(x, g2, beta2)
        ffn = jax.nn.relu(x_norm2 @ W1 + b1) @ W2 + b2
        return x + ffn

    def _L1_ffn_ref(x, Wq, bq, Wk, bk, Wv, bv, Wo, bo, g1, be1, g2, be2, Wg, bg, We, bexp):
        import jax, jax.numpy as jnp
        import numpy as np
        H = 16
        EPS = 1e-05

        def layernorm(x, g, b):
            m = jnp.mean(x, axis=-1, keepdims=True)
            v = jnp.mean((x - m) ** 2, axis=-1, keepdims=True)
            return (x - m) * jax.lax.rsqrt(v + EPS) * g + b
        B, S, D = x.shape
        Dh = D // H
        TOP_K = 2
        q = (x @ Wq + bq).reshape(B, S, H, Dh)
        k = (x @ Wk + bk).reshape(B, S, H, Dh)
        v = (x @ Wv + bv).reshape(B, S, H, Dh)
        scores = jnp.einsum('bqhd,bkhd->bhqk', q, k) / jnp.sqrt(jnp.float32(Dh))
        attn = jax.nn.softmax(scores, axis=-1)
        ctx = jnp.einsum('bhqk,bkhd->bqhd', attn, v).reshape(B, S, D)
        attn_out = ctx @ Wo + bo
        x = x + layernorm(attn_out, g1, be1)
        gate_probs = jax.nn.softmax(x @ Wg + bg, axis=-1)
        top_vals, top_idx = jax.lax.top_k(gate_probs, TOP_K)
        all_out = jnp.einsum('bsd,edf->bsef', x, We) + bexp
        picked = jnp.take_along_axis(all_out, top_idx[..., None], axis=2)
        moe_out = jnp.sum(top_vals[..., None] * picked, axis=2)
        return x + layernorm(moe_out, g2, be2)
    x = x + _L0_xattn_ref(_layernorm(x, axis=-1), ctx_1024, ctx_1024, L0_xattn_Wq_w, L0_xattn_Wq_b, L0_xattn_out_w, L0_xattn_out_b)
    x = x + _L0_attn_ref(_layernorm(x, axis=-1), L0_attn_pos, L0_attn_in_proj_weight, L0_attn_in_proj_bias, L0_attn_pos_proj_weight, L0_attn_pos_proj_bias, L0_attn_out_proj_weight, L0_attn_out_proj_bias, L0_attn_r_w_bias, L0_attn_r_r_bias)
    x = x + _L0_ffn_ref(_layernorm(x, axis=-1), L0_ffn_g_shared, L0_ffn_W1_s, L0_ffn_b1_s, L0_ffn_W2_s, L0_ffn_b2_s, L0_ffn_g_routed, L0_ffn_W1_r, L0_ffn_b1_r, L0_ffn_W2_r, L0_ffn_b2_r, L0_ffn_centroids)
    x = x + _L1_xattn_ref(_layernorm(x, axis=-1), ctx_1024, mask_BxS2_bk0, L1_xattn_Wq, L1_xattn_bq, L1_xattn_Wkv, L1_xattn_bkv, L1_xattn_Wo, L1_xattn_bo)
    x = x + _L1_attn_ref(_layernorm(x, axis=-1), L1_attn_Wq, L1_attn_bq, L1_attn_Wk, L1_attn_bk, L1_attn_Wv, L1_attn_bv, L1_attn_Wo, L1_attn_bo, L1_attn_W1, L1_attn_b1, L1_attn_W2, L1_attn_b2, L1_attn_g1, L1_attn_beta1, L1_attn_g2, L1_attn_beta2)
    x = x + _L1_ffn_ref(_layernorm(x, axis=-1), L1_ffn_Wq, L1_ffn_bq, L1_ffn_Wk, L1_ffn_bk, L1_ffn_Wv, L1_ffn_bv, L1_ffn_Wo, L1_ffn_bo, L1_ffn_g1, L1_ffn_be1, L1_ffn_g2, L1_ffn_be2, L1_ffn_Wg, L1_ffn_bg, L1_ffn_We, L1_ffn_bexp)
    return x

_drawn_inputs = setup_inputs


def setup_inputs(seed=0):
    import zlib

    import numpy as np

    out = dict(_drawn_inputs(seed))
    spreads = {'L0_attn_in_proj_bias': (0.0, 0.1),
     'L0_attn_pos_proj_bias': (0.0, 2.0),
     'L0_attn_out_proj_bias': (0.0, 0.1),
     'L0_ffn_g_shared': (1.0, 0.6),
     'L0_ffn_g_routed': (1.0, 0.6),
     'L1_attn_bq': (0.0, 0.8),
     'L1_attn_bk': (0.0, 0.8),
     'L1_attn_bv': (0.0, 0.1),
     'L1_attn_bo': (0.0, 0.1),
     'L1_attn_b1': (0.0, 0.392),
     'L1_attn_b2': (0.0, 0.1),
     'L1_attn_g1': (1.0, 0.6),
     'L1_attn_beta1': (0.0, 0.8),
     'L1_attn_g2': (1.0, 0.6),
     'L1_attn_beta2': (0.0, 0.589),
     'L1_ffn_bq': (0.0, 0.8),
     'L1_ffn_bk': (0.0, 2.0),
     'L1_ffn_bv': (0.0, 0.1),
     'L1_ffn_bo': (0.0, 0.1),
     'L1_ffn_g1': (1.0, 0.2),
     'L1_ffn_be1': (0.0, 0.1),
     'L1_ffn_g2': (1.0, 0.2),
     'L1_ffn_be2': (0.0, 0.382),
     'L1_ffn_bg': (0.0, 0.1),
     'L1_ffn_bexp': (0.0, 0.1)}
    factors = {'L0_attn_r_w_bias': 4.827,
     'L0_attn_r_r_bias': 3.758,
     'L0_ffn_b1_s': 6.991,
     'L0_ffn_W1_r': 3.199,
     'L0_ffn_b1_r': 8.0,
     'L0_ffn_W2_r': 3.382,
     'L0_ffn_b2_r': 8.0,
     'L0_ffn_centroids': 3.249,
     'L1_xattn_Wq': 24.607,
     'L1_xattn_bq': 200.0,
     'L1_xattn_bkv': 3.815,
     'L1_xattn_bo': 2.777,
     'L1_attn_Wq': 8.0,
     'L1_attn_Wk': 8.0,
     'L1_attn_Wv': 3.897,
     'L1_ffn_Wq': 3.692,
     'L1_ffn_Wk': 3.618}
    for name, (base, spread) in spreads.items():
        noise = np.random.default_rng([zlib.crc32(name.encode()), seed]).standard_normal(out[name].shape)
        drawn = base * np.exp(spread * noise) if base else spread * noise
        out[name] = jnp.asarray(drawn.astype(out[name].dtype))
    for name, factor in factors.items():
        out[name] = (out[name] * factor).astype(out[name].dtype)
    return out
```

```python
from contextlib import ExitStack

import numpy as np

import concourse.bass as bass
from concourse import mybir

F32 = mybir.dt.float32
F16 = mybir.dt.float16
U8 = mybir.dt.uint8
U32 = mybir.dt.uint32
ALU = mybir.AluOpType
ACT = mybir.ActivationFunctionType
X_AXIS = mybir.AxisListType.X

P = 128
B, S, D, S2 = 4, 256, 256, 4096
T = B * S // P
KT = D // P
NTOK = B * S
H, HD = 16, 16
H0, DH0 = 16, 64
W0 = H0 * DH0
R0 = 2 * B - 1
HID = 1024
HM = HID // P
ER, ES = 8, 2
LN_EPS = 1e-5
RMS_EPS = float(np.finfo(np.float32).eps)
SCALE = float(HD) ** -0.5
GH = 4
NG = B * H // GH
CH = S2 // P
KB = 1024
NKB = S2 // KB
MASKED, UNMASK_ROW = -60000.0, 16384.0
R_MASK, R_MAX = 64, 65
SENTINEL = -5.0
HV = HD + 1

COLS = ["L0_xattn_Wq_b:8", "L0_attn_pos_proj_bias:2", "bq0:2", "L0_attn_r_r_bias:2", "L0_ffn_g_shared:2",
        "L0_ffn_g_routed:2", "L1_xattn_bq:2", "bk_x:2", "L1_attn_g1:2", "L1_attn_beta1:2", "L1_attn_g2:2",
        "L1_attn_beta2:2", "L1_attn_bq:2", "L1_attn_bk:2", "bq_swapped:2", "bk_swapped:2", "L1_attn_b1:8",
        "L1_ffn_bq:2", "L1_ffn_bk:2"]
ROWS = ["L0_xattn_out_b:256", "L0_attn_r_w_bias:256",
        "L0_attn_out_proj_bias:256", "bv_x:256", "L1_xattn_bo:256", "L1_attn_bv:256", "L1_attn_bo:256",
        "L1_attn_b2:256", "L1_ffn_bv:256", "L1_ffn_bo:256", "L1_ffn_g1:256", "L1_ffn_be1:256",
        "L1_ffn_g2:256", "L1_ffn_be2:256", "L1_ffn_bg:8"]


def offsets(names):
    at, out = 0, {}
    for n in names:
        name, width = n.split(":")
        out[name] = (at, int(width))
        at += int(width)
    return out, at


COL_AT, NCOLS = offsets(COLS)
ROW_AT, NROWS = offsets(ROWS)


def build(nc, a, out, stop=99):
    with ExitStack() as top:
        def sem(name):
            return top.enter_context(nc.semaphore(name))

        def sb(name, shape, dt=F32, scope=top):
            return scope.enter_context(nc.sbuf_tensor(name, shape, dt))

        def dram(name, shape, dt):
            return nc.dram_tensor(name, shape, dt, kind="Internal").ap()

        k_scr = dram("k_scr", [B, H // GH, 2, GH * HD, S2], F16)
        q_scr = dram("q_scr", [B, H // GH, 2, GH * HD, S], F16)
        v_scr = dram("v_scr", [NG, P, CH, GH * HV], F32)
        mask_scr = dram("mask_scr", [NG, S2], F16)
        self_scr = [dram(f"self_scr{i}", [2, 2, D, NTOK], F16) for i in range(2)]

        x = sb("x", [P, T, D])
        u = sb("u", [P, T, D])
        tok = sb("tok", [P, T, D])
        xT = sb("xT", [P, KT, NTOK])
        ident = sb("ident", [P, P])
        cols = sb("cols", [P, NCOLS])
        rows = sb("rows", [P, NROWS])
        stats = sb("stats", [P, T, 6])
        meanvar = sb("meanvar", [P, T, 2])
        var_eps = sb("var_eps", [P, T])
        deviation = sb("deviation", [P, T])
        rstd = sb("rstd", [P, T])
        rtmp = sb("rtmp", [P, T])
        logit = sb("logit", [P, T, ER])
        score = sb("score", [P, T, 2 * ER])
        top8 = sb("top8", [P, T, 8])
        rest = sb("rest", [P, T, 2 * ER])
        esum = sb("esum", [P, T])
        gate = sb("gate", [P, ER, T])
        gate_t = sb("gate_t", [P, T, ER + ES])
        gateT = sb("gateT", [ER + ES, NTOK])
        wkv = sb("wkv", [P, KT, 2 * D])
        wqo_x = sb("wqo_x", [P, 2, KT, D])
        wb = sb("wb", [P, 4096])

        def col(name, i):
            at = COL_AT[name][0] + i
            return cols[:, at:at + 1]

        def row(name, lo=0, hi=None, parts=slice(0, P)):
            at, n = ROW_AT[name]
            return rows[parts, at + lo:at + (n if hi is None else hi)]

        psum = [top.enter_context(nc.psum_tensor(f"bank{i}", [P, 512], F32)) for i in range(4)]
        pair = [top.enter_context(nc.psum_tensor(f"pair{i}", [P, 1024], F32)) for i in range(2)]
        bank = psum + [pair[0][:, 0:512], pair[0][:, 512:1024], pair[1][:, 0:512], pair[1][:, 512:1024]]
        bank = [b_[:, :] for b_ in bank]

        b_in = wb[:, 0:1536].rearrange("p (k n) -> p k n", k=KT)
        b_q = wb[:, 1536:2048].rearrange("p (k n) -> p k n", k=KT)
        b_o = wb[:, 2048:2560].rearrange("p (k n) -> p k n", k=KT)
        b_p = wb[:, 2560:3072].rearrange("p (k n) -> p k n", k=KT)
        b_pos = wb[:, 3072:3072 + KT * R0].rearrange("p (k n) -> p k n", k=KT)
        b_mask = wb[:, 3100:3100 + KT * H].rearrange("p (k n) -> p k n", k=KT)
        r_w = wb[:, 0:3072].rearrange("p (w k n) -> p w k n", w=6, k=KT)
        l_w = wb[:, 0:2048].rearrange("p (w k n) -> p w k n", w=4, k=KT)

        s_start = sem("inputs_loaded")
        s_wa = sem("large_weights_loaded")
        s_wb = sem("weight_area_loaded")
        s_wkv = sem("cross_weights_loaded")
        s_dve = sem("vector_steps")
        s_act = sem("scalar_steps")
        s_pool = sem("pool_steps")
        s_x = sem("residual_updated")
        s_store = sem("output_stored")

        s_var = sem("norm_variance")
        s_dev = sem("norm_deviation")
        s_nt = sem("norm_tiles")
        s_tmm = sem("tiles_transposed")
        s_tev = sem("transposes_copied")
        counted = {"norms": 0, "normed": 0, "turned": 0, "copied": 0}

        class Norm:

            def __init__(self, tiles=T):
                self.root, self.tiles = counted["norms"], counted["normed"]
                counted["norms"] += 1
                counted["normed"] += tiles

            def wait(self, eng, n):
                eng.wait_ge(s_nt, self.tiles + n)

        class Turn:

            def __init__(self, src, dests):
                self.src, self.dests = src, dests
                self.mm, self.ev = counted["turned"], counted["copied"]
                counted["turned"] += 4
                counted["copied"] += 4 * len(dests)

        class Steps:

            def __init__(self, eng, s):
                self.eng, self.s, self.n, self.base = eng, s, 0, 0

            def link(self, ins):
                ins.then_inc(self.s, 1)
                self.n += 1

            def settle(self):
                self.eng.wait_ge(self.s, self.base + self.n)

        def dve_rstd(dve, st, nm):
            dve.wait_ge(s_dev, nm.root + 1)
            st.link(dve.reciprocal(rstd[:, :], deviation[:, :]))
            st.settle()
            st.link(dve.tensor_tensor(rtmp[:, :], rstd[:, :], rstd[:, :], ALU.mult))
            st.settle()
            st.link(dve.tensor_tensor(rtmp[:, :], rtmp[:, :], var_eps[:, :], ALU.mult))
            st.settle()
            st.link(dve.tensor_scalar(rtmp[:, :], rtmp[:, :], -0.5, 1.5, ALU.mult, ALU.add))
            st.settle()
            st.link(dve.tensor_tensor(rstd[:, :], rstd[:, :], rtmp[:, :], ALU.mult))
            st.settle()

        def dve_norm(dve, st, nm, src, dst):
            for t in range(T):
                st.link(dve.bn_stats(stats[:, t, :], src[:, t, :]))
            st.settle()
            for t in range(T):
                st.link(dve.bn_aggr(meanvar[:, t, :], stats[:, t, :]))
            st.settle()
            dve.tensor_scalar(var_eps[:, :], meanvar[:, :, 1], LN_EPS, None, ALU.add).then_inc(s_var, 1)
            dve.wait_ge(s_var, nm.root + 1)
            dve_rstd(dve, st, nm)
            for t in range(T):
                dve.tensor_scalar(dst[:, t, :], src[:, t, :], meanvar[:, t, 0:1], rstd[:, t:t + 1],
                                  ALU.subtract, ALU.mult).then_inc(s_nt, 1)
            nm.wait(dve, T)

        def act_dev(act, nm):
            act.wait_ge(s_var, nm.root + 1)
            act.activation(deviation[:, :], var_eps[:, :], ACT.Sqrt).then_inc(s_dev, 1)

        def pe_turn(pe, tr, ready):
            for half in range(2):
                ready(half)
                for k in range(KT):
                    job = 2 * half + k
                    if job >= 2:
                        pe.wait_ge(s_tev, tr.ev + len(tr.dests) * (job - 1))
                    for j in range(4):
                        last = pe.transpose(bank[job % 2][:, j * P:(j + 1) * P],
                                            tr.src[:, 4 * half + j, k * P:(k + 1) * P], ident[:, :])
                    last.then_inc(s_tmm, 1)

        def act_turn(act, tr):
            for half in range(2):
                for k in range(KT):
                    job = 2 * half + k
                    act.wait_ge(s_tmm, tr.mm + job + 1)
                    for dst, scale, bias in tr.dests:
                        o = dst[:, k, half * 512:(half + 1) * 512]
                        if scale is None:
                            act.activation(o, bank[job % 2], ACT.Copy).then_inc(s_tev, 1)
                        elif bias is None:
                            act.activation(o, bank[job % 2], ACT.Copy, scale=col(scale, k)).then_inc(s_tev, 1)
                        else:
                            act.activation(o, bank[job % 2], ACT.Identity, scale=col(scale, k),
                                           bias=col(bias, k)).then_inc(s_tev, 1)

        def turned(eng, tr, half=1):
            eng.wait_ge(s_tev, tr.ev + len(tr.dests) * 2 * (half + 1))

        class Gemm:

            def __init__(self, name, lhs, w, residual=None):
                self.lhs, self.w, self.kt, self.banks = lhs, w, KT, (2, 3)
                self.mm = sem(f"{name}_product")
                self.ev = sem(f"{name}_taken") if residual is None else s_x
                self.base = 0 if residual is None else residual * T

        def pe_gemm(pe, g, tr):
            n = g.w.shape[2]
            for t in range(T):
                if t % 4 == 0:
                    turned(pe, tr, t // 4)
                if t >= len(g.banks):
                    pe.wait_ge(g.ev, g.base + t - len(g.banks) + 1)
                for k in range(g.kt):
                    last = pe.matmul(bank[g.banks[t % len(g.banks)]][:, 0:n], g.lhs[:, k, t * P:(t + 1) * P],
                                     g.w[:, k, :], start=(k == 0), stop=(k == g.kt - 1))
                last.then_inc(g.mm, 1)

        def gemm_out(g, t):
            return bank[g.banks[t % len(g.banks)]][:, 0:g.w.shape[2]]

        with ExitStack() as sc:
            CB = 8
            NCB = S2 // P // CB
            NBUF = 3
            w0q = sb("w0q", [P, KT, W0], F32, sc)
            w0o = sb("w0o", [P, W0 // P, D], F32, sc)
            row0 = sb("row0", [P, W0], F32, sc)
            ctx_sb = [sb(f"ctx_sb{i}", [P, CB, D + 1], F32, sc) for i in range(NBUF)]
            q0T = sb("q0T", [P, W0 // P, NTOK], F32, sc)
            gram = sb("gram", [P, KT, D + 1], F32, sc)
            gw = sb("gw", [P, KT, W0], F32, sc)
            gw_row = sb("gw_row", [1, W0], F32, sc)
            kv0 = sb("kv0", [P, H0 // 2, P], F32, sc)
            lin = [sb(f"lin{i}", [P, H0, DH0], F32, sc) for i in range(2)]
            lin_max = sb("lin_max", [P, 2, H0], F32, sc)
            lin_sum = sb("lin_sum", [P, 2, H0], F32, sc)
            linT = sb("linT", [P, W0 // P, P], F32, sc)
        norm0 = Norm()
        turn0 = Turn(u, [(xT, None, None)])
        s_ctx = [sem(f"ctx_loaded{i}") for i in range(NBUF)]
        s_ones = sem("ctx_ones_set")
        s_gram_blk = sem("ctx_block_used")
        s_q0 = sem("q0_product")
        s_q0e = sem("q0_copied")
        s_gram = sem("gram_product")
        s_grame = sem("gram_copied")
        s_gw = sem("gram_w_product")
        s_gwe = sem("gram_w_copied")
        s_kv0 = sem("kv0_product")
        s_kv0e = sem("kv0_copied")
        s_lg = sem("linear_logits")
        s_lgs = sem("linear_logits_shifted")
        s_lge = sem("linear_exp")
        s_lgn = sem("linear_weights")
        s_lt = sem("linear_transposed")
        s_lte = sem("linear_transposes_copied")
        s_lo = sem("linear_out")

        with ExitStack() as sc:
            qkv = sb("qkv", [P, T, 3 * D], F32, sc)
            rel = sb("rel", [P, T, R0 * H], F32, sc)
            posT = sb("posT", [P, KT, R0], F32, sc)
            pos_blk = sb("pos_blk", [P, KT, R0, H], F32, sc)
            rel_w = sb("rel_w", [P, KT, R0 * H], F32, sc)
            rel_bias = sb("rel_bias", [P, R0 * H], F32, sc)
            bqrr = sb("bqrr", [P, KT], F32, sc)
            bqrr_rep = sb("bqrr_rep", [P, KT, P], F32, sc)
            row_in = sb("row_in", [P, 3 * D], F32, sc)
            prod = [sb(f"prod{i}", [P, B, D], F32, sc) for i in range(2)]
            sc0 = sb("sc0", [P, B, B, H], F32, sc)
            sc0_max = sb("sc0_max", [P, B, H], F32, sc)
            cT = [sb(f"cT{i}", [P, KT, 512], F32, sc) for i in range(3)]
            k_f = [sb(f"k_f{i}", [P, 512], F32, sc) for i in range(2)]
            k_hi = [sb(f"k_hi{i}", [P, 512], F16, sc) for i in range(3)]
            k_lo = [sb(f"k_lo{i}", [P, 512], F16, sc) for i in range(3)]
            VC = CH // 4
            v_st = [sb(f"v_st{i}", [P, H // GH, VC, GH * HV], F32, sc) for i in range(2)]
            m_u32 = sb("m_u32", [B, S2 // 4], U32, sc)
            m_16 = sb("m_16", [B, S2], F16, sc)
        norm1 = Norm()
        turn1 = Turn(u, [(xT, None, None)])
        s_rin = sem("in_proj_bias_loaded")
        s_posT = sem("pos_product")
        s_posb = sem("pos_blocks")
        s_relw = sem("rel_w_product")
        s_relwe = sem("rel_w_copied")
        s_qkv = sem("qkv_product")
        s_qkve = sem("qkv_taken")
        s_at0 = sem("batch_scores_shifted")
        s_at0e = sem("batch_exp")
        s_tok1 = sem("batch_context_tiles")
        turn1o = Turn(tok, [(xT, None, None)])
        gemm1 = Gemm("out1", xT, b_o, residual=1)
        s_cT = [sem(f"ctxT_loaded{i}") for i in range(3)]
        s_kp = sem("k_product")
        s_kf = sem("k_copied")
        s_klo = sem("k_low_part")
        s_kst = [sem(f"k_stored{i}") for i in range(3)]
        s_vp = sem("v_product")
        s_ve = sem("v_copied")
        s_vst = [sem(f"v_stored{i}") for i in range(2)]
        s_vones = sem("v_ones_set")
        s_m8 = sem("mask_loaded")
        s_m16 = sem("mask_row")
        s_mst = sem("mask_stored")

        with ExitStack() as sc:
            xTs = sb("xTs", [P, KT, NTOK], F32, sc)
            junk3 = sb("junk3", [P, D], F32, sc)
            w_1 = [sb(f"w_1{i}", [P, KT, HID], F32, sc) for i in range(2)]
            w_2 = [sb(f"w_2{i}", [P, HM, D], F32, sc) for i in range(2)]
            b_1 = [sb(f"b_1{i}", [P, HM], F32, sc) for i in range(2)]
            hid = sb("hid", [P, HM, NTOK], F32, sc)
            xTr = hid[:, 0:KT, :]
            cent = sb("cent", [P, KT, ER], F32, sc)
            b2_all = sb("b2_all", [ER + ES, D], F32, sc)
            rinv = sb("rinv", [P, T], F32, sc)
            g_now = [sb(f"g_now{i}", [P, T], F32, sc) for i in range(2)]
        norm2 = Norm()
        rms = Norm(tiles=0)
        s_sq = sem("squares_summed")
        s_un = sem("rms_tiles")
        turn2 = Turn(tok, [(xTs, "L0_ffn_g_shared", None), (xT, "L0_ffn_g_routed", None), (xTr, None, None)])
        s_w3 = sem("router_weights_loaded")
        s_wexp = [sem(f"expert_loaded{i}") for i in range(2)]
        s_log = sem("router_logits")
        s_logs = sem("router_logits_scaled")
        s_loge = sem("router_exp")
        s_gate = sem("gates_ready")
        s_gT = sem("gates_transposed")
        s_gTe = sem("gates_copied")
        s_b2 = sem("b2_product")
        s_b2e = sem("b2_taken")
        s_w1 = sem("expert_hidden_product")
        s_gelu = sem("expert_hidden")
        s_w2 = sem("expert_out_product")
        s_acc = sem("expert_accumulated")

        attention_scope = ExitStack()
        NP_ = 4
        pexp = [sb(f"pexp{i}", [P, GH, S], F32, attention_scope) for i in range(NP_)]
        mx_part = sb("mx_part", [P, GH * 2 * (S2 // 512)], F32, attention_scope)
        mx = sb("mx", [P, 128], F32, attention_scope)
        m_neg = sb("m_neg", [P, P], F32, attention_scope)
        m_res = sb("m_res", [P, P], F32, attention_scope)
        m_prt = sb("m_prt", [P, 3, P], F16, attention_scope)
        oT = [sb(f"oT{i}", [P, S], F32, attention_scope) for i in range(2)]
        o_grp = sb("o_grp", [P, NG, 2, GH, HD], F32, attention_scope)
        den = sb("den", [P, 2, GH], F32, attention_scope)
        with ExitStack() as sc:
            q_hi = sb("q_hi", [P, KT, NTOK], F16, sc)
            q_lo = sb("q_lo", [P, KT, NTOK], F16, sc)
            kst = [sb(f"kst{i}", [P, GH, S2], F16, sc) for i in range(2)]
            qa = [sb(f"qa{i}", [P, GH, S], F16, sc) for i in range(2)]
            qb = [sb(f"qb{i}", [P, GH, S], F16, sc) for i in range(2)]
            vst = [sb(f"vst{i}", [P, CH, GH * HV], F32, sc) for i in range(2)]
        norm3 = Norm()
        turn3 = Turn(u, [(xT, None, None)])
        s_qx = sem("cross_q_product")
        s_qxh = sem("cross_q_high")
        s_qxl = sem("cross_q_low")
        s_qst = sem("cross_q_stored")
        s_init4 = sem("stack_rows_set")
        s_kq = [sem(f"group_loaded{i}") for i in range(2)]
        s_vl = [sem(f"group_values_loaded{i}") for i in range(2)]
        s_s1 = sem("scores_first_pass")
        s_mx = sem("partial_maxima")
        s_mxa = sem("group_maxima")
        s_mT = sem("maxima_transposed")
        s_mp = sem("maxima_parts")
        s_mrow = sem("maxima_rows_stored")
        s_s2 = sem("scores_second_pass")
        s_exp = sem("weights")
        s_pv = sem("weighted_values")
        s_oc = sem("weighted_values_copied")
        s_oT = sem("weighted_values_transposed")
        s_on = sem("group_normalised")
        s_grp = sem("group_vector_steps")
        turn3o = Turn(tok, [(xT, None, None)])
        gemm3 = Gemm("out3", xT, wqo_x[:, 1], residual=3)
        s_tok3 = sem("cross_context_tiles")

        class Counted:

            def __init__(self, name, each):
                self.s, self.each = sem("self_" + name), each

        signals = {
            "fproj": Counted("qk_product", 8), "fhi": Counted("high_parts", 0),
            "flo": Counted("low_parts", 8),
            "fst": Counted("parts_stored", 64), "qk_loaded": Counted("stacks_loaded", 512),
            "rows_set": Counted("constant_rows_set", 3), "vproj": Counted("v_product", T),
            "vtaken": Counted("v_copied", T), "s1": Counted("scores_first_pass", B * H),
            "mx": Counted("maxima", B * H), "mT": Counted("maxima_transposed", 1),
            "mp": Counted("maxima_parts", 1), "mrow": Counted("maxima_rows_stored", 48),
            "s2": Counted("scores_second_pass", 2 * NG), "exp": Counted("weights", 2 * NG),
            "pv": Counted("weighted_values", 2 * NG), "oc": Counted("weighted_values_copied", GH * NG),
            "oT": Counted("weighted_values_transposed", NG), "on": Counted("group_normalised", NG),
        }

        class SelfAttention:

            def __init__(self, turn, scope):
                i = f"self{turn}_"
                self.turn = turn
                self.hi = sb(i + "hi", [P, KT, NTOK], F16, scope)
                self.lo = sb(i + "lo", [P, KT, NTOK], F16, scope)
                self.k = sb(i + "k", [P, B * H, S], F16, scope)
                self.q = sb(i + "q", [P, B * H, S], F16, scope)
                self.v = sb(i + "v", [P, T, H, HV], F32, scope)

            def wait(self, eng, what, n):
                eng.wait_ge(signals[what].s, self.turn * signals[what].each + n)

        with ExitStack() as sc:
            sa5 = SelfAttention(0, sc)
            cosT = sb("cosT", [P, S], F32, sc)
            sinT = sb("sinT", [P, S], F32, sc)
            rot_a = [sb(f"rot_a{i}", [P, 512], F32, sc) for i in range(2)]
            rot_b = [sb(f"rot_b{i}", [P, 512], F32, sc) for i in range(2)]
        with ExitStack() as sc:
            hid5 = sb("hid5", [P, HM, NTOK], F32, sc)
            r_w1 = sb("r_w1", [P, KT, HID], F32, sc)
            r_w2 = sb("r_w2", [P, HM, D], F32, sc)
        norm4a, norm4b, norm5 = Norm(), Norm(), Norm()
        turn4 = Turn(tok, [(xT, "L1_attn_g1", "L1_attn_beta1")])
        turn4o = Turn(tok, [(xT, None, None)])
        gemm4 = Gemm("out4", xT, r_w[:, 5])
        turn5 = Turn(tok, [(xT, "L1_attn_g2", "L1_attn_beta2")])
        s_rope = sem("rotary_tables_loaded")
        s_tok4 = sem("self5_context_tiles")
        s_h5 = sem("mlp_hidden_product")
        s_h5e = sem("mlp_hidden")
        s_m2 = sem("mlp_out_product")

        with ExitStack() as sc:
            sa6 = SelfAttention(1, sc)
            b2_l = sb("b2_l", [ER, D], F32, sc)
            wg_l = sb("wg_l", [P, KT, ER], F32, sc)
        with ExitStack() as sc:
            l_we = sb("l_we", [P, ER // 2, KT, 2 * D], F32, sc)
        attention_scope.close()
        norm6, norm6a, norm6m = Norm(), Norm(), Norm()
        turn6 = Turn(u, [(xT, None, None)])
        turn6o = Turn(tok, [(xT, None, None)])
        gemm6 = Gemm("out6", xT, l_w[:, 3])
        turn7 = Turn(u, [(xT, None, None)])
        s_w6 = sem("last_weights_loaded")
        s_tok6 = sem("self6_context_tiles")
        s_y6 = sem("last_residual_tiles")
        s_log6 = sem("router6_logits")
        s_logs6 = sem("router6_logits_shifted")
        s_loge6 = sem("router6_exp")
        s_gate6 = sem("gates6_ready")
        s_gT6 = sem("gates6_transposed")
        s_gTe6 = sem("gates6_copied")
        s_b26 = sem("bexp_product")
        s_b2e6 = sem("bexp_taken")
        s_we = sem("expert6_product")
        s_wee = sem("expert6_accumulated")

        block = top.enter_context(nc.Block())

        N_START = 5
        ctx_blocks = [(b, c) for b in range(B) for c in range(NCB)]
        NPB = S2 // 512
        proj_blocks = [(b, c) for b in range(B) for c in range(NPB)]
        K_PER_STEP = 3
        FIRST_STEP = 8
        S1N = GH * 2 * (S2 // 512)
        GROUP_DMAS = 4 + 1 + 8

        def each_group(eng, body):
            body(0, 0, 1, True, False)
            body(1, 1, 1, False, False)
            with eng.Fori(0, (NG - 4) // 2) as i:
                for par in range(2):
                    body(2 * i + (2 + par), par, i + 2, False, False)
            body(NG - 2, 0, NG // 2, False, False)
            body(NG - 1, 1, NG // 2, False, True)

        def context_stored(eng):
            for i in range(3):
                eng.wait_ge(s_kst[i], 64 * len(range(i, 2 * len(proj_blocks), 3)))
            for i in range(2):
                eng.wait_ge(s_vst[i], 64 * 8)
            eng.wait_ge(s_mst, 16 * (H // GH))

        @block.sync
        def _(sp):
            def store():
                sp.wait_ge(s_x, min(stop, 6) * T)
                sp.dma_start(out.rearrange("b (h p) d -> p (b h) d", p=P), x[:, :, :]).then_inc(s_store, 16)
                sp.wait_ge(s_store, 16)

            sp.dma_start(x[:, :, :], a["x"].rearrange("b (h p) d -> p (b h) d", p=P)).then_inc(s_start, 16)
            sp.dma_start(ident[:, :], a["ident"]).then_inc(s_start, 16)
            sp.dma_start(cols[:, :], a["cols"]).then_inc(s_start, 16)
            sp.dma_start(rows[:, :], a["rows"].to_broadcast([P, NROWS])).then_inc(s_start, 16)
            sp.dma_start(row0[:, :], a["row0"].to_broadcast([P, W0])).then_inc(s_start, 16)
            sp.dma_start(w0q[:, :, :], a["w0qT"].rearrange("(k p) n -> p k n", p=P)).then_inc(s_wa, 16)
            sp.dma_start(w0o[:, :, :], a["w0oT"].rearrange("(k p) n -> p k n", p=P)).then_inc(s_wa, 16)
            sp.wait_ge(s_ones, NBUF)
            for n, (b, c) in enumerate(ctx_blocks):
                if n >= NBUF:
                    sp.wait_ge(s_gram_blk, n - NBUF + 1)
                src = a["ctx"][b].rearrange("(n p c) d -> n p c d", p=P, c=CB)[c]
                sp.dma_start(ctx_sb[n % NBUF][:, :, 0:D], src).then_inc(s_ctx[n % NBUF], 16)
                if n == 2:
                    for dst, name in ((b_in, "w1inT"), (b_q, "w1q"), (b_o, "w1oT"), (b_p, "w1pT"), (b_pos, "posT"),
                                      (b_mask, "head_mask")):
                        sp.dma_start(dst, a[name].rearrange("(k p) n -> p k n", p=P)).then_inc(s_wb, 16)
                    sp.dma_start(wkv[:, :, :], a["wkv"].rearrange("(k p) n -> p k n", p=P)).then_inc(s_wkv, 16)
                    sp.dma_start(wqo_x[:, 0], a["wq_x"].rearrange("(k p) n -> p k n", p=P)).then_inc(s_wkv, 16)
                    sp.dma_start(wqo_x[:, 1], a["wo_x"].rearrange("(k p) n -> p k n", p=P)).then_inc(s_wkv, 16)
            if stop <= 1:
                store()
                return
            sp.wait_ge(s_x, T)
            sp.dma_start(row_in[:, :], a["row_in"].to_broadcast([P, 3 * D])).then_inc(s_rin, 16)
            sp.dma_start(m_u32[:, :], a["mask"]).then_inc(s_m8, 16)
            def store_projection(n):
                b, c = proj_blocks[n]
                for m in range(KT):
                    job = 2 * n + m
                    sp.wait_ge(s_klo, job + 1)
                    for part, src in enumerate((k_hi[job % 3], k_lo[job % 3])):
                        for g in range(2):
                            sp.dma_start(k_scr[b, 2 * m + g, part, :, c * 512:(c + 1) * 512],
                                         src[64 * g:64 * g + 64, :]).then_inc(s_kst[job % 3], 16)
                if n % 2 == 1:
                    vb = n // 2
                    sp.wait_ge(s_ve, 4 * (n + 1))
                    cb = (vb % 4) * VC
                    for g in range(H // GH):
                        sp.dma_start(v_scr[b * 4 + g, :, cb:cb + VC, :], v_st[vb % 2][:, g]).then_inc(s_vst[vb % 2], 16)

            for n, (b, c) in enumerate(proj_blocks):
                if n >= 2:
                    store_projection(n - 2)
                if n >= 3:
                    sp.wait_ge(s_vp, 4 * (n - 2))
                sp.dma_start(cT[n % 3][:, :, :], a["ctxT"][b].rearrange("(k p) n -> p k n", p=P)[:, :, c * 512:(c + 1) * 512])\
                    .then_inc(s_cT[n % 3], 16)
            store_projection(len(proj_blocks) - 2)
            store_projection(len(proj_blocks) - 1)
            if stop <= 2:
                store()
                return
            sp.wait_ge(s_x, 2 * T)
            sp.dma_start(r_w, a["r_w"].rearrange("w (k p) n -> p w k n", p=P)).then_inc(s_wb, 16)
            sp.wait_ge(s_x, 2 * T)
            context_stored(sp)
            sp.dma_start(cent[:, :, :], a["cent"].rearrange("(k p) n -> p k n", p=P)).then_inc(s_w3, 16)
            sp.dma_start(b2_all[:, :], a["b2_all"]).then_inc(s_w3, 16)

            def expert(n, e, par):
                one = bass.ds(e, 1)
                sp.dma_start(w_1[par][:, :, :], a["w1_all"][one].rearrange("o (k p) n -> (o p) k n", p=P))\
                    .then_inc(s_wexp[par], 16)
                sp.dma_start(w_2[par][:, :, :], a["w2_all"][one].rearrange("o (k p) n -> (o p) k n", p=P))\
                    .then_inc(s_wexp[par], 16)
                sp.dma_start(b_1[par][:, :], a["b1_all"][one].rearrange("o p n -> (o p) n")).then_inc(s_wexp[par], 16)

            expert(0, ER, 0)
            expert(1, ER + 1, 1)
            with sp.Fori(0, ER // 2) as i:
                for par in range(2):
                    sp.wait_ge(s_w2, (2 * i + par) * T + T)
                    expert(None, 2 * i + par, par)
            if stop <= 3:
                store()
                return
            for k in range(KT):
                sp.wait_ge(s_qxl, 2 * (k + 1))
                for part, src in enumerate((q_hi, q_lo)):
                    for g in range(2):
                        sp.dma_start(q_scr[:, 2 * k + g, part].rearrange("b f q -> f b q"),
                                     src[64 * g:64 * g + 64, k, :].rearrange("f (b q) -> f b q", b=B)).then_inc(s_qst, 16)
            sp.wait_ge(s_qst, 16 * 8)
            sp.wait_ge(s_init4, 6)

            k_g = k_scr.rearrange("b g s f n -> (b g) s f n")
            q_g = q_scr.rearrange("b g s f n -> (b g) s f n")

            def load_group(g, par):
                one = bass.ds(g, 1)
                b_row = mask_scr[one, :].rearrange("o (x n) -> o x n", x=1).to_broadcast([1, GH, S2])
                for r, part in enumerate((0, 0, 1, 1)):
                    sp.dma_start(kst[par][16 * r:16 * r + 16, :, :],
                                 k_g[one, part].rearrange("o (h d) n -> (o d) h n", d=HD)).then_inc(s_kq[par], 16)
                sp.dma_start(kst[par][R_MASK:R_MASK + 1, :, :], b_row).then_inc(s_kq[par], 16)
                for dst in (qa[par], qb[par]):
                    for r, part in enumerate((0, 1, 0, 1)):
                        sp.dma_start(dst[16 * r:16 * r + 16, :, :],
                                     q_g[one, part].rearrange("o (h d) n -> (o d) h n", d=HD)).then_inc(s_kq[par], 16)
                sp.dma_start(vst[par][:, :, :], v_scr[one].rearrange("o p c n -> (o p) c n")).then_inc(s_vl[par], 16)

            def max_rows(par):
                for i in range(3):
                    sp.dma_start(qb[par][R_MAX + i:R_MAX + i + 1, :, :], m_prt[0:2 * GH, i, :]).then_inc(s_mrow, 16)

            load_group(0, 0)
            sp.wait_ge(s_mp, 1)
            max_rows(0)

            def next_group(g, par, turn, first, last):
                if last:
                    return
                if not first:
                    sp.wait_ge(s_pv, g * CH)
                load_group(g + 1, 1 - par)
                sp.wait_ge(s_mp, g + 2)
                max_rows(1 - par)

            each_group(sp, next_group)

            def self_io(sa, scr, tensors):
                for n, what in enumerate(tensors):
                    sa.wait(sp, "flo", 4 * (n + 1))
                    for part, src in enumerate((sa.hi, sa.lo)):
                        sp.dma_start(scr[n, part].rearrange("(k p) q -> p k q", p=P), src[:, :, :]).then_inc(signals["fst"].s, 16)
                    sa.wait(sp, "fst", 32 * (n + 1))
                    if n == 0:
                        sa.wait(sp, "rows_set", 3)
                    order, dst = ((0, 1, 0, 1), sa.q) if what == "q" else ((0, 0, 1, 1), sa.k)
                    for r, part in enumerate(order):
                        for b in range(B):
                            sp.dma_start(dst[16 * r:16 * r + 16, b * H:(b + 1) * H, :],
                                         scr[n, part].rearrange("(h d) (b q) -> b d h q", d=HD, b=B)[b])\
                                .then_inc(signals["qk_loaded"].s, 16)
                sa.wait(sp, "mp", 1)
                for i in range(3):
                    sp.dma_start(sa.q[R_MAX + i:R_MAX + i + 1, :, :], sa_parts[:, i, :]).then_inc(signals["mrow"].s, 16)

            sa_parts = m_prt
            if stop <= 4:
                store()
                return
            sp.wait_ge(s_x, 4 * T)
            sp.dma_start(cosT[:, :], a["cosT"]).then_inc(s_rope, 16)
            sp.dma_start(sinT[:, :], a["sinT"]).then_inc(s_rope, 16)
            self_io(sa5, self_scr[0], "qk")
            sa5.wait(sp, "on", NG)
            sp.dma_start(r_w1[:, :, :], a["r_w1"].rearrange("(k p) n -> p k n", p=P)).then_inc(s_wa, 16)
            sp.dma_start(r_w2[:, :, :], a["r_w2"].rearrange("(k p) n -> p k n", p=P)).then_inc(s_wa, 16)
            if stop <= 5:
                store()
                return
            sp.wait_ge(s_x, 5 * T)
            sp.dma_start(l_w, a["l_w"].rearrange("w (k p) n -> p w k n", p=P)).then_inc(s_wb, 16)
            sp.dma_start(b2_l[:, :], a["bexp"]).then_inc(s_w6, 16)
            sp.dma_start(wg_l[:, :, :], a["wg"].rearrange("(k p) n -> p k n", p=P)).then_inc(s_w6, 16)
            self_io(sa6, self_scr[1], "qk")
            sa6.wait(sp, "on", NG)
            sp.dma_start(l_we[:, :, :, :], a["l_we"].rearrange("e (k p) n -> p e k n", p=P)).then_inc(s_wa, 16)
            store()

        @block.tensor
        def _(pe):
            def tiles_ready(nm):
                return lambda half: nm.wait(pe, 4 * (half + 1))

            pe.wait_ge(s_start, 16 * N_START)
            pe_turn(pe, turn0, tiles_ready(norm0))
            pe.wait_ge(s_wa, 32)
            job = 0
            for half in range(2):
                turned(pe, turn0, half)
                for m in range(W0 // P):
                    if job >= 2:
                        pe.wait_ge(s_q0e, job - 1)
                    for k in range(KT):
                        last = pe.matmul(bank[2 + job % 2], w0q[:, k, m * P:(m + 1) * P],
                                         xT[:, k, half * 512:(half + 1) * 512], start=(k == 0), stop=(k == KT - 1))
                    last.then_inc(s_q0, 1)
                    job += 1

            def gram_of(b):
                if b >= 1:
                    pe.wait_ge(s_grame, 2 * b)
                for c in range(NCB):
                    n = b * NCB + c
                    pe.wait_ge(s_ctx[n % NBUF], 16 * (n // NBUF + 1))
                    for j in range(CB):
                        for m in range(KT):
                            last = pe.matmul(bank[m][:, 0:D + 1], ctx_sb[n % NBUF][:, j, m * P:(m + 1) * P],
                                             ctx_sb[n % NBUF][:, j, :], start=(c == 0 and j == 0),
                                             stop=(c == NCB - 1 and j == CB - 1))
                    last.then_inc(s_gram_blk, 1)

            def kv_of(b):
                pe.wait_ge(s_grame, 2 * (b + 1))
                if b == 0:
                    pe.wait_ge(s_q0e, W0 // P * 2)
                else:
                    pe.wait_ge(s_x, 2 * b)
                    pe.wait_ge(s_lte, 4 * b)
                n = 6 * b
                for m in range(KT + 1):
                    cs, rws = (slice(m * P, (m + 1) * P), slice(0, P)) if m < KT else (slice(D, D + 1), slice(0, 1))
                    for h in range(2):
                        if n >= 6 * b + 2:
                            pe.wait_ge(s_gwe, n - 1)
                        for k in range(KT):
                            last = pe.matmul(bank[2 + n % 2][rws, :], gram[:, k, cs],
                                             w0q[:, k, h * 512:(h + 1) * 512], start=(k == 0), stop=(k == KT - 1))
                        last.then_inc(s_gw, 1)
                        n += 1
                pe.wait_ge(s_gwe, 6 * (b + 1))
                for j in range(2):
                    for i in range(4):
                        h = 4 * j + i
                        hc = slice(h * P, (h + 1) * P)
                        o = bank[2 + j][:, i * P:(i + 1) * P]
                        for k in range(KT):
                            pe.matmul(o, w0q[:, k, hc], gw[:, k, hc], start=(k == 0), stop=False)
                        last = pe.matmul(o, row0[0:1, h * P:(h + 1) * P], gw_row[:, hc],
                                         start=False, stop=True)
                    last.then_inc(s_kv0, 1)

            def logits_of(b):
                pe.wait_ge(s_kv0e, 4 * (b + 1))
                for hf in range(2):
                    t = 2 * b + hf
                    if b >= 1:
                        pe.wait_ge(s_lgs, t - 1)
                    for m in range(W0 // P):
                        last = pe.matmul(pair[hf][:, m * P:(m + 1) * P], q0T[:, m, t * P:(t + 1) * P], kv0[:, m, :],
                                         start=(m % 4 == 0), stop=(m % 4 == 3), skip_group_check=True)
                    last.then_inc(s_lg, 1)

            def out_of(b):
                for hf in range(2):
                    t = 2 * b + hf
                    pe.wait_ge(s_lgn, t + 1)
                    for j in range(2):
                        n = 2 * t + j
                        if n >= 1:
                            pe.wait_ge(s_lte, n)
                        for i in range(4):
                            m = 4 * j + i
                            last = pe.transpose(bank[3][:, i * P:(i + 1) * P],
                                                lin[hf][:, 2 * m:2 * m + 2, :].rearrange("p h d -> p (h d)"), ident[:, :])
                        last.then_inc(s_lt, 1)
                    pe.wait_ge(s_lte, 2 * t + 2)
                    if t >= 1:
                        pe.wait_ge(s_x, t)
                    for m in range(W0 // P):
                        last = pe.matmul(bank[2][:, 0:D], linT[:, m, :], w0o[:, m, :], start=(m == 0),
                                         stop=(m == W0 // P - 1))
                    last.then_inc(s_lo, 1)

            turned(pe, turn0)
            for b in range(B + 1):
                if b < B:
                    gram_of(b)
                if b > 0:
                    out_of(b - 1)
                if b < B:
                    kv_of(b)
                    logits_of(b)
            if stop <= 1:
                return

            pe.wait_ge(s_wb, 16 * 6)
            for m in range(KT):
                for k in range(KT):
                    last = pe.matmul(bank[4 + m][:, 0:R0], b_p[:, k, m * P:(m + 1) * P], b_pos[:, k, :],
                                     start=(k == 0), stop=(k == KT - 1))
            last.then_inc(s_posT, 1)
            pe.wait_ge(s_posb, 1)
            for m in range(KT):
                for k in range(KT):
                    last = pe.matmul(bank[4 + m][:, 0:R0 * H], b_q[:, k, m * P:(m + 1) * P],
                                     pos_blk[:, k].rearrange("p j h -> p (j h)"), start=(k == 0), stop=(k == KT - 1))
            for k in range(KT):
                last = pe.matmul(bank[6][:, 0:R0 * H], bqrr_rep[:, k, :], pos_blk[:, k].rearrange("p j h -> p (j h)"),
                                 start=(k == 0), stop=(k == KT - 1))
            last.then_inc(s_relw, 1)
            pe_turn(pe, turn1, tiles_ready(norm1))
            pe.wait_ge(s_relwe, 3)
            for t in range(T):
                if t % 4 == 0:
                    turned(pe, turn1, t // 4)
                if t >= 1:
                    pe.wait_ge(s_qkve, 3 * t)
                for k in range(KT):
                    lhs = xT[:, k, t * P:(t + 1) * P]
                    pe.matmul(bank[2][:, :], lhs, b_in[:, k, 0:512], start=(k == 0), stop=(k == KT - 1))
                    pe.matmul(bank[3][:, 0:256], lhs, b_in[:, k, 512:768], start=(k == 0), stop=(k == KT - 1))
                    last = pe.matmul(bank[7][:, 0:R0 * H], lhs, rel_w[:, k, :], start=(k == 0), stop=(k == KT - 1))
                last.then_inc(s_qkv, 1)

            pe.wait_ge(s_wkv, 48)
            for n, (b, c) in enumerate(proj_blocks):
                pe.wait_ge(s_cT[n % 3], 16 * (n // 3 + 1))
                for m in range(KT):
                    job = 2 * n + m
                    if job >= 2:
                        pe.wait_ge(s_kf, 2 * (job - 1))
                    for k in range(KT):
                        last = pe.matmul(bank[4 + job % 2], wkv[:, k, m * P:(m + 1) * P], cT[n % 3][:, k, :],
                                         start=(k == 0), stop=(k == KT - 1))
                    last.then_inc(s_kp, 1)
                for j in range(4):
                    job = 4 * n + j
                    if job == 1:
                        pe.wait_ge(s_qkve, 3 * T)
                    if job >= 2:
                        pe.wait_ge(s_ve, job - 1)
                    for k in range(KT):
                        last = pe.matmul(bank[6 + job % 2][:, 0:D], cT[n % 3][:, k, j * P:(j + 1) * P],
                                         wkv[:, k, D:2 * D], start=(k == 0), stop=(k == KT - 1))
                    last.then_inc(s_vp, 1)

            pe_turn(pe, turn1o, lambda half: pe.wait_ge(s_tok1, T))
            pe_gemm(pe, gemm1, turn1o)
            if stop <= 2:
                return

            pe_turn(pe, turn2, lambda half: pe.wait_ge(s_un, 4 * (half + 1)))
            turned(pe, turn2)
            pe.wait_ge(s_w3, 32)
            for t in range(T):
                for k in range(KT):
                    last = pe.matmul(bank[2][:, t * ER:(t + 1) * ER], xTr[:, k, t * P:(t + 1) * P], cent[:, k, :],
                                     start=(k == 0), stop=(k == KT - 1), skip_group_check=True)
            last.then_inc(s_log, 1)
            pe.wait_ge(s_gate, 1)
            for j in range(2):
                for i in range(4):
                    last = pe.transpose(bank[j][0:ER + ES, i * P:(i + 1) * P], gate_t[:, 4 * j + i, :], ident[:, :])
                last.then_inc(s_gT, 1)
            pe.wait_ge(s_gTe, 2)
            for t in range(T):
                if t >= 2:
                    pe.wait_ge(s_b2e, t - 1)
                pe.matmul(bank[2 + t % 2][:, 0:D], gateT[:, t * P:(t + 1) * P], b2_all[:, :], start=True, stop=True)\
                    .then_inc(s_b2, 1)

            def expert(n, par, src, load, first):
                pe.wait_ge(s_wexp[par], load)
                for job in range(2 * HM):
                    half, m = divmod(job, HM)
                    if not (first and job < 4):
                        pe.wait_ge(s_gelu, n * 2 * HM + job - 3)
                    for k in range(KT):
                        last = pe.matmul(bank[job % 4], w_1[par][:, k, m * P:(m + 1) * P],
                                         src[:, k, half * 512:(half + 1) * 512], start=(k == 0), stop=(k == KT - 1))
                    last.then_inc(s_w1, 1)
                for t in range(T):
                    if t % 4 == 0:
                        pe.wait_ge(s_gelu, n * 2 * HM + (t // 4 + 1) * HM)
                    if not (first and t < 4):
                        pe.wait_ge(s_acc, n * T + t - 3)
                    for m in range(HM):
                        last = pe.matmul(bank[4 + t % 4][:, 0:D], hid[:, m, t * P:(t + 1) * P], w_2[par][:, m, :],
                                         start=(m == 0), stop=(m == HM - 1))
                    last.then_inc(s_w2, 1)

            pe.wait_ge(s_b2e, T)
            expert(0, 0, xTs, 48, True)
            expert(1, 1, xTs, 48, False)
            with pe.Fori(0, ER // 2) as i:
                for par in range(2):
                    expert(2 * i + (2 + par), par, xT, 48 * i + 96, False)
            if stop <= 3:
                return

            pe_turn(pe, turn3, tiles_ready(norm3))
            turned(pe, turn3)
            for m in range(KT):
                for half in range(2):
                    job = 2 * m + half
                    if job >= 2:
                        pe.wait_ge(s_qxl, job - 1)
                    for k in range(KT):
                        last = pe.matmul(bank[2 + job % 2], wqo_x[:, 0, k, m * P:(m + 1) * P],
                                         xT[:, k, half * 512:(half + 1) * 512], start=(k == 0), stop=(k == KT - 1))
                    last.then_inc(s_qx, 1)
            pe.wait_ge(s_qxl, 4)

            def first_pass(g, par, i):
                h, qt, kb = i // 16, (i // 8) % 2, i % 8
                if not (par is None and i < 2):
                    pe.wait_ge(s_mx, g * S1N + (i - 1))
                par = par or 0
                pe.matmul(bank[i % 2], qa[par][:, h, qt * P:(qt + 1) * P],
                          kst[par][:, h, kb * 512:(kb + 1) * 512], start=True, stop=True).then_inc(s_s1, 1)

            def turn_maxima(g, first):
                pe.wait_ge(s_mxa, g + 1)
                if not first:
                    pe.wait_ge(s_on, g - 1)
                pe.transpose(bank[3][0:2 * GH, 0:P], mx[:, 0:2 * GH], ident[:, :]).then_inc(s_mT, 1)

            def group_ready(g, par, n):
                pe.wait_ge(s_kq[par], n * (16 * GROUP_DMAS))

            def weigh(g, par, c, turn, first):
                pe.wait_ge(s_exp, g * CH + (c + 1))
                if c == 0:
                    pe.wait_ge(s_vl[par], turn * 16)
                    if not first:
                        pe.wait_ge(s_oc, g * GH)
                slot = (par * CH + c) % NP_
                for h in range(GH):
                    last = pe.matmul(bank[2][32 * h:32 * h + HV, 0:S], vst[par][:, c, h * HV:(h + 1) * HV],
                                     pexp[slot][:, h, :], start=(c == 0), stop=(c == CH - 1))
                last.then_inc(s_pv, 1)

            def turn_out(g, par, first):
                pe.wait_ge(s_oc, g * GH + GH)
                if not first:
                    pe.wait_ge(s_on, g)
                for qt in range(2):
                    last = pe.transpose(bank[3][:, 256 + qt * P:256 + (qt + 1) * P], oT[par][:, qt * P:(qt + 1) * P],
                                        ident[:, :])
                last.then_inc(s_oT, 1)

            def weigh_group(g, par, turn, first, last_group):
                pe.wait_ge(s_mrow, g * 48 + 48)
                done = 0
                for c in range(CH):
                    if not (first and c < 2):
                        pe.wait_ge(s_exp, g * CH + (c - 1))
                    for h in range(GH):
                        last = pe.matmul(pair[c % 2][:, h * S:(h + 1) * S], kst[par][:, h, c * P:(c + 1) * P],
                                         qb[par][:, h, :], start=True, stop=True)
                    last.then_inc(s_s2, 1)
                    if c >= 1:
                        weigh(g, par, c - 1, turn, first)
                    if c == 2 and not first:
                        turn_out(g - 1, 1 - par, isinstance(g, int) and g == 1)
                    if not last_group and c >= FIRST_STEP:
                        if c == FIRST_STEP:
                            group_ready(g + 1, 1 - par, turn + par)
                        for i in range(done, min(done + K_PER_STEP, S1N)):
                            first_pass(g + 1, 1 - par, i)
                        done = min(done + K_PER_STEP, S1N)
                        if c == CH - 2:
                            turn_maxima(g + 1, first)
                assert last_group or done == S1N
                weigh(g, par, CH - 1, turn, first)

            group_ready(0, 0, 1)
            for i in range(S1N):
                first_pass(0, None, i)
            turn_maxima(0, True)
            each_group(pe, weigh_group)
            turn_out(NG - 1, 1, False)
            pe_turn(pe, turn3o, lambda half: pe.wait_ge(s_tok3, B))
            pe_gemm(pe, gemm3, turn3o)
            if stop <= 4:
                return

            def self_proj(sa, ws, nprod):
                for n in range(2):
                    for m in range(KT):
                        for half in range(2):
                            job = 4 * n + 2 * m + half
                            if job >= 1:
                                sa.wait(pe, "flo", job)
                            for w in range(nprod):
                                for k in range(KT):
                                    last = pe.matmul(bank[4 + w], ws[n * nprod + w][:, k, m * P:(m + 1) * P],
                                                     xT[:, k, half * 512:(half + 1) * 512], start=(k == 0),
                                                     stop=(k == KT - 1))
                            last.then_inc(signals["fproj"].s, 1)

            def self_values(sa, w):
                for t in range(T):
                    if t >= 2:
                        sa.wait(pe, "vtaken", t - 1)
                    for k in range(KT):
                        last = pe.matmul(bank[2 + t % 2][:, 0:D], xT[:, k, t * P:(t + 1) * P], w[:, k, :],
                                         start=(k == 0), stop=(k == KT - 1))
                    last.then_inc(signals["vproj"].s, 1)

            def self_attention(sa):
                sa.wait(pe, "qk_loaded", 16 * 32)
                sa.wait(pe, "rows_set", 3)
                for n in range(B * H):
                    hp, qt = divmod(n, 2)
                    if n >= 4:
                        sa.wait(pe, "mx", n - 3)
                    for i in range(2):
                        h = 2 * hp + i
                        last = pe.matmul(bank[4 + n % 4][:, i * S:(i + 1) * S], sa.q[:, h, qt * P:(qt + 1) * P],
                                         sa.k[:, h, :], start=True, stop=True)
                    last.then_inc(signals["s1"].s, 1)
                sa.wait(pe, "mx", B * H)
                pe.transpose(bank[3][:, 0:P], mx[:, :], ident[:, :]).then_inc(signals["mT"].s, 1)
                sa.wait(pe, "mrow", 48)

                def weigh(n):
                    g, c = divmod(n, 2)
                    sa.wait(pe, "exp", n + 1)
                    if c == 0 and g >= 1:
                        sa.wait(pe, "oc", GH * g)
                    if n == 0:
                        sa.wait(pe, "vtaken", T)
                    b, g4 = divmod(g, H // GH)
                    for h in range(GH):
                        last = pe.matmul(bank[2][32 * h:32 * h + HV, 0:S], sa.v[:, 2 * b + c, g4 * GH + h, :],
                                         pexp[n % NP_][:, h, :], start=(c == 0), stop=(c == 1))
                    last.then_inc(signals["pv"].s, 1)

                def turn_out(g):
                    sa.wait(pe, "oc", GH * (g + 1))
                    if g >= 1:
                        sa.wait(pe, "on", g)
                    for qt in range(2):
                        last = pe.transpose(bank[3][:, 256 + qt * P:256 + (qt + 1) * P],
                                            oT[g % 2][:, qt * P:(qt + 1) * P], ident[:, :])
                    last.then_inc(signals["oT"].s, 1)

                for n in range(2 * NG):
                    g, c = divmod(n, 2)
                    if n >= 2:
                        sa.wait(pe, "exp", n - 1)
                    for h in range(GH):
                        last = pe.matmul(pair[n % 2][:, h * S:(h + 1) * S], sa.k[:, g * GH + h, c * P:(c + 1) * P],
                                         sa.q[:, g * GH + h, :], start=True, stop=True)
                    last.then_inc(signals["s2"].s, 1)
                    if n >= 1:
                        weigh(n - 1)
                    if c == 1 and g >= 1:
                        turn_out(g - 1)
                weigh(2 * NG - 1)
                turn_out(NG - 1)

            pe_turn(pe, turn4, tiles_ready(norm4b))
            turned(pe, turn4)
            pe.wait_ge(s_wb, 16 * 7)
            self_proj(sa5, [r_w[:, i] for i in range(4)], 2)
            self_values(sa5, r_w[:, 4])
            self_attention(sa5)
            pe_turn(pe, turn4o, lambda half: pe.wait_ge(s_tok4, B))
            pe_gemm(pe, gemm4, turn4o)
            pe_turn(pe, turn5, tiles_ready(norm5))
            pe.wait_ge(s_wa, 16 * 4)
            job = 0
            for half in range(2):
                turned(pe, turn5, half)
                for m in range(HM):
                    if job >= 4:
                        pe.wait_ge(s_h5e, job - 3)
                    for k in range(KT):
                        last = pe.matmul(bank[4 + job % 4], r_w1[:, k, m * P:(m + 1) * P],
                                         xT[:, k, half * 512:(half + 1) * 512], start=(k == 0), stop=(k == KT - 1))
                    last.then_inc(s_h5, 1)
                    job += 1
            for t in range(T):
                pe.wait_ge(s_h5e, HM * (t // 4 + 1))
                if t >= 2:
                    pe.wait_ge(s_x, 4 * T + t - 1)
                for m in range(HM):
                    last = pe.matmul(bank[2 + t % 2][:, 0:D], hid5[:, m, t * P:(t + 1) * P], r_w2[:, m, :],
                                     start=(m == 0), stop=(m == HM - 1))
                last.then_inc(s_m2, 1)
            if stop <= 5:
                return

            pe_turn(pe, turn6, tiles_ready(norm6))
            turned(pe, turn6)
            pe.wait_ge(s_wb, 16 * 8)
            self_proj(sa6, [l_w[:, 0], l_w[:, 1]], 1)
            self_values(sa6, l_w[:, 2])
            self_attention(sa6)
            pe_turn(pe, turn6o, lambda half: pe.wait_ge(s_tok6, B))
            pe_gemm(pe, gemm6, turn6o)
            pe_turn(pe, turn7, lambda half: pe.wait_ge(s_y6, T))
            turned(pe, turn7)
            pe.wait_ge(s_w6, 32)
            for t in range(T):
                for k in range(KT):
                    last = pe.matmul(bank[2][:, t * ER:(t + 1) * ER], xT[:, k, t * P:(t + 1) * P], wg_l[:, k, :],
                                     start=(k == 0), stop=(k == KT - 1), skip_group_check=True)
            last.then_inc(s_log6, 1)
            pe.wait_ge(s_gate6, 1)
            for j in range(2):
                for i in range(4):
                    last = pe.transpose(bank[j][0:ER, i * P:(i + 1) * P], gate_t[:, 4 * j + i, 0:ER], ident[:, :])
                last.then_inc(s_gT6, 1)
            pe.wait_ge(s_gTe6, 2)
            for t in range(T):
                if t >= 2:
                    pe.wait_ge(s_b2e6, t - 1)
                pe.matmul(bank[2 + t % 2][:, 0:D], gateT[0:ER, t * P:(t + 1) * P], b2_l[:, :], start=True, stop=True)\
                    .then_inc(s_b26, 1)
            pe.wait_ge(s_wa, 16 * 5)
            n = 0
            for e in range(ER // 2):
                for t in range(T):
                    if n >= 4:
                        pe.wait_ge(s_wee, 2 * (n - 3))
                    for k in range(KT):
                        last = pe.matmul(bank[4 + n % 4], xT[:, k, t * P:(t + 1) * P],
                                         l_we[:, e, k, :], start=(k == 0), stop=(k == KT - 1))
                    last.then_inc(s_we, 1)
                    n += 1

        @block.scalar
        def _(act):
            act.wait_ge(s_start, 16 * N_START)
            act_dev(act, norm0)
            act_turn(act, turn0)
            for job in range(2 * W0 // P):
                half, m = divmod(job, W0 // P)
                act.wait_ge(s_q0, job + 1)
                act.activation(q0T[:, m, half * 512:(half + 1) * 512], bank[2 + job % 2], ACT.Identity,
                               bias=col("L0_xattn_Wq_b", m)).then_inc(s_q0e, 1)
            for b in range(B):
                for hf in range(2):
                    t = 2 * b + hf
                    act.wait_ge(s_lgs, t + 1)
                    act.activation(lin[hf][:, :, :], lin[hf][:, :, :], ACT.Exp).then_inc(s_lge, 1)
                for hf in range(2):
                    t = 2 * b + hf
                    for j in range(2):
                        n = 2 * t + j
                        act.wait_ge(s_lt, n + 1)
                        if j == 0 and t >= 1:
                            act.wait_ge(s_lo, t)
                        act.activation(linT[:, 4 * j:4 * j + 4, :].rearrange("p m q -> p (m q)"), bank[3], ACT.Copy)\
                            .then_inc(s_lte, 1)
            if stop <= 1:
                return
            act_dev(act, norm1)
            act_turn(act, turn1)
            act.wait_ge(s_vones, 2)
            for n, (b, c) in enumerate(proj_blocks):
                if n in (6, 12):
                    i = n // 6 - 1
                    act.wait_ge(s_at0, i + 1)
                    act.activation(sc0[:, :, :, :], sc0[:, :, :, :], ACT.Exp, scale=SCALE).then_inc(s_at0e, 1)
                for m in range(KT):
                    job = 2 * n + m
                    act.wait_ge(s_kp, job + 1)
                    if job >= 2:
                        act.wait_ge(s_klo, job - 1)
                    if job >= 3:
                        act.wait_ge(s_kst[job % 3], 64 * (job // 3))
                    act.activation(k_f[job % 2][:, :], bank[4 + job % 2], ACT.Identity, bias=col("bk_x", m))\
                        .then_inc(s_kf, 1)
                    act.activation(k_hi[job % 3][:, :], bank[4 + job % 2], ACT.Identity, bias=col("bk_x", m))\
                        .then_inc(s_kf, 1)
                for j in range(4):
                    job = 4 * n + j
                    vb, cc = divmod(job, VC)
                    act.wait_ge(s_vp, job + 1)
                    if cc == 0 and vb >= 2:
                        act.wait_ge(s_vst[vb % 2], 64 * (vb // 2))
                    dst = v_st[vb % 2][:, :, cc, :].rearrange("p g (h d) -> p g h d", d=HV)[:, :, :, 0:HD]
                    act.activation(dst, bank[6 + job % 2][:, 0:D].rearrange("p (g h d) -> p g h d", h=GH, d=HD),
                                   ACT.Copy).then_inc(s_ve, 1)
            act_turn(act, turn1o)
            if stop <= 2:
                return
            act_dev(act, norm2)
            context_stored(act)
            for t in range(T):
                norm2.wait(act, t + 1)
                if t:
                    act.wait_ge(s_sq, t)
                act.activation(junk3[:, :], u[:, t, :], ACT.Square, accum_out=var_eps[:, t:t + 1]).then_inc(s_sq, 1)
            act_dev(act, rms)
            act_turn(act, turn2)
            act.wait_ge(s_logs, 1)
            act.activation(logit[:, :, :], logit[:, :, :], ACT.Exp, scale=-1.0).then_inc(s_loge, 1)
            for j in range(2):
                act.wait_ge(s_gT, j + 1)
                act.activation(gateT[:, j * 512:(j + 1) * 512], bank[j][0:ER + ES, :], ACT.Copy).then_inc(s_gTe, 1)

            def expert(n, par, first):
                for job in range(2 * HM):
                    half, m = divmod(job, HM)
                    act.wait_ge(s_w1, n * 2 * HM + job + 1)
                    if m == 0 and not first:
                        act.wait_ge(s_w2, (n - 1) * T + 4 * (half + 1))
                    act.activation(hid[:, m, half * 512:(half + 1) * 512], bank[job % 4], ACT.Gelu,
                                   bias=b_1[par][:, m:m + 1]).then_inc(s_gelu, 1)

            act.wait_ge(s_log, 1)
            act.wait_ge(s_wexp[0], 48)
            expert(0, 0, True)
            act.wait_ge(s_wexp[1], 48)
            expert(1, 1, False)
            with act.Fori(0, ER // 2) as i:
                for par in range(2):
                    act.wait_ge(s_wexp[par], 48 * i + 96)
                    expert(2 * i + (2 + par), par, False)
            if stop <= 3:
                return
            act_dev(act, norm3)
            act_turn(act, turn3)
            for m in range(KT):
                for half in range(2):
                    job = 2 * m + half
                    act.wait_ge(s_qx, job + 1)
                    act.activation(q_hi[:, m, half * 512:(half + 1) * 512], bank[2 + job % 2], ACT.Identity,
                                   bias=col("L1_xattn_bq", m)).then_inc(s_qxh, 1)

            def exp_group(g, par, turn, first, last):
                for c in range(CH):
                    act.wait_ge(s_s2, g * CH + (c + 1))
                    if not (first and c < NP_):
                        act.wait_ge(s_pv, g * CH + (c - NP_ + 1))
                    slot = (par * CH + c) % NP_
                    act.activation(pexp[slot][:, :, :].rearrange("p h q -> p (h q)"), pair[c % 2][:, :], ACT.Exp,
                                   scale=SCALE).then_inc(s_exp, 1)

            each_group(act, exp_group)
            act_turn(act, turn3o)
            if stop <= 4:
                return

            def self_exp(sa):
                for n in range(2 * NG):
                    sa.wait(act, "s2", n + 1)
                    if n >= NP_:
                        sa.wait(act, "pv", n - NP_ + 1)
                    act.activation(pexp[n % NP_][:, :, :].rearrange("p h q -> p (h q)"), pair[n % 2][:, :], ACT.Exp,
                                   scale=SCALE).then_inc(signals["exp"].s, 1)

            act_dev(act, norm4a)
            act_dev(act, norm4b)
            act_turn(act, turn4)
            self_exp(sa5)
            act_turn(act, turn4o)
            act_dev(act, norm5)
            act_turn(act, turn5)
            for job in range(2 * HM):
                half, m = divmod(job, HM)
                act.wait_ge(s_h5, job + 1)
                act.activation(hid5[:, m, half * 512:(half + 1) * 512], bank[4 + job % 4], ACT.Relu,
                               bias=col("L1_attn_b1", m)).then_inc(s_h5e, 1)
            if stop <= 5:
                return
            act_dev(act, norm6)
            act_turn(act, turn6)
            for job in range(8):
                n, m, half = job // 4, (job // 2) % 2, job % 2
                sa6.wait(act, "fproj", job + 1)
                if job == 4:
                    sa6.wait(act, "fst", 32)
                act.activation(sa6.hi[:, m, half * 512:(half + 1) * 512], bank[4], ACT.Identity,
                               bias=col(("L1_ffn_bq", "L1_ffn_bk")[n], m)).then_inc(signals["fhi"].s, 1)
            self_exp(sa6)
            act_turn(act, turn6o)
            act_dev(act, norm6a)
            act_turn(act, turn7)
            act.wait_ge(s_logs6, 1)
            act.activation(logit[:, :, :], logit[:, :, :], ACT.Exp).then_inc(s_loge6, 1)
            for j in range(2):
                act.wait_ge(s_gT6, j + 1)
                act.activation(gateT[0:ER, j * 512:(j + 1) * 512], bank[j][0:ER, :], ACT.Copy).then_inc(s_gTe6, 1)
            act_dev(act, norm6m)

        @block.vector
        def _(dve):
            st = Steps(dve, s_dve)
            for i in range(NBUF):
                dve.memset(ctx_sb[i][:, :, D:D + 1], 1.0).then_inc(s_ones, 1)
            st.link(dve.memset(kv0[:, :, :], 0.0))
            dve.wait_ge(s_start, 16 * N_START)
            dve_norm(dve, st, norm0, x, u)

            def bcast(ap, n):
                return ap.to_broadcast(list(ap.shape[:-1]) + [n])

            def per_tile_rows(name, n=T):
                at = ROW_AT[name][0]
                return rows[:, at:at + D].rearrange("p (o d) -> p o d", o=1).to_broadcast([P, n, D])

            st.link(dve.tensor_tensor(x[:, :, :], x[:, :, :], per_tile_rows("L0_xattn_out_b"), ALU.add))
            st.settle()
            for b in range(B):
                dve.wait_ge(s_gram_blk, NCB * (b + 1))
                if b >= 1:
                    dve.wait_ge(s_gw, 6 * b)
                for m in range(KT):
                    dve.tensor_copy(gram[:, m, :], bank[m][:, 0:D + 1]).then_inc(s_grame, 1)
                dve.wait_ge(s_grame, 2 * (b + 1))
                if b >= 1:
                    for hf in range(2):
                        t = 2 * (b - 1) + hf
                        dve.wait_ge(s_lo, t + 1)
                        dve.tensor_tensor(x[:, t, :], x[:, t, :], bank[2][:, 0:D], ALU.add).then_inc(s_x, 1)
                n = 6 * b
                if b >= 1:
                    dve.wait_ge(s_kv0, 2 * b)
                for m in range(KT + 1):
                    for h in range(2):
                        hc = slice(h * 512, (h + 1) * 512)
                        dve.wait_ge(s_gw, n + 1)
                        if m < KT:
                            ins = dve.scalar_tensor_tensor(out=gw[:, m, hc], in0=row0[:, h * 512:(h + 1) * 512],
                                                           scalar=gram[:, m, D:D + 1], in1=bank[2 + n % 2],
                                                           op0=ALU.mult, op1=ALU.add)
                        else:
                            ins = dve.scalar_tensor_tensor(out=gw_row[:, hc],
                                                           in0=row0[0:1, h * 512:(h + 1) * 512],
                                                           scalar=float(S2), in1=bank[2 + n % 2][0:1, :],
                                                           op0=ALU.mult, op1=ALU.add)
                        ins.then_inc(s_gwe, 1)
                        n += 1
                if b == 0:
                    st.settle()
                if b >= 1:
                    dve.wait_ge(s_lg, 2 * b)
                for j in range(2):
                    dve.wait_ge(s_kv0, 2 * b + j + 1)
                    for i in range(2):
                        r = slice(64 * i, 64 * i + 64)
                        src = bank[2 + j][r, :].rearrange("p (m c) -> p m c", c=P)[:, :, r]
                        dve.tensor_scalar(kv0[r, 4 * j:4 * j + 4, r], src, float(DH0) ** -0.5, None, ALU.mult)\
                            .then_inc(s_kv0e, 1)
                for hf in range(2):
                    t = 2 * b + hf
                    dve.wait_ge(s_lg, t + 1)
                    lg = pair[hf][:, :].rearrange("p (h d) -> p h d", d=DH0)
                    st.link(dve.tensor_reduce(lin_max[:, hf, :], lg, X_AXIS, ALU.max))
                    st.settle()
                    if b >= 1:
                        dve.wait_ge(s_lt, 2 * t - 2)
                    dve.tensor_tensor(lin[hf][:, :, :], lg, bcast(lin_max[:, hf, :].rearrange("p (h o) -> p h o", o=1), DH0),
                                      ALU.subtract).then_inc(s_lgs, 1)
                for hf in range(2):
                    t = 2 * b + hf
                    dve.wait_ge(s_lge, t + 1)
                    st.link(dve.tensor_reduce(lin_sum[:, hf, :], lin[hf][:, :, :], X_AXIS, ALU.add))
                    st.settle()
                    st.link(dve.reciprocal(lin_sum[:, hf, :], lin_sum[:, hf, :]))
                    st.settle()
                    dve.tensor_tensor(lin[hf][:, :, :], lin[hf][:, :, :],
                                      bcast(lin_sum[:, hf, :].rearrange("p (h o) -> p h o", o=1), DH0), ALU.mult)\
                        .then_inc(s_lgn, 1)
            for t in (T - 2, T - 1):
                dve.wait_ge(s_lo, t + 1)
                dve.tensor_tensor(x[:, t, :], x[:, t, :], bank[2][:, 0:D], ALU.add).then_inc(s_x, 1)

            if stop <= 1:
                return
            dve.wait_ge(s_x, T)

            dve_norm(dve, st, norm1, x, u)
            dve.wait_ge(s_posT, 1)
            for m in range(KT):
                st.link(dve.tensor_scalar(posT[:, m, :], bank[4 + m][:, 0:R0], col("L0_attn_pos_proj_bias", m), None, ALU.add))
                st.link(dve.tensor_tensor(bqrr[:, m:m + 1], col("bq0", m), col("L0_attn_r_r_bias", m), ALU.add))
            st.settle()
            for m in range(KT):
                st.link(dve.tensor_tensor(pos_blk[:, m], bcast(posT[:, m, :].rearrange("p (j o) -> p j o", o=1), H),
                                          b_mask[:, m, :].rearrange("p (o h) -> p o h", o=1).to_broadcast([P, R0, H]), ALU.mult))
                st.link(dve.tensor_copy(bqrr_rep[:, m, :], bcast(bqrr[:, m:m + 1], P)))
            dve.wait_ge(s_rin, 16)
            st.settle()
            dve.tensor_tensor(row_in[:, 0:D], row_in[:, 0:D], row("L0_attn_r_w_bias"), ALU.add).then_inc(s_posb, 1)
            dve.wait_ge(s_relw, 1)
            for m in range(KT):
                dve.tensor_copy(rel_w[:, m, :], bank[4 + m][:, 0:R0 * H]).then_inc(s_relwe, 1)
            dve.tensor_copy(rel_bias[:, :], bank[6][:, 0:R0 * H]).then_inc(s_relwe, 1)
            dve.wait_ge(s_relwe, 3)
            dve.wait_ge(s_posb, 1)
            for t in range(T):
                dve.wait_ge(s_qkv, t + 1)
                dve.tensor_tensor(qkv[:, t, 0:512], bank[2], row_in[:, 0:512], ALU.add).then_inc(s_qkve, 1)
                dve.tensor_tensor(qkv[:, t, 512:768], bank[3][:, 0:256], row_in[:, 512:768], ALU.add).then_inc(s_qkve, 1)
                dve.tensor_tensor(rel[:, t, :], bank[7][:, 0:R0 * H], rel_bias[:, :], ALU.add).then_inc(s_qkve, 1)
            dve.wait_ge(s_qkve, 3 * T)
            for hf in range(2):
                for t in range(B):
                    tile = 2 * t + hf
                    q_b = qkv[:, tile, 0:D].rearrange("p (o d) -> p o d", o=1).to_broadcast([P, B, D])
                    k_all = qkv[:, hf:T:2, D:2 * D]
                    st.link(dve.tensor_tensor(prod[t % 2][:, :, :], q_b, k_all, ALU.mult))
                    st.settle()
                    st.link(dve.tensor_reduce(sc0[:, t].rearrange("p s h -> p (s h)"),
                                              prod[t % 2][:, :, :].rearrange("p s (h d) -> p (s h) d", d=HD), X_AXIS, ALU.add))
                    st.settle()
                    lo = (B - 1 - t) * H
                    st.link(dve.tensor_tensor(sc0[:, t].rearrange("p s h -> p (s h)"), sc0[:, t].rearrange("p s h -> p (s h)"),
                                              rel[:, tile, lo:lo + B * H], ALU.add))
                st.settle()
                by_key = sc0[:, :, :, :].rearrange("p t s h -> p t h s")
                st.link(dve.tensor_reduce(sc0_max[:, :, :], by_key, X_AXIS, ALU.max))
                st.settle()
                max_b = sc0_max[:, :, :].rearrange("p t (o h) -> p t o h", o=1).to_broadcast([P, B, B, H])
                dve.tensor_tensor(sc0[:, :, :, :], sc0[:, :, :, :], max_b, ALU.subtract).then_inc(s_at0, 1)
                dve.wait_ge(s_at0e, hf + 1)
                st.link(dve.tensor_reduce(sc0_max[:, :, :], by_key, X_AXIS, ALU.add))
                st.settle()
                st.link(dve.reciprocal(sc0_max[:, :, :], sc0_max[:, :, :]))
                st.settle()
                st.link(dve.tensor_tensor(sc0[:, :, :, :], sc0[:, :, :, :], max_b, ALU.mult))
                st.settle()
                for t in range(B):
                    tile = 2 * t + hf
                    w_b = bcast(sc0[:, t].rearrange("p s (h o) -> p s h o", o=1), HD)
                    v_all = qkv[:, hf:T:2, 2 * D:3 * D].rearrange("p s (h d) -> p s h d", d=HD)
                    st.link(dve.tensor_tensor(prod[t % 2][:, :, :].rearrange("p s (h d) -> p s h d", d=HD), v_all, w_b, ALU.mult))
                    st.settle()
                    dve.tensor_reduce(tok[:, tile, :], prod[t % 2][:, :, :].rearrange("p s f -> p f s"), X_AXIS, ALU.add)\
                        .then_inc(s_tok1, 1)
            dve.wait_ge(s_tok1, T)

            def add_out(g, dst, src):
                for t in range(T):
                    dve.wait_ge(g.mm, t + 1)
                    dve.tensor_tensor(dst[:, t, :], src[:, t, :], gemm_out(g, t), ALU.add).then_inc(g.ev, 1)

            st.link(dve.tensor_tensor(x[:, :, :], x[:, :, :], per_tile_rows("L0_attn_out_proj_bias"), ALU.add))
            st.settle()
            add_out(gemm1, x, x)
            st.link(dve.memset(score[:, :, ER:2 * ER], SENTINEL))
            if stop <= 2:
                return
            dve.wait_ge(s_x, 2 * T)

            dve_norm(dve, st, norm2, x, u)
            dve.wait_ge(s_sq, T)
            st.link(dve.tensor_scalar(var_eps[:, :], var_eps[:, :], 1.0 / D, RMS_EPS, ALU.mult, ALU.add))
            st.settle()
            dve.tensor_copy(esum[:, :], var_eps[:, :]).then_inc(s_var, 1)
            dve_rstd(dve, st, rms)
            for t in range(T):
                dve.tensor_scalar(tok[:, t, :], u[:, t, :], rstd[:, t:t + 1], None, ALU.mult).then_inc(s_un, 1)
            context_stored(dve)
            st.link(dve.tensor_tensor(rinv[:, :], rstd[:, :], var_eps[:, :], ALU.mult))
            st.settle()
            dve.wait_ge(s_log, 1)
            dve.tensor_tensor(logit[:, :, :], bank[2][:, 0:T * ER].rearrange("p (t e) -> p t e", e=ER),
                              bcast(rinv[:, :].rearrange("p (t o) -> p t o", o=1), ER), ALU.mult).then_inc(s_logs, 1)
            dve.wait_ge(s_loge, 1)
            st.link(dve.tensor_scalar(logit[:, :, :], logit[:, :, :], 1.0, None, ALU.add))
            st.settle()
            st.link(dve.reciprocal(score[:, :, 0:ER], logit[:, :, :]))
            st.settle()
            st.link(dve.tensor_reduce(esum[:, :], score[:, :, 0:ER], X_AXIS, ALU.add))
            st.settle()
            st.link(dve.reciprocal(esum[:, :], esum[:, :]))
            st.settle()

            def top_two():
                for t in range(T):
                    st.link(dve.max(top8[:, t, :], score[:, t, 0:ER]))
                st.settle()
                st.link(dve.memset(top8[:, :, 2:8], SENTINEL))
                st.settle()
                for t in range(T):
                    st.link(dve.match_replace(rest[:, t, :], top8[:, t, :], score[:, t, :], 0.0))
                st.settle()

            top_two()
            st.link(dve.tensor_tensor(gate[:, :, :].rearrange("p e t -> p t e"), score[:, :, 0:ER], rest[:, :, 0:ER], ALU.subtract))
            st.settle()
            st.link(dve.tensor_tensor(gate[:, :, :], gate[:, :, :],
                                      esum[:, :].rearrange("p (o t) -> p o t", o=1).to_broadcast([P, ER, T]), ALU.mult))
            st.link(dve.memset(gate_t[:, :, ER:ER + ES], 1.0))
            st.settle()
            dve.tensor_copy(gate_t[:, :, 0:ER], gate[:, :, :].rearrange("p e t -> p t e")).then_inc(s_gate, 1)
            for t in range(T):
                dve.wait_ge(s_b2, t + 1)
                dve.tensor_tensor(tok[:, t, :], u[:, t, :], bank[2 + t % 2][:, 0:D], ALU.add).then_inc(s_b2e, 1)
            dve.wait_ge(s_b2e, T)
            for n in range(ES):
                for t in range(T):
                    dve.wait_ge(s_w2, n * T + t + 1)
                    if n:
                        dve.wait_ge(s_acc, t + 1)
                    dve.tensor_tensor(tok[:, t, :], tok[:, t, :], bank[4 + t % 4][:, 0:D], ALU.add).then_inc(s_acc, 1)
            st.settle()
            base = st.n
            with dve.Fori(0, ER // 2) as i:
                for par in range(2):
                    dve.tensor_copy(g_now[par][:, :], gate[:, bass.ds(2 * i + par, 1), :].rearrange("p o t -> p (o t)"))\
                        .then_inc(s_dve, 1)
                    dve.wait_ge(s_dve, 2 * i + (base + par + 1))
                    for t in range(T):
                        dve.wait_ge(s_w2, (2 * i) * T + (2 + par) * T + t + 1)
                        dve.wait_ge(s_acc, (2 * i) * T + (1 + par) * T + t + 1)
                        dve.scalar_tensor_tensor(out=tok[:, t, :], in0=bank[4 + t % 4][:, 0:D],
                                                 scalar=g_now[par][:, t:t + 1], in1=tok[:, t, :],
                                                 op0=ALU.mult, op1=ALU.add).then_inc(s_acc, 1)
            st.n = base + ER
            dve.wait_ge(s_acc, (ER + ES) * T)
            for t in range(T):
                dve.tensor_tensor(x[:, t, :], x[:, t, :], tok[:, t, :], ALU.add).then_inc(s_x, 1)
            if stop <= 3:
                return
            dve.wait_ge(s_x, 3 * T)

            dve.memset(kst[0][64:128, :, :], 1.0).then_inc(s_init4, 1)
            dve.memset(kst[1][64:128, :, :], 1.0).then_inc(s_init4, 1)
            for q_ in (*qa, *qb):
                st.link(dve.memset(q_[64:128, :, :], 0.0))
            st.link(dve.memset(oT[0][:, :], 0.0))
            st.link(dve.memset(oT[1][:, :], 0.0))
            st.settle()
            for q_ in (*qa, *qb):
                dve.memset(q_[R_MASK:R_MASK + 1, :, :], UNMASK_ROW).then_inc(s_init4, 1)
            dve_norm(dve, st, norm3, x, u)
            for m in range(KT):
                for half in range(2):
                    job = 2 * m + half
                    dve.wait_ge(s_qxh, job + 1)
                    dve.scalar_tensor_tensor(out=q_lo[:, m, half * 512:(half + 1) * 512], in0=bank[2 + job % 2],
                                             scalar=col("L1_xattn_bq", m), in1=q_hi[:, m, half * 512:(half + 1) * 512],
                                             op0=ALU.add, op1=ALU.subtract).then_inc(s_qxl, 1)
            def group_max(g, i):
                dve.wait_ge(s_s1, g * S1N + (i + 1))
                dve.tensor_reduce(mx_part[:, i:i + 1], bank[i % 2], X_AXIS, ALU.max).then_inc(s_mx, 1)

            def split_max(st, src, rws, s_out):
                st.link(dve.tensor_scalar(m_neg[rws, :], src, -1.0, None, ALU.mult))
                st.settle()
                st.link(dve.tensor_copy(m_prt[rws, 0, :], m_neg[rws, :]))
                st.settle()
                st.link(dve.tensor_tensor(m_res[rws, :], m_neg[rws, :], m_prt[rws, 0, :], ALU.subtract))
                st.settle()
                st.link(dve.tensor_copy(m_prt[rws, 1, :], m_res[rws, :]))
                st.settle()
                dve.tensor_tensor(m_prt[rws, 2, :], m_res[rws, :], m_prt[rws, 1, :], ALU.subtract).then_inc(s_out, 1)

            def group_maxima(g):
                dve.wait_ge(s_mx, g * S1N + S1N)
                dve.tensor_reduce(mx[:, 0:2 * GH], mx_part[:, :].rearrange("p (j k) -> p j k", k=8), X_AXIS, ALU.max)\
                    .then_inc(s_mxa, 1)

            def group_parts(st, g, first):
                dve.wait_ge(s_mT, g + 1)
                if not first:
                    dve.wait_ge(s_mrow, g * 48)
                split_max(st, bank[3][0:2 * GH, 0:P], slice(0, 2 * GH), s_mp)

            def copy_out(s_out, par):
                for h in range(GH):
                    dve.tensor_copy(oT[par][32 * h:32 * h + HV, :], bank[2][32 * h:32 * h + HV, 0:S]).then_inc(s_out, 1)

            def normalise(st, g, s_out):
                o = bank[3][:, 256:512].rearrange("p (q h d) -> p q h d", q=2, h=GH)
                st.link(dve.reciprocal(den[:, :, :], o[:, :, :, HD]))
                st.settle()
                dst = o_grp[:, g] if isinstance(g, int) else o_grp[:, bass.ds(g, 1)].rearrange("p o q h d -> p (o q) h d")
                dve.tensor_tensor(dst, o[:, :, :, 0:HD], bcast(den[:, :, :].rearrange("p q (h o) -> p q h o", o=1), HD),
                                  ALU.mult).then_inc(s_out, 1)

            def gather(s_out, bias):
                for b in range(B):
                    src = o_grp[:, 4 * b:4 * b + 4].rearrange("p g q h d -> p q g (h d)")
                    bias_b = row(bias).rearrange("p (o g c) -> p o g c", o=1, c=GH * HD).to_broadcast([P, 2, 4, GH * HD])
                    dst = tok[:, 2 * b:2 * b + 2, :].rearrange("p q (g c) -> p q g c", c=GH * HD)
                    dve.tensor_tensor(dst, src, bias_b, ALU.add).then_inc(s_out, 1)

            for i in range(S1N):
                group_max(0, i)
            group_maxima(0)
            group_parts(st, 0, True)
            grp = Steps(dve, s_grp)
            STEPS = 5

            def group_vector(g, par, turn, first, last):
                grp.base, grp.n = g * STEPS, 0
                for c in range(CH):
                    if c == 2 and first:
                        grp.link(dve.memset(den[:, :, :], 1.0))
                    elif c == 2:
                        dve.wait_ge(s_oT, g)
                        normalise(grp, g - 1, s_on)
                    if not last and c >= FIRST_STEP:
                        lo = (c - FIRST_STEP) * K_PER_STEP
                        for i in range(lo, min(lo + K_PER_STEP, S1N)):
                            group_max(g + 1, i)
                        if lo < S1N <= lo + K_PER_STEP:
                            group_maxima(g + 1)
                if not last:
                    group_parts(grp, g + 1, False)
                    assert grp.n == STEPS
                dve.wait_ge(s_pv, g * CH + CH)
                copy_out(s_oc, par)

            each_group(dve, group_vector)
            dve.wait_ge(s_oT, NG)
            normalise(st, NG - 1, s_on)
            dve.wait_ge(s_on, NG)
            gather(s_tok3, "bv_x")
            dve.wait_ge(s_tok3, B)
            st.link(dve.tensor_tensor(x[:, :, :], x[:, :, :], per_tile_rows("L1_xattn_bo"), ALU.add))
            st.settle()
            add_out(gemm3, x, x)
            if stop <= 4:
                return
            dve.wait_ge(s_x, 4 * T)

            def self_setup(sa):
                dve.memset(sa.k[64:128, :, :], 1.0).then_inc(signals["rows_set"].s, 1)
                dve.memset(sa.q[64:128, :, :], 0.0).then_inc(signals["rows_set"].s, 1)
                dve.memset(sa.v[:, :, :, HD:HV], 1.0).then_inc(signals["rows_set"].s, 1)

            def self_take_values(sa):
                for t in range(T):
                    sa.wait(dve, "vproj", t + 1)
                    dve.tensor_copy(sa.v[:, t, :, 0:HD], bank[2 + t % 2][:, 0:D].rearrange("p (h d) -> p h d", d=HD))\
                        .then_inc(signals["vtaken"].s, 1)

            def self_attention(sa):
                for n in range(B * H):
                    hp, qt = divmod(n, 2)
                    sa.wait(dve, "s1", n + 1)
                    dst = mx[:, 4 * hp + qt:4 * hp + qt + 3:2]
                    dve.tensor_reduce(dst, bank[4 + n % 4].rearrange("p (i k) -> p i k", i=2), X_AXIS, ALU.max)\
                        .then_inc(signals["mx"].s, 1)
                sa.wait(dve, "mT", 1)
                split_max(st, bank[3][:, 0:P], slice(0, P), signals["mp"].s)
                for g in range(NG):
                    sa.wait(dve, "pv", 2 * (g + 1))
                    copy_out(signals["oc"].s, g % 2)
                    if g >= 1:
                        sa.wait(dve, "oT", g)
                        normalise(st, g - 1, signals["on"].s)
                sa.wait(dve, "oT", NG)
                normalise(st, NG - 1, signals["on"].s)
                sa.wait(dve, "on", NG)

            self_setup(sa5)
            dve_norm(dve, st, norm4a, x, u)
            dve_norm(dve, st, norm4b, u, tok)
            dve.wait_ge(s_rope, 32)
            for job in range(8):
                n, m, half = job // 4, (job // 2) % 2, job % 2
                i = job % 2
                sa5.wait(dve, "fproj", job + 1)
                if job >= 1:
                    sa5.wait(dve, "flo", job)
                if job == 4:
                    sa5.wait(dve, "fst", 32)
                tb = lambda ap: ap[:, :].rearrange("p (o q) -> p o q", o=1).to_broadcast([P, 2, S])
                v2 = lambda ap: ap.rearrange("p (b q) -> p b q", b=2)
                st.link(dve.scalar_tensor_tensor(out=v2(rot_a[i][:, :]), in0=v2(bank[4]), scalar=col(("L1_attn_bq", "L1_attn_bk")[n], m),
                                                 in1=tb(cosT), op0=ALU.add, op1=ALU.mult))
                st.link(dve.scalar_tensor_tensor(out=v2(rot_b[i][:, :]), in0=v2(bank[5]), scalar=col(("bq_swapped", "bk_swapped")[n], m),
                                                 in1=tb(sinT), op0=ALU.add, op1=ALU.mult))
                st.settle()
                st.link(dve.tensor_tensor(rot_a[i][:, :], rot_a[i][:, :], rot_b[i][:, :], ALU.add))
                st.settle()
                hc = slice(half * 512, (half + 1) * 512)
                st.link(dve.tensor_copy(sa5.hi[:, m, hc], rot_a[i][:, :]))
                st.settle()
                dve.tensor_tensor(sa5.lo[:, m, hc], rot_a[i][:, :], sa5.hi[:, m, hc], ALU.subtract).then_inc(signals["flo"].s, 1)
            self_take_values(sa5)
            self_attention(sa5)
            gather(s_tok4, "L1_attn_bv")
            dve.wait_ge(s_tok4, B)
            st.link(dve.tensor_tensor(u[:, :, :], u[:, :, :], per_tile_rows("L1_attn_bo"), ALU.add))
            st.settle()
            add_out(gemm4, u, u)
            dve.wait_ge(gemm4.ev, T)
            dve_norm(dve, st, norm5, u, tok)
            st.link(dve.tensor_tensor(x[:, :, :], x[:, :, :], u[:, :, :], ALU.add))
            st.settle()
            st.link(dve.tensor_tensor(x[:, :, :], x[:, :, :], per_tile_rows("L1_attn_b2"), ALU.add))
            st.settle()
            for t in range(T):
                dve.wait_ge(s_m2, t + 1)
                dve.tensor_tensor(x[:, t, :], x[:, t, :], bank[2 + t % 2][:, 0:D], ALU.add).then_inc(s_x, 1)
            if stop <= 5:
                return
            dve.wait_ge(s_x, 5 * T)

            self_setup(sa6)
            dve_norm(dve, st, norm6, x, u)
            for job in range(8):
                n, m, half = job // 4, (job // 2) % 2, job % 2
                hc = slice(half * 512, (half + 1) * 512)
                sa6.wait(dve, "fhi", job + 1)
                dve.scalar_tensor_tensor(out=sa6.lo[:, m, hc], in0=bank[4], scalar=col(("L1_ffn_bq", "L1_ffn_bk")[n], m),
                                         in1=sa6.hi[:, m, hc], op0=ALU.add, op1=ALU.subtract).then_inc(signals["flo"].s, 1)
            self_take_values(sa6)
            self_attention(sa6)
            gather(s_tok6, "L1_ffn_bv")
            for t in range(T):
                dve.wait_ge(gemm6.mm, t + 1)
                dve.tensor_tensor(tok[:, t, :], gemm_out(gemm6, t), row("L1_ffn_bo"), ALU.add).then_inc(gemm6.ev, 1)
            dve.wait_ge(gemm6.ev, T)
            dve_norm(dve, st, norm6a, tok, tok)
            st.link(dve.tensor_tensor(tok[:, :, :], tok[:, :, :], per_tile_rows("L1_ffn_g1"), ALU.mult))
            st.settle()
            st.link(dve.tensor_tensor(tok[:, :, :], tok[:, :, :], per_tile_rows("L1_ffn_be1"), ALU.add))
            st.settle()
            for t in range(T):
                dve.tensor_tensor(u[:, t, :], u[:, t, :], tok[:, t, :], ALU.add).then_inc(s_y6, 1)
            dve.wait_ge(s_y6, T)
            st.link(dve.tensor_tensor(x[:, :, :], x[:, :, :], u[:, :, :], ALU.add))
            st.settle()
            st.link(dve.tensor_tensor(x[:, :, :], x[:, :, :], per_tile_rows("L1_ffn_be2"), ALU.add))
            st.settle()
            dve.wait_ge(s_log6, 1)
            st.link(dve.tensor_tensor(logit[:, :, :], bank[2][:, 0:T * ER].rearrange("p (t e) -> p t e", e=ER),
                                      row("L1_ffn_bg").rearrange("p (o e) -> p o e", o=1).to_broadcast([P, T, ER]), ALU.add))
            st.settle()
            st.link(dve.tensor_reduce(esum[:, :], logit[:, :, :], X_AXIS, ALU.max))
            st.settle()
            esum_b = bcast(esum[:, :].rearrange("p (t o) -> p t o", o=1), ER)
            dve.tensor_tensor(logit[:, :, :], logit[:, :, :], esum_b, ALU.subtract).then_inc(s_logs6, 1)
            dve.wait_ge(s_loge6, 1)
            st.link(dve.tensor_reduce(esum[:, :], logit[:, :, :], X_AXIS, ALU.add))
            st.settle()
            st.link(dve.reciprocal(esum[:, :], esum[:, :]))
            st.settle()
            st.link(dve.tensor_tensor(score[:, :, 0:ER], logit[:, :, :], esum_b, ALU.mult))
            st.settle()
            top_two()
            dve.tensor_tensor(gate_t[:, :, 0:ER], score[:, :, 0:ER], rest[:, :, 0:ER], ALU.subtract).then_inc(s_gate6, 1)
            for t in range(T):
                dve.wait_ge(s_b26, t + 1)
                dve.tensor_copy(tok[:, t, :], bank[2 + t % 2][:, 0:D]).then_inc(s_b2e6, 1)
            dve.wait_ge(s_b2e6, T)
            dve.wait_ge(s_gate6, 1)
            n = 0
            for e in range(ER // 2):
                for t in range(T):
                    dve.wait_ge(s_we, n + 1)
                    for j in range(2):
                        if e or j:
                            dve.wait_ge(s_wee, 2 * n + 1 if j else 2 * (n - T) + 2)
                        dve.scalar_tensor_tensor(out=tok[:, t, :], in0=bank[4 + n % 4][:, j * D:(j + 1) * D],
                                                 scalar=gate_t[:, t, 2 * e + j:2 * e + j + 1], in1=tok[:, t, :],
                                                 op0=ALU.mult, op1=ALU.add).then_inc(s_wee, 1)
                    n += 1
            dve.wait_ge(s_wee, ER * T)
            dve_norm(dve, st, norm6m, tok, tok)
            st.link(dve.tensor_tensor(tok[:, :, :], tok[:, :, :], per_tile_rows("L1_ffn_g2"), ALU.mult))
            st.settle()
            for t in range(T):
                dve.tensor_tensor(x[:, t, :], x[:, t, :], tok[:, t, :], ALU.add).then_inc(s_x, 1)
            dve.wait_ge(s_x, 6 * T)

        @block.gpsimd
        def _(pool):
            if stop <= 1:
                return
            pool.wait_ge(s_x, T)
            for i in range(2):
                pool.memset(v_st[i][:, :, :, :], 1.0).then_inc(s_vones, 1)
            pool.wait_ge(s_m8, 16)
            pool.tensor_scalar(m_16[:, :], m_u32[:, :].bitcast(U8), MASKED, None, ALU.mult).then_inc(s_m16, 1)
            pool.wait_ge(s_m16, 1)
            for j in range(H // GH):
                pool.dma_start(mask_scr.rearrange("(b j) n -> j b n", b=B)[j], m_16[:, :]).then_inc(s_mst, 16)
            for n, (b, c) in enumerate(proj_blocks):
                for m in range(KT):
                    job = 2 * n + m
                    i = job % 3
                    pool.wait_ge(s_kf, 2 * (job + 1))
                    if job >= 3:
                        pool.wait_ge(s_kst[i], 64 * (job // 3))
                    pool.tensor_tensor(k_lo[i][:, :], k_f[job % 2][:, :], k_hi[i][:, :], ALU.subtract).then_inc(s_klo, 1)


def kernel(**inputs):
    import concourse.bacc as bacc
    from concourse.bass_utils import run_bass_kernel_spmd as run

    i = {n: np.asarray(v) for n, v in inputs.items()}

    def t(name):
        return i[name].T

    pos_in_head = np.arange(P) % HD
    inv_freq = np.float32(1.0) / np.float32(10000.0) ** (np.arange(0, HD, 2, dtype=np.float32) / np.float32(HD))
    angles = np.arange(S, dtype=np.float32)[None, :] * inv_freq[pos_in_head // 2][:, None]
    signs = np.where(pos_in_head % 2 == 0, -1.0, 1.0)[:, None]
    swap = np.arange(D) ^ 1
    named = {
        **{n: i[n] for n in ("L0_xattn_Wq_b", "L0_attn_pos_proj_bias", "L0_ffn_g_shared", "L0_ffn_g_routed",
                             "L1_xattn_bq", "L1_attn_g1", "L1_attn_beta1", "L1_attn_g2", "L1_attn_beta2",
                             "L1_attn_bq", "L1_attn_bk", "L1_attn_b1", "L1_ffn_bq", "L1_ffn_bk", "L0_xattn_out_b",
                             "L0_attn_in_proj_bias", "L0_attn_out_proj_bias", "L1_xattn_bo", "L1_attn_bv",
                             "L1_attn_bo", "L1_attn_b2", "L1_ffn_bv", "L1_ffn_bo", "L1_ffn_g1", "L1_ffn_be1",
                             "L1_ffn_g2", "L1_ffn_be2", "L1_ffn_bg")},
        "bq0": i["L0_attn_in_proj_bias"][0:D],
        "L0_attn_r_r_bias": i["L0_attn_r_r_bias"].reshape(-1),
        "L0_attn_r_w_bias": i["L0_attn_r_w_bias"].reshape(-1),
        "bk_x": i["L1_xattn_bkv"][0:D],
        "bv_x": i["L1_xattn_bkv"][D:2 * D],
        "bq_swapped": i["L1_attn_bq"][swap],
        "bk_swapped": i["L1_attn_bk"][swap],
    }
    arrays = {
        "x": i["x"], "ctx": i["ctx_1024"], "ctxT": i["ctx_1024"].transpose(0, 2, 1),
        "mask": i["mask_BxS2_bk0"].view(np.uint32),
        "ident": np.eye(P, dtype=np.float32),
        "cols": np.concatenate([named[n.split(":")[0]].reshape(-1, P).T for n in COLS], axis=1),
        "rows": np.concatenate([named[n.split(":")[0]] for n in ROWS])[None, :],
        "row0": i["L0_xattn_Wq_b"][None, :], "row_in": i["L0_attn_in_proj_bias"][None, :],
        "w0qT": t("L0_xattn_Wq_w"), "w0oT": t("L0_xattn_out_w"),
        "w1inT": t("L0_attn_in_proj_weight"), "w1q": i["L0_attn_in_proj_weight"][0:D],
        "w1oT": t("L0_attn_out_proj_weight"), "w1pT": t("L0_attn_pos_proj_weight"),
        "posT": i["L0_attn_pos"][0:R0, 0, :].T,
        "head_mask": (np.arange(D)[:, None] // HD == np.arange(H)[None, :]).astype(np.float32),
        "wkv": i["L1_xattn_Wkv"], "wq_x": i["L1_xattn_Wq"], "wo_x": i["L1_xattn_Wo"],
        "cent": i["L0_ffn_centroids"],
        "b2_all": np.concatenate([i["L0_ffn_b2_r"], i["L0_ffn_b2_s"]]),
        "w1_all": np.concatenate([i["L0_ffn_W1_r"], i["L0_ffn_W1_s"]]),
        "w2_all": np.concatenate([i["L0_ffn_W2_r"], i["L0_ffn_W2_s"]]),
        "b1_all": np.concatenate([i["L0_ffn_b1_r"], i["L0_ffn_b1_s"]]).reshape(ER + ES, HM, P).transpose(0, 2, 1),
        "r_w": np.stack([i["L1_attn_Wq"], i["L1_attn_Wq"][:, swap], i["L1_attn_Wk"], i["L1_attn_Wk"][:, swap],
                         i["L1_attn_Wv"], i["L1_attn_Wo"]]),
        "r_w1": i["L1_attn_W1"], "r_w2": i["L1_attn_W2"],
        "cosT": np.cos(angles).astype(np.float32), "sinT": (np.sin(angles) * signs).astype(np.float32),
        "l_w": np.stack([i["L1_ffn_Wq"], i["L1_ffn_Wk"], i["L1_ffn_Wv"], i["L1_ffn_Wo"]]),
        "l_we": i["L1_ffn_We"].reshape(ER // 2, 2, D, D).transpose(0, 2, 1, 3).reshape(ER // 2, D, 2 * D),
        "wg": i["L1_ffn_Wg"], "bexp": i["L1_ffn_bexp"],
    }
    nc = bacc.Bacc("TRN2", target_bir_lowering=False, num_devices=1)
    held, aps = {}, {}
    for name, v in arrays.items():
        v = np.ascontiguousarray(v)
        held[f"in_{name}"] = v
        aps[name] = nc.dram_tensor(f"in_{name}", v.shape, mybir.dt.from_np(v.dtype), kind="ExternalInput").ap()
    out = nc.dram_tensor("out", (B, S, D), F32, kind="ExternalOutput").ap()
    build(nc, aps, out)
    r = run(nc, [held], core_ids=[0])
    return r.results[0]["out"]
```

```python
from contextlib import ExitStack

import numpy as np

import concourse.bass as bass
from concourse import mybir

F32 = mybir.dt.float32
F16 = mybir.dt.float16
U8 = mybir.dt.uint8
U32 = mybir.dt.uint32
ALU = mybir.AluOpType
ACT = mybir.ActivationFunctionType
X_AXIS = mybir.AxisListType.X

P = 128
B, S, D, S2 = 4, 256, 256, 4096
T = B * S // P
KT = D // P
NTOK = B * S
H, HD = 16, 16
H0, DH0 = 16, 64
W0 = H0 * DH0
R0 = 2 * B - 1
HID = 1024
HM = HID // P
WPIECES = 2 * KT * HID // 512
W_SCALE = 1024.0
ER, ES = 8, 2
LN_EPS = 1e-5
RMS_EPS = float(np.finfo(np.float32).eps)
SCALE = float(HD) ** -0.5
GH = 4
NG = B * H // GH
CH = S2 // P
KB = 1024
NKB = S2 // KB
MASKED, UNMASK_ROW = -60000.0, 16384.0
R_MASK, R_MAX = 64, 65
SENTINEL = -5.0
HV = HD + 1

COLS = ["L0_xattn_Wq_b:8", "L0_attn_pos_proj_bias:2", "bq0:2", "L0_attn_r_r_bias:2", "L0_ffn_g_shared:2",
        "L0_ffn_g_routed:2", "L1_xattn_bq:2", "bk_x:2", "L1_attn_g1:2", "L1_attn_beta1:2", "L1_attn_g2:2",
        "L1_attn_beta2:2", "L1_attn_bq:2", "L1_attn_bk:2", "bq_swapped:2", "bk_swapped:2", "L1_attn_b1:8",
        "L1_ffn_bq:2", "L1_ffn_bk:2"]
ROWS = ["L0_xattn_out_b:256", "L0_attn_r_w_bias:256",
        "L0_attn_out_proj_bias:256", "bv_x:256", "L1_xattn_bo:256", "L1_attn_bv:256", "L1_attn_bo:256",
        "L1_attn_b2:256", "L1_ffn_bv:256", "L1_ffn_bo:256", "L1_ffn_g1:256", "L1_ffn_be1:256",
        "L1_ffn_g2:256", "L1_ffn_be2:256", "L1_ffn_bg:8"]


def offsets(names):
    at, out = 0, {}
    for n in names:
        name, width = n.split(":")
        out[name] = (at, int(width))
        at += int(width)
    return out, at


COL_AT, NCOLS = offsets(COLS)
ROW_AT, NROWS = offsets(ROWS)


def build(nc, a, out, stop=99):
    with ExitStack() as top:
        def sem(name):
            return top.enter_context(nc.semaphore(name))

        def sb(name, shape, dt=F32, scope=top):
            return scope.enter_context(nc.sbuf_tensor(name, shape, dt))

        def dram(name, shape, dt):
            return nc.dram_tensor(name, shape, dt, kind="Internal").ap()

        k_scr = dram("k_scr", [B, H // GH, 2, GH * HD, S2], F16)
        q_scr = dram("q_scr", [B, H // GH, 2, GH * HD, S], F16)
        v_scr = dram("v_scr", [NG, P, CH, GH * HV], F32)
        mask_scr = dram("mask_scr", [NG, S2], F16)
        self_scr = [dram(f"self_scr{i}", [2, 2, D, NTOK], F16) for i in range(2)]

        x = sb("x", [P, T, D])
        u = sb("u", [P, T, D])
        tok = sb("tok", [P, T, D])
        xT = sb("xT", [P, KT, NTOK])
        ident = sb("ident", [P, P])
        cols = sb("cols", [P, NCOLS])
        rows = sb("rows", [P, NROWS])
        stats = sb("stats", [P, T, 6])
        meanvar = sb("meanvar", [P, T, 2])
        var_eps = sb("var_eps", [P, T])
        deviation = sb("deviation", [P, T])
        rstd = sb("rstd", [P, T])
        rtmp = sb("rtmp", [P, T])
        logit = sb("logit", [P, T, ER])
        score = sb("score", [P, T, 2 * ER])
        top8 = sb("top8", [P, T, 8])
        rest = sb("rest", [P, T, 2 * ER])
        esum = sb("esum", [P, T])
        gate = sb("gate", [P, ER, T])
        gate_t = sb("gate_t", [P, T, ER + ES])
        gateT = sb("gateT", [ER + ES, NTOK])
        wkv = sb("wkv", [P, KT, 2 * D])
        wqo_x = sb("wqo_x", [P, 2, KT, D])
        wb = sb("wb", [P, 4096])

        def col(name, i):
            at = COL_AT[name][0] + i
            return cols[:, at:at + 1]

        def row(name, lo=0, hi=None, parts=slice(0, P)):
            at, n = ROW_AT[name]
            return rows[parts, at + lo:at + (n if hi is None else hi)]

        psum = [top.enter_context(nc.psum_tensor(f"bank{i}", [P, 512], F32)) for i in range(4)]
        pair = [top.enter_context(nc.psum_tensor(f"pair{i}", [P, 1024], F32)) for i in range(2)]
        bank = psum + [pair[0][:, 0:512], pair[0][:, 512:1024], pair[1][:, 0:512], pair[1][:, 512:1024]]
        bank = [b_[:, :] for b_ in bank]

        b_in = wb[:, 0:1536].rearrange("p (k n) -> p k n", k=KT)
        b_q = wb[:, 1536:2048].rearrange("p (k n) -> p k n", k=KT)
        b_o = wb[:, 2048:2560].rearrange("p (k n) -> p k n", k=KT)
        b_p = wb[:, 2560:3072].rearrange("p (k n) -> p k n", k=KT)
        b_pos = wb[:, 3072:3072 + KT * R0].rearrange("p (k n) -> p k n", k=KT)
        b_mask = wb[:, 3100:3100 + KT * H].rearrange("p (k n) -> p k n", k=KT)
        r_w = wb[:, 0:3072].rearrange("p (w k n) -> p w k n", w=6, k=KT)
        l_w = wb[:, 0:2048].rearrange("p (w k n) -> p w k n", w=4, k=KT)

        s_start = sem("inputs_loaded")
        s_wa = sem("large_weights_loaded")
        s_wb = sem("weight_area_loaded")
        s_wkv = sem("cross_weights_loaded")
        s_dve = sem("vector_steps")
        s_x = sem("residual_updated")
        s_store = sem("output_stored")

        s_var = sem("norm_variance")
        s_dev = sem("norm_deviation")
        s_nt = sem("norm_tiles")
        s_tmm = sem("tiles_transposed")
        s_tev = sem("transposes_copied")
        counted = {"norms": 0, "normed": 0, "turned": 0, "copied": 0}

        class Norm:

            def __init__(self, tiles=T):
                self.root, self.tiles = counted["norms"], counted["normed"]
                counted["norms"] += 1
                counted["normed"] += tiles

            def wait(self, eng, n):
                eng.wait_ge(s_nt, self.tiles + n)

        class Turn:

            def __init__(self, src, dests):
                self.src, self.dests = src, dests
                self.mm, self.ev = counted["turned"], counted["copied"]
                counted["turned"] += 4
                counted["copied"] += 4 * len(dests)

        class Steps:

            def __init__(self, eng, s):
                self.eng, self.s, self.n, self.base = eng, s, 0, 0

            def link(self, ins):
                ins.then_inc(self.s, 1)
                self.n += 1

            def settle(self):
                self.eng.wait_ge(self.s, self.base + self.n)

        def dve_rstd(dve, st, nm):
            dve.wait_ge(s_dev, nm.root + 1)
            st.link(dve.reciprocal(rstd[:, :], deviation[:, :]))
            st.settle()
            st.link(dve.tensor_tensor(rtmp[:, :], rstd[:, :], rstd[:, :], ALU.mult))
            st.settle()
            st.link(dve.tensor_tensor(rtmp[:, :], rtmp[:, :], var_eps[:, :], ALU.mult))
            st.settle()
            st.link(dve.tensor_scalar(rtmp[:, :], rtmp[:, :], -0.5, 1.5, ALU.mult, ALU.add))
            st.settle()
            st.link(dve.tensor_tensor(rstd[:, :], rstd[:, :], rtmp[:, :], ALU.mult))
            st.settle()

        def dve_norm(dve, st, nm, src, dst):
            for t in range(T):
                st.link(dve.bn_stats(stats[:, t, :], src[:, t, :]))
            st.settle()
            for t in range(T):
                st.link(dve.bn_aggr(meanvar[:, t, :], stats[:, t, :]))
            st.settle()
            dve.tensor_scalar(var_eps[:, :], meanvar[:, :, 1], LN_EPS, None, ALU.add).then_inc(s_var, 1)
            dve.wait_ge(s_var, nm.root + 1)
            dve_rstd(dve, st, nm)
            for t in range(T):
                dve.tensor_scalar(dst[:, t, :], src[:, t, :], meanvar[:, t, 0:1], rstd[:, t:t + 1],
                                  ALU.subtract, ALU.mult).then_inc(s_nt, 1)
            nm.wait(dve, T)

        def act_dev(act, nm):
            act.wait_ge(s_var, nm.root + 1)
            act.activation(deviation[:, :], var_eps[:, :], ACT.Sqrt).then_inc(s_dev, 1)

        def pe_turn(pe, tr, ready):
            for half in range(2):
                ready(half)
                for k in range(KT):
                    job = 2 * half + k
                    if job >= 2:
                        pe.wait_ge(s_tev, tr.ev + len(tr.dests) * (job - 1))
                    for j in range(4):
                        last = pe.transpose(bank[job % 2][:, j * P:(j + 1) * P],
                                            tr.src[:, 4 * half + j, k * P:(k + 1) * P], ident[:, :])
                    last.then_inc(s_tmm, 1)

        def act_turn(act, tr):
            for half in range(2):
                for k in range(KT):
                    job = 2 * half + k
                    act.wait_ge(s_tmm, tr.mm + job + 1)
                    for dst, scale, bias in tr.dests:
                        o = dst[:, k, half * 512:(half + 1) * 512]
                        if scale is None:
                            act.activation(o, bank[job % 2], ACT.Copy).then_inc(s_tev, 1)
                        elif bias is None:
                            act.activation(o, bank[job % 2], ACT.Copy, scale=col(scale, k)).then_inc(s_tev, 1)
                        else:
                            act.activation(o, bank[job % 2], ACT.Identity, scale=col(scale, k),
                                           bias=col(bias, k)).then_inc(s_tev, 1)

        def turned(eng, tr, half=1):
            eng.wait_ge(s_tev, tr.ev + len(tr.dests) * 2 * (half + 1))

        class Gemm:

            def __init__(self, name, lhs, w, residual=None):
                self.lhs, self.w, self.kt, self.banks = lhs, w, KT, (2, 3)
                self.mm = sem(f"{name}_product")
                self.ev = sem(f"{name}_taken") if residual is None else s_x
                self.base = 0 if residual is None else residual * T

        def pe_gemm(pe, g, tr):
            n = g.w.shape[2]
            for t in range(T):
                if t % 4 == 0:
                    turned(pe, tr, t // 4)
                if t >= len(g.banks):
                    pe.wait_ge(g.ev, g.base + t - len(g.banks) + 1)
                for k in range(g.kt):
                    last = pe.matmul(bank[g.banks[t % len(g.banks)]][:, 0:n], g.lhs[:, k, t * P:(t + 1) * P],
                                     g.w[:, k, :], start=(k == 0), stop=(k == g.kt - 1))
                last.then_inc(g.mm, 1)

        def gemm_out(g, t):
            return bank[g.banks[t % len(g.banks)]][:, 0:g.w.shape[2]]

        with ExitStack() as sc:
            CB = 8
            NCB = S2 // P // CB
            NBUF = 3
            w0q = sb("w0q", [P, KT, W0], F32, sc)
            w0o = sb("w0o", [P, W0 // P, D], F32, sc)
            row0 = sb("row0", [P, W0], F32, sc)
            ctx_sb = [sb(f"ctx_sb{i}", [P, CB, D + 1], F32, sc) for i in range(NBUF)]
            q0T = sb("q0T", [P, W0 // P, NTOK], F32, sc)
            gram = sb("gram", [P, KT, D + 1], F32, sc)
            gw = sb("gw", [P, KT, W0], F32, sc)
            gw_row = sb("gw_row", [1, W0], F32, sc)
            kv0 = sb("kv0", [P, H0 // 2, P], F32, sc)
            lin = [sb(f"lin{i}", [P, H0, DH0], F32, sc) for i in range(2)]
            lin_max = sb("lin_max", [P, 2, H0], F32, sc)
            lin_sum = sb("lin_sum", [P, 2, H0], F32, sc)
            linT = sb("linT", [P, W0 // P, P], F32, sc)
        norm0 = Norm()
        turn0 = Turn(u, [(xT, None, None)])
        s_ctx = [sem(f"ctx_loaded{i}") for i in range(NBUF)]
        s_ones = sem("ctx_ones_set")
        s_gram_blk = sem("ctx_block_used")
        s_q0 = sem("q0_product")
        s_q0e = sem("q0_copied")
        s_grame = sem("gram_copied")
        s_gw = sem("gram_w_product")
        s_gwe = sem("gram_w_copied")
        s_kv0 = sem("kv0_product")
        s_kv0e = sem("kv0_copied")
        s_lg = sem("linear_logits")
        s_lgs = sem("linear_logits_shifted")
        s_lge = sem("linear_exp")
        s_lgn = sem("linear_weights")
        s_lt = sem("linear_transposed")
        s_lte = sem("linear_transposes_copied")
        s_lo = sem("linear_out")

        with ExitStack() as sc:
            qkv = sb("qkv", [P, T, 3 * D], F32, sc)
            rel = sb("rel", [P, T, R0 * H], F32, sc)
            posT = sb("posT", [P, KT, R0], F32, sc)
            pos_blk = sb("pos_blk", [P, KT, R0, H], F32, sc)
            rel_w = sb("rel_w", [P, KT, R0 * H], F32, sc)
            rel_bias = sb("rel_bias", [P, R0 * H], F32, sc)
            bqrr = sb("bqrr", [P, KT], F32, sc)
            bqrr_rep = sb("bqrr_rep", [P, KT, P], F32, sc)
            row_in = sb("row_in", [P, 3 * D], F32, sc)
            prod = [sb(f"prod{i}", [P, B, D], F32, sc) for i in range(2)]
            sc0 = sb("sc0", [P, B, B, H], F32, sc)
            sc0_max = sb("sc0_max", [P, B, H], F32, sc)
            cT = [sb(f"cT{i}", [P, KT, 512], F32, sc) for i in range(3)]
            k_f = [sb(f"k_f{i}", [P, 512], F32, sc) for i in range(2)]
            k_hi = [sb(f"k_hi{i}", [P, 512], F16, sc) for i in range(3)]
            k_lo = [sb(f"k_lo{i}", [P, 512], F16, sc) for i in range(3)]
            VC = CH // 4
            v_st = [sb(f"v_st{i}", [P, H // GH, VC, GH * HV], F32, sc) for i in range(2)]
            m_u32 = sb("m_u32", [B, S2 // 4], U32, sc)
            m_16 = sb("m_16", [B, S2], F16, sc)
        norm1 = Norm()
        turn1 = Turn(u, [(xT, None, None)])
        s_rin = sem("in_proj_bias_loaded")
        s_posT = sem("pos_product")
        s_posb = sem("pos_blocks")
        s_relw = sem("rel_w_product")
        s_relwe = sem("rel_w_copied")
        s_qkv = sem("qkv_product")
        s_qkve = sem("qkv_taken")
        s_at0 = sem("batch_scores_shifted")
        s_at0e = sem("batch_exp")
        s_tok1 = sem("batch_context_tiles")
        turn1o = Turn(tok, [(xT, None, None)])
        gemm1 = Gemm("out1", xT, b_o, residual=1)
        s_cT = [sem(f"ctxT_loaded{i}") for i in range(3)]
        s_kp = sem("k_product")
        s_kf = sem("k_copied")
        s_klo = sem("k_low_part")
        s_kst = [sem(f"k_stored{i}") for i in range(3)]
        s_vp = sem("v_product")
        s_ve = sem("v_copied")
        s_vst = [sem(f"v_stored{i}") for i in range(2)]
        s_vones = sem("v_ones_set")
        s_m8 = sem("mask_loaded")
        s_m16 = sem("mask_row")
        s_mst = sem("mask_stored")

        with ExitStack() as sc:
            xTs = sb("xTs", [P, KT, NTOK], F32, sc)
            junk3 = sb("junk3", [P, D], F32, sc)
            w_f = sb("w_f", [P, WPIECES, 512], F32, sc)
            w_part = [[sb(f"w_{part}{i}", [P, WPIECES, 512], F16, sc) for i in range(2)] for part in ("hi", "lo")]
            b_1 = [sb(f"b_1{i}", [P, HM], F32, sc) for i in range(2)]
            x_part = [[sb(f"x_{src}_{part}", [P, KT, NTOK], F16, sc) for part in ("hi", "lo")] for src in ("s", "r")]
            hid_f = sb("hid_f", [P, 4, 512], F32, sc)
            hid_part = [sb(f"hid_{part}", [P, HM, NTOK], F16, sc) for part in ("hi", "lo")]
            xTr = hid_f[:, :, :].rearrange("p (k a) n -> p k (a n)", k=KT)
            cent = sb("cent", [P, KT, ER], F32, sc)
            b2_all = sb("b2_all", [ER + ES, D], F32, sc)
            rinv = sb("rinv", [P, T], F32, sc)
            g_now = [sb(f"g_now{i}", [P, T], F32, sc) for i in range(2)]
        norm2 = Norm()
        rms = Norm(tiles=0)
        s_sq = sem("squares_summed")
        s_un = sem("rms_tiles")
        turn2 = Turn(tok, [(xTs, "L0_ffn_g_shared", None), (xT, "L0_ffn_g_routed", None), (xTr, None, None)])
        s_w3 = sem("router_weights_loaded")
        s_wexp = sem("expert_loaded")
        s_whi = sem("expert_weights_high")
        s_wlo = sem("expert_weights_low")
        s_xlo = sem("expert_inputs_parts")
        s_hhi = sem("expert_hidden_high")
        s_hlo = sem("expert_hidden_low")
        s_log = sem("router_logits")
        s_logs = sem("router_logits_scaled")
        s_loge = sem("router_exp")
        s_gate = sem("gates_ready")
        s_gT = sem("gates_transposed")
        s_gTe = sem("gates_copied")
        s_b2 = sem("b2_product")
        s_b2e = sem("b2_taken")
        s_w1 = sem("expert_hidden_product")
        s_gelu = sem("expert_hidden")
        s_w2 = sem("expert_out_product")
        s_acc = sem("expert_accumulated")

        attention_scope = ExitStack()
        NP_ = 4
        pexp = [sb(f"pexp{i}", [P, GH, S], F32, attention_scope) for i in range(NP_)]
        mx_part = sb("mx_part", [P, GH * 2 * (S2 // 512)], F32, attention_scope)
        mx = sb("mx", [P, 128], F32, attention_scope)
        m_neg = sb("m_neg", [P, P], F32, attention_scope)
        m_res = sb("m_res", [P, P], F32, attention_scope)
        m_prt = sb("m_prt", [P, 3, P], F16, attention_scope)
        oT = [sb(f"oT{i}", [P, S], F32, attention_scope) for i in range(2)]
        o_grp = sb("o_grp", [P, NG, 2, GH, HD], F32, attention_scope)
        den = sb("den", [P, 2, GH], F32, attention_scope)
        with ExitStack() as sc:
            q_hi = sb("q_hi", [P, KT, NTOK], F16, sc)
            q_lo = sb("q_lo", [P, KT, NTOK], F16, sc)
            kst = [sb(f"kst{i}", [P, GH, S2], F16, sc) for i in range(2)]
            qa = [sb(f"qa{i}", [P, GH, S], F16, sc) for i in range(2)]
            qb = [sb(f"qb{i}", [P, GH, S], F16, sc) for i in range(2)]
            vst = [sb(f"vst{i}", [P, CH, GH * HV], F32, sc) for i in range(2)]
        norm3 = Norm()
        turn3 = Turn(u, [(xT, None, None)])
        s_qx = sem("cross_q_product")
        s_qxh = sem("cross_q_high")
        s_qxl = sem("cross_q_low")
        s_qst = sem("cross_q_stored")
        s_init4 = sem("stack_rows_set")
        s_qz = sem("query_rows_zeroed")
        s_qa = [sem(f"group_queries_loaded{i}") for i in range(2)]
        s_qb = [sem(f"group_queries_again_loaded{i}") for i in range(2)]
        s_kh = [[sem(f"group_keys{f}_loaded{i}") for f in range(2)] for i in range(2)]
        s_vl = [sem(f"group_values_loaded{i}") for i in range(2)]
        s_s1 = sem("scores_first_pass")
        s_mx = sem("partial_maxima")
        s_mxa = sem("group_maxima")
        s_mT = sem("maxima_transposed")
        s_mp = sem("maxima_parts")
        s_mrow = sem("maxima_rows_stored")
        s_s2 = sem("scores_second_pass")
        s_exp = sem("weights")
        s_pv = sem("weighted_values")
        s_oc = sem("weighted_values_copied")
        s_oT = sem("weighted_values_transposed")
        s_on = sem("group_normalised")
        s_grp = sem("group_vector_steps")
        turn3o = Turn(tok, [(xT, None, None)])
        gemm3 = Gemm("out3", xT, wqo_x[:, 1], residual=3)
        s_tok3 = sem("cross_context_tiles")

        class Counted:

            def __init__(self, name, each):
                self.s, self.each = sem("self_" + name), each

        signals = {
            "fproj": Counted("qk_product", 8), "fhi": Counted("high_parts", 0),
            "flo": Counted("low_parts", 8),
            "fst": Counted("parts_stored", 64), "qk_loaded": Counted("stacks_loaded", 512),
            "rows_set": Counted("constant_rows_set", 3), "vproj": Counted("v_product", T),
            "vtaken": Counted("v_copied", T), "s1": Counted("scores_first_pass", B * H),
            "mx": Counted("maxima", B * H), "mT": Counted("maxima_transposed", 1),
            "mp": Counted("maxima_parts", 1), "mrow": Counted("maxima_rows_stored", 48),
            "s2": Counted("scores_second_pass", 2 * NG), "exp": Counted("weights", 2 * NG),
            "pv": Counted("weighted_values", 2 * NG), "oc": Counted("weighted_values_copied", NG),
            "oT": Counted("weighted_values_transposed", NG), "on": Counted("group_normalised", NG),
        }

        class SelfAttention:

            def __init__(self, turn, scope):
                i = f"self{turn}_"
                self.turn = turn
                self.hi = sb(i + "hi", [P, KT, NTOK], F16, scope)
                self.lo = sb(i + "lo", [P, KT, NTOK], F16, scope)
                self.k = sb(i + "k", [P, B * H, S], F16, scope)
                self.q = sb(i + "q", [P, B * H, S], F16, scope)
                self.v = sb(i + "v", [P, T, H, HV], F32, scope)

            def wait(self, eng, what, n):
                eng.wait_ge(signals[what].s, self.turn * signals[what].each + n)

        with ExitStack() as sc:
            sa5 = SelfAttention(0, sc)
            cosT = sb("cosT", [P, S], F32, sc)
            sinT = sb("sinT", [P, S], F32, sc)
            rot_a = [sb(f"rot_a{i}", [P, 512], F32, sc) for i in range(2)]
            rot_b = [sb(f"rot_b{i}", [P, 512], F32, sc) for i in range(2)]
        with ExitStack() as sc:
            hid5 = sb("hid5", [P, HM, NTOK], F32, sc)
            r_w1 = sb("r_w1", [P, KT, HID], F32, sc)
            r_w2 = sb("r_w2", [P, HM, D], F32, sc)
        norm4a, norm4b, norm5 = Norm(), Norm(), Norm()
        turn4 = Turn(tok, [(xT, "L1_attn_g1", "L1_attn_beta1")])
        turn4o = Turn(tok, [(xT, None, None)])
        gemm4 = Gemm("out4", xT, r_w[:, 5])
        turn5 = Turn(tok, [(xT, "L1_attn_g2", "L1_attn_beta2")])
        s_rope = sem("rotary_tables_loaded")
        s_tok4 = sem("self5_context_tiles")
        s_h5 = sem("mlp_hidden_product")
        s_h5e = sem("mlp_hidden")
        s_m2 = sem("mlp_out_product")

        with ExitStack() as sc:
            sa6 = SelfAttention(1, sc)
            b2_l = sb("b2_l", [ER, D], F32, sc)
            wg_l = sb("wg_l", [P, KT, ER], F32, sc)
        with ExitStack() as sc:
            l_we = sb("l_we", [P, ER // 2, KT, 2 * D], F32, sc)
        attention_scope.close()
        norm6, norm6a, norm6m = Norm(), Norm(), Norm()
        turn6 = Turn(u, [(xT, None, None)])
        turn6o = Turn(tok, [(xT, None, None)])
        gemm6 = Gemm("out6", xT, l_w[:, 3])
        turn7 = Turn(u, [(xT, None, None)])
        s_w6 = sem("last_weights_loaded")
        s_tok6 = sem("self6_context_tiles")
        s_y6 = sem("last_residual_tiles")
        s_log6 = sem("router6_logits")
        s_logs6 = sem("router6_logits_shifted")
        s_loge6 = sem("router6_exp")
        s_gate6 = sem("gates6_ready")
        s_gT6 = sem("gates6_transposed")
        s_gTe6 = sem("gates6_copied")
        s_b26 = sem("bexp_product")
        s_b2e6 = sem("bexp_taken")
        s_we = sem("expert6_product")
        s_wee = sem("expert6_accumulated")

        block = top.enter_context(nc.Block())

        N_START = 5
        ctx_blocks = [(b, c) for b in range(B) for c in range(NCB)]
        NPB = S2 // 512
        proj_blocks = [(b, c) for b in range(B) for c in range(NPB)]
        S1N = GH * 2 * (S2 // 512)
        COPY_STEP = 2
        NORM_STEP = 4
        MAX_STEP = 27
        PER_STEP = S1N // CH
        AHEAD = PER_STEP * (CH - 1 - MAX_STEP)

        def first_pass_at(g, par, turn, c):
            if isinstance(g, int) and (g == NG - 1 or (g == NG - 2 and c > MAX_STEP)):
                return []
            if c <= MAX_STEP:
                return [(g + 1, 1 - par, turn + par, AHEAD + PER_STEP * c + i) for i in range(PER_STEP)]
            return [(g + 2, par, turn + 1, PER_STEP * (c - 1 - MAX_STEP) + i) for i in range(PER_STEP)]

        def product_of(i):
            f, h, qt, kb = i // 32, i // 8 % 4, i // 4 % 2, i % 4
            return h, qt, 4 * f + kb

        def each_group(eng, body):
            body(0, 0, 1, True, False)
            body(1, 1, 1, False, False)
            with eng.Fori(0, (NG - 4) // 2) as i:
                for par in range(2):
                    body(2 * i + (2 + par), par, i + 2, False, False)
            body(NG - 2, 0, NG // 2, False, False)
            body(NG - 1, 1, NG // 2, False, True)

        def context_stored(eng):
            for i in range(3):
                eng.wait_ge(s_kst[i], 64 * len(range(i, 2 * len(proj_blocks), 3)))
            for i in range(2):
                eng.wait_ge(s_vst[i], 64 * 8)
            eng.wait_ge(s_mst, 16 * (H // GH))

        @block.sync
        def _(sp):
            def store():
                sp.wait_ge(s_x, min(stop, 6) * T)
                sp.dma_start(out.rearrange("b (h p) d -> p (b h) d", p=P), x[:, :, :]).then_inc(s_store, 16)
                sp.wait_ge(s_store, 16)

            sp.dma_start(x[:, :, :], a["x"].rearrange("b (h p) d -> p (b h) d", p=P)).then_inc(s_start, 16)
            sp.dma_start(ident[:, :], a["ident"]).then_inc(s_start, 16)
            sp.dma_start(cols[:, :], a["cols"]).then_inc(s_start, 16)
            sp.dma_start(rows[:, :], a["rows"].to_broadcast([P, NROWS])).then_inc(s_start, 16)
            sp.dma_start(row0[:, :], a["row0"].to_broadcast([P, W0])).then_inc(s_start, 16)
            sp.dma_start(w0q[:, :, :], a["w0qT"].rearrange("(k p) n -> p k n", p=P)).then_inc(s_wa, 16)
            sp.dma_start(w0o[:, :, :], a["w0oT"].rearrange("(k p) n -> p k n", p=P)).then_inc(s_wa, 16)
            sp.wait_ge(s_ones, NBUF)
            for n, (b, c) in enumerate(ctx_blocks):
                if n >= NBUF:
                    sp.wait_ge(s_gram_blk, n - NBUF + 1)
                src = a["ctx"][b].rearrange("(n p c) d -> n p c d", p=P, c=CB)[c]
                sp.dma_start(ctx_sb[n % NBUF][:, :, 0:D], src).then_inc(s_ctx[n % NBUF], 16)
                if n == 2:
                    for dst, name in ((b_in, "w1inT"), (b_q, "w1q"), (b_o, "w1oT"), (b_p, "w1pT"), (b_pos, "posT"),
                                      (b_mask, "head_mask")):
                        sp.dma_start(dst, a[name].rearrange("(k p) n -> p k n", p=P)).then_inc(s_wb, 16)
                    sp.dma_start(wkv[:, :, :], a["wkv"].rearrange("(k p) n -> p k n", p=P)).then_inc(s_wkv, 16)
                    sp.dma_start(wqo_x[:, 0], a["wq_x"].rearrange("(k p) n -> p k n", p=P)).then_inc(s_wkv, 16)
                    sp.dma_start(wqo_x[:, 1], a["wo_x"].rearrange("(k p) n -> p k n", p=P)).then_inc(s_wkv, 16)
            if stop <= 1:
                store()
                return
            sp.wait_ge(s_x, T)
            sp.dma_start(row_in[:, :], a["row_in"].to_broadcast([P, 3 * D])).then_inc(s_rin, 16)
            sp.dma_start(m_u32[:, :], a["mask"]).then_inc(s_m8, 16)
            def store_projection(n):
                b, c = proj_blocks[n]
                for m in range(KT):
                    job = 2 * n + m
                    sp.wait_ge(s_klo, job + 1)
                    for part, src in enumerate((k_hi[job % 3], k_lo[job % 3])):
                        for g in range(2):
                            sp.dma_start(k_scr[b, 2 * m + g, part, :, c * 512:(c + 1) * 512],
                                         src[64 * g:64 * g + 64, :]).then_inc(s_kst[job % 3], 16)
                if n % 2 == 1:
                    vb = n // 2
                    sp.wait_ge(s_ve, 4 * (n + 1))
                    cb = (vb % 4) * VC
                    for g in range(H // GH):
                        sp.dma_start(v_scr[b * 4 + g, :, cb:cb + VC, :], v_st[vb % 2][:, g]).then_inc(s_vst[vb % 2], 16)

            for n, (b, c) in enumerate(proj_blocks):
                if n >= 2:
                    store_projection(n - 2)
                if n >= 3:
                    sp.wait_ge(s_vp, 4 * (n - 2))
                sp.dma_start(cT[n % 3][:, :, :], a["ctxT"][b].rearrange("(k p) n -> p k n", p=P)[:, :, c * 512:(c + 1) * 512])\
                    .then_inc(s_cT[n % 3], 16)
            store_projection(len(proj_blocks) - 2)
            store_projection(len(proj_blocks) - 1)
            if stop <= 2:
                store()
                return
            sp.wait_ge(s_x, 2 * T)
            sp.dma_start(r_w, a["r_w"].rearrange("w (k p) n -> p w k n", p=P)).then_inc(s_wb, 16)
            sp.wait_ge(s_x, 2 * T)
            context_stored(sp)
            sp.dma_start(cent[:, :, :], a["cent"].rearrange("(k p) n -> p k n", p=P)).then_inc(s_w3, 16)
            sp.dma_start(b2_all[:, :], a["b2_all"]).then_inc(s_w3, 16)

            def expert(e, par):
                one = bass.ds(e, 1)
                sp.dma_start(w_f[:, 0:WPIECES // 2, :].rearrange("p (k a) n -> p k (a n)", k=KT),
                             a["w1_all"][one].rearrange("o (k p) n -> (o p) k n", p=P)).then_inc(s_wexp, 16)
                sp.dma_start(w_f[:, WPIECES // 2:WPIECES, :].rearrange("p b (a n) -> p (b a) n", n=D),
                             a["w2_all"][one].rearrange("o (k p) n -> (o p) k n", p=P)).then_inc(s_wexp, 16)
                sp.dma_start(b_1[par][:, :], a["b1_all"][one].rearrange("o p n -> (o p) n")).then_inc(s_wexp, 16)

            expert(ER, 0)
            sp.wait_ge(s_wlo, WPIECES)
            expert(ER + 1, 1)
            with sp.Fori(0, ER // 2) as i:
                for par in range(2):
                    sp.wait_ge(s_wlo, (2 * i + par) * WPIECES + 2 * WPIECES)
                    expert(2 * i + par, par)
            if stop <= 3:
                store()
                return
            for k in range(KT):
                sp.wait_ge(s_qxl, 2 * (k + 1))
                for part, src in enumerate((q_hi, q_lo)):
                    for g in range(2):
                        sp.dma_start(q_scr[:, 2 * k + g, part].rearrange("b f q -> f b q"),
                                     src[64 * g:64 * g + 64, k, :].rearrange("f (b q) -> f b q", b=B)).then_inc(s_qst, 16)
            sp.wait_ge(s_qst, 16 * 8)
            sp.wait_ge(s_init4, 6)

            k_g = k_scr.rearrange("b g s f n -> (b g) s f n")
            q_g = q_scr.rearrange("b g s f n -> (b g) s f n")

            def q_parts(dst, g, s_):
                one = bass.ds(g, 1)
                for r, part in enumerate((0, 1, 0, 1)):
                    sp.dma_start(dst[16 * r:16 * r + 16, :, :],
                                 q_g[one, part].rearrange("o (h d) n -> (o d) h n", d=HD)).then_inc(s_, 16)

            def load_keys(g, par, f):
                one = bass.ds(g, 1)
                kc = slice(f * S2 // 2, (f + 1) * S2 // 2)
                for h in range(GH):
                    for part in range(2):
                        src = k_g[one, part, h * HD:(h + 1) * HD, kc].to_broadcast([2, HD, S2 // 2])
                        sp.dma_start(kst[par][32 * part:32 * part + 32, h, kc], src).then_inc(s_kh[par][f], 16)
                src = mask_scr[one, kc].rearrange("g (o n) -> g o n", o=1).to_broadcast([1, GH, S2 // 2])
                sp.dma_start(kst[par][R_MASK:R_MASK + 1, :, kc], src).then_inc(s_kh[par][f], 16)

            def load_values(g, par):
                sp.dma_start(vst[par][:, :, :], v_scr[bass.ds(g, 1)].rearrange("o p c n -> (o p) c n")).then_inc(s_vl[par], 16)

            def max_rows(par):
                for i in range(3):
                    sp.dma_start(qb[par][R_MAX + i:R_MAX + i + 1, :, :], m_prt[0:2 * GH, i, :]).then_inc(s_mrow, 16)

            q_parts(qa[0], 0, s_qa[0])
            load_keys(0, 0, 0)
            load_keys(0, 0, 1)
            q_parts(qb[0], 0, s_qb[0])
            load_values(0, 0)
            q_parts(qa[1], 1, s_qa[1])
            load_keys(1, 1, 0)
            sp.wait_ge(s_mp, 1)
            max_rows(0)

            def next_group(g, par, turn, first, last):
                if last:
                    return
                if not first:
                    sp.wait_ge(s_s2, g * CH)
                load_keys(g + 1, 1 - par, 1)
                q_parts(qb[1 - par], g + 1, s_qb[1 - par])
                if not first:
                    sp.wait_ge(s_pv, g * CH)
                load_values(g + 1, 1 - par)
                if not (isinstance(g, int) and g == NG - 2):
                    sp.wait_ge(s_s1, g * S1N + S1N)
                    q_parts(qa[par], g + 2, s_qa[par])
                    sp.wait_ge(s_s2, g * CH + CH // 2)
                    load_keys(g + 2, par, 0)
                sp.wait_ge(s_mp, g + 2)
                max_rows(1 - par)

            each_group(sp, next_group)

            def self_io(sa, scr, tensors):
                for n, what in enumerate(tensors):
                    sa.wait(sp, "flo", 4 * (n + 1))
                    for part, src in enumerate((sa.hi, sa.lo)):
                        sp.dma_start(scr[n, part].rearrange("(k p) q -> p k q", p=P), src[:, :, :]).then_inc(signals["fst"].s, 16)
                    sa.wait(sp, "fst", 32 * (n + 1))
                    if n == 0:
                        sa.wait(sp, "rows_set", 3)
                    order, dst = ((0, 1, 0, 1), sa.q) if what == "q" else ((0, 0, 1, 1), sa.k)
                    for r, part in enumerate(order):
                        for b in range(B):
                            sp.dma_start(dst[16 * r:16 * r + 16, b * H:(b + 1) * H, :],
                                         scr[n, part].rearrange("(h d) (b q) -> b d h q", d=HD, b=B)[b])\
                                .then_inc(signals["qk_loaded"].s, 16)
                sa.wait(sp, "mp", 1)
                for i in range(3):
                    sp.dma_start(sa.q[R_MAX + i:R_MAX + i + 1, :, :], sa_parts[:, i, :]).then_inc(signals["mrow"].s, 16)

            sa_parts = m_prt
            if stop <= 4:
                store()
                return
            sp.wait_ge(s_x, 4 * T)
            sp.dma_start(cosT[:, :], a["cosT"]).then_inc(s_rope, 16)
            sp.dma_start(sinT[:, :], a["sinT"]).then_inc(s_rope, 16)
            self_io(sa5, self_scr[0], "qk")
            sa5.wait(sp, "on", NG)
            sp.dma_start(r_w1[:, :, :], a["r_w1"].rearrange("(k p) n -> p k n", p=P)).then_inc(s_wa, 16)
            sp.dma_start(r_w2[:, :, :], a["r_w2"].rearrange("(k p) n -> p k n", p=P)).then_inc(s_wa, 16)
            if stop <= 5:
                store()
                return
            sp.wait_ge(s_x, 5 * T)
            sp.dma_start(l_w, a["l_w"].rearrange("w (k p) n -> p w k n", p=P)).then_inc(s_wb, 16)
            sp.dma_start(b2_l[:, :], a["bexp"]).then_inc(s_w6, 16)
            sp.dma_start(wg_l[:, :, :], a["wg"].rearrange("(k p) n -> p k n", p=P)).then_inc(s_w6, 16)
            self_io(sa6, self_scr[1], "qk")
            sa6.wait(sp, "on", NG)
            sp.dma_start(l_we[:, :, :, :], a["l_we"].rearrange("e (k p) n -> p e k n", p=P)).then_inc(s_wa, 16)
            store()

        @block.tensor
        def _(pe):
            def tiles_ready(nm):
                return lambda half: nm.wait(pe, 4 * (half + 1))

            pe.wait_ge(s_start, 16 * N_START)
            pe_turn(pe, turn0, tiles_ready(norm0))
            pe.wait_ge(s_wa, 32)
            job = 0
            for half in range(2):
                turned(pe, turn0, half)
                for m in range(W0 // P):
                    if job >= 2:
                        pe.wait_ge(s_q0e, job - 1)
                    for k in range(KT):
                        last = pe.matmul(bank[2 + job % 2], w0q[:, k, m * P:(m + 1) * P],
                                         xT[:, k, half * 512:(half + 1) * 512], start=(k == 0), stop=(k == KT - 1))
                    last.then_inc(s_q0, 1)
                    job += 1

            def gram_of(b):
                if b >= 1:
                    pe.wait_ge(s_grame, 2 * b)
                for c in range(NCB):
                    n = b * NCB + c
                    pe.wait_ge(s_ctx[n % NBUF], 16 * (n // NBUF + 1))
                    for j in range(CB):
                        for m in range(KT):
                            last = pe.matmul(bank[m][:, 0:D + 1], ctx_sb[n % NBUF][:, j, m * P:(m + 1) * P],
                                             ctx_sb[n % NBUF][:, j, :], start=(c == 0 and j == 0),
                                             stop=(c == NCB - 1 and j == CB - 1))
                    last.then_inc(s_gram_blk, 1)

            def kv_of(b):
                pe.wait_ge(s_grame, 2 * (b + 1))
                if b == 0:
                    pe.wait_ge(s_q0e, W0 // P * 2)
                else:
                    pe.wait_ge(s_x, 2 * b)
                    pe.wait_ge(s_lte, 4 * b)
                n = 6 * b
                for m in range(KT + 1):
                    cs, rws = (slice(m * P, (m + 1) * P), slice(0, P)) if m < KT else (slice(D, D + 1), slice(0, 1))
                    for h in range(2):
                        if n >= 6 * b + 2:
                            pe.wait_ge(s_gwe, n - 1)
                        for k in range(KT):
                            last = pe.matmul(bank[2 + n % 2][rws, :], gram[:, k, cs],
                                             w0q[:, k, h * 512:(h + 1) * 512], start=(k == 0), stop=(k == KT - 1))
                        last.then_inc(s_gw, 1)
                        n += 1
                pe.wait_ge(s_gwe, 6 * (b + 1))
                for j in range(2):
                    for i in range(4):
                        h = 4 * j + i
                        hc = slice(h * P, (h + 1) * P)
                        o = bank[2 + j][:, i * P:(i + 1) * P]
                        for k in range(KT):
                            pe.matmul(o, w0q[:, k, hc], gw[:, k, hc], start=(k == 0), stop=False)
                        last = pe.matmul(o, row0[0:1, h * P:(h + 1) * P], gw_row[:, hc],
                                         start=False, stop=True)
                    last.then_inc(s_kv0, 1)

            def logits_of(b):
                pe.wait_ge(s_kv0e, 4 * (b + 1))
                for hf in range(2):
                    t = 2 * b + hf
                    if b >= 1:
                        pe.wait_ge(s_lgs, t - 1)
                    for m in range(W0 // P):
                        last = pe.matmul(pair[hf][:, m * P:(m + 1) * P], q0T[:, m, t * P:(t + 1) * P], kv0[:, m, :],
                                         start=(m % 4 == 0), stop=(m % 4 == 3), skip_group_check=True)
                    last.then_inc(s_lg, 1)

            def out_of(b):
                for hf in range(2):
                    t = 2 * b + hf
                    pe.wait_ge(s_lgn, t + 1)
                    for j in range(2):
                        n = 2 * t + j
                        if n >= 1:
                            pe.wait_ge(s_lte, n)
                        for i in range(4):
                            m = 4 * j + i
                            last = pe.transpose(bank[3][:, i * P:(i + 1) * P],
                                                lin[hf][:, 2 * m:2 * m + 2, :].rearrange("p h d -> p (h d)"), ident[:, :])
                        last.then_inc(s_lt, 1)
                    pe.wait_ge(s_lte, 2 * t + 2)
                    if t >= 1:
                        pe.wait_ge(s_x, t)
                    for m in range(W0 // P):
                        last = pe.matmul(bank[2][:, 0:D], linT[:, m, :], w0o[:, m, :], start=(m == 0),
                                         stop=(m == W0 // P - 1))
                    last.then_inc(s_lo, 1)

            turned(pe, turn0)
            for b in range(B + 1):
                if b < B:
                    gram_of(b)
                if b > 0:
                    out_of(b - 1)
                if b < B:
                    kv_of(b)
                    logits_of(b)
            if stop <= 1:
                return

            pe.wait_ge(s_wb, 16 * 6)
            for m in range(KT):
                for k in range(KT):
                    last = pe.matmul(bank[4 + m][:, 0:R0], b_p[:, k, m * P:(m + 1) * P], b_pos[:, k, :],
                                     start=(k == 0), stop=(k == KT - 1))
            last.then_inc(s_posT, 1)
            pe.wait_ge(s_posb, 1)
            for m in range(KT):
                for k in range(KT):
                    last = pe.matmul(bank[4 + m][:, 0:R0 * H], b_q[:, k, m * P:(m + 1) * P],
                                     pos_blk[:, k].rearrange("p j h -> p (j h)"), start=(k == 0), stop=(k == KT - 1))
            for k in range(KT):
                last = pe.matmul(bank[6][:, 0:R0 * H], bqrr_rep[:, k, :], pos_blk[:, k].rearrange("p j h -> p (j h)"),
                                 start=(k == 0), stop=(k == KT - 1))
            last.then_inc(s_relw, 1)
            pe_turn(pe, turn1, tiles_ready(norm1))
            pe.wait_ge(s_relwe, 3)
            for t in range(T):
                if t % 4 == 0:
                    turned(pe, turn1, t // 4)
                if t >= 1:
                    pe.wait_ge(s_qkve, 3 * t)
                for k in range(KT):
                    lhs = xT[:, k, t * P:(t + 1) * P]
                    pe.matmul(bank[2][:, :], lhs, b_in[:, k, 0:512], start=(k == 0), stop=(k == KT - 1))
                    pe.matmul(bank[3][:, 0:256], lhs, b_in[:, k, 512:768], start=(k == 0), stop=(k == KT - 1))
                    last = pe.matmul(bank[7][:, 0:R0 * H], lhs, rel_w[:, k, :], start=(k == 0), stop=(k == KT - 1))
                last.then_inc(s_qkv, 1)

            pe.wait_ge(s_wkv, 48)
            for n, (b, c) in enumerate(proj_blocks):
                pe.wait_ge(s_cT[n % 3], 16 * (n // 3 + 1))
                for m in range(KT):
                    job = 2 * n + m
                    if job >= 2:
                        pe.wait_ge(s_kf, 2 * (job - 1))
                    for k in range(KT):
                        last = pe.matmul(bank[4 + job % 2], wkv[:, k, m * P:(m + 1) * P], cT[n % 3][:, k, :],
                                         start=(k == 0), stop=(k == KT - 1))
                    last.then_inc(s_kp, 1)
                for j in range(4):
                    job = 4 * n + j
                    if job == 1:
                        pe.wait_ge(s_qkve, 3 * T)
                    if job >= 2:
                        pe.wait_ge(s_ve, job - 1)
                    for k in range(KT):
                        last = pe.matmul(bank[6 + job % 2][:, 0:D], cT[n % 3][:, k, j * P:(j + 1) * P],
                                         wkv[:, k, D:2 * D], start=(k == 0), stop=(k == KT - 1))
                    last.then_inc(s_vp, 1)

            pe_turn(pe, turn1o, lambda half: pe.wait_ge(s_tok1, T))
            pe_gemm(pe, gemm1, turn1o)
            if stop <= 2:
                return

            pe_turn(pe, turn2, lambda half: pe.wait_ge(s_un, 4 * (half + 1)))
            turned(pe, turn2)
            pe.wait_ge(s_w3, 32)
            for t in range(T):
                for k in range(KT):
                    last = pe.matmul(bank[4][:, t * ER:(t + 1) * ER], xTr[:, k, t * P:(t + 1) * P], cent[:, k, :],
                                     start=(k == 0), stop=(k == KT - 1), skip_group_check=True)
            last.then_inc(s_log, 1)

            def turn_gates():
                pe.wait_ge(s_gate, 1)
                pe.wait_ge(s_gelu, 4 * HM)
                for j in range(2):
                    for i in range(4):
                        last = pe.transpose(bank[j][0:ER + ES, i * P:(i + 1) * P], gate_t[:, 4 * j + i, :], ident[:, :])
                    last.then_inc(s_gT, 1)

            def expert(n, par, src, first=False, between=None):
                w_hi, w_lo = w_part[0][par], w_part[1][par]
                pe.wait_ge(s_wlo, n * WPIECES + WPIECES)
                for job in range(2 * HM):
                    half, m = divmod(job, HM)
                    if not (first and job < 4):
                        pe.wait_ge(s_gelu, n * 2 * HM + job - 3)
                    hc = slice(half * 512, (half + 1) * 512)
                    for k in range(KT):
                        piece, at = k * (HID // 512) + m // 4, m % 4 * P
                        for w, x_ in ((w_hi, 0), (w_hi, 1), (w_lo, 0)):
                            last = pe.matmul(bank[job % 4], w[:, piece, at:at + P], src[x_][:, k, hc],
                                             start=(k == 0 and x_ == 0 and w is w_hi),
                                             stop=(k == KT - 1 and w is w_lo))
                    last.then_inc(s_w1, 1)
                if between:
                    between()
                for t in range(T):
                    if t % 4 == 0:
                        pe.wait_ge(s_hlo, n * 2 * HM + (t // 4 + 1) * HM)
                    if not (first and t < 4):
                        pe.wait_ge(s_acc, n * T + t - 3)
                    elif t == 0:
                        pe.wait_ge(s_logs, 1)
                    for m in range(HM):
                        wc = slice(m % 2 * D, (m % 2 + 1) * D)
                        for h_, w in ((0, w_hi), (0, w_lo), (1, w_hi)):
                            last = pe.matmul(bank[4 + t % 4][:, 0:D], hid_part[h_][:, m, t * P:(t + 1) * P],
                                             w[:, WPIECES // 2 + m // 2, wc], start=(m == 0 and h_ == 0 and w is w_hi),
                                             stop=(m == HM - 1 and h_ == 1))
                    last.then_inc(s_w2, 1)

            pe.wait_ge(s_xlo, 2 * KT)
            expert(0, 0, x_part[0], first=True)
            expert(1, 1, x_part[0], between=turn_gates)
            pe.wait_ge(s_gTe, 2)
            for t in range(T):
                if t >= 2:
                    pe.wait_ge(s_b2e, t - 1)
                pe.matmul(bank[2 + t % 2][:, 0:D], gateT[:, t * P:(t + 1) * P], b2_all[:, :], start=True, stop=True)\
                    .then_inc(s_b2, 1)
            pe.wait_ge(s_b2e, T)
            with pe.Fori(0, (ER - 2) // 2) as i:
                for par in range(2):
                    expert(2 * i + (2 + par), par, x_part[1])
            for par in range(2):
                expert(ER + par, par, x_part[1])
            if stop <= 3:
                return

            pe_turn(pe, turn3, tiles_ready(norm3))
            turned(pe, turn3)
            for m in range(KT):
                for half in range(2):
                    job = 2 * m + half
                    if job >= 2:
                        pe.wait_ge(s_qxl, job - 1)
                    for k in range(KT):
                        last = pe.matmul(bank[2 + job % 2], wqo_x[:, 0, k, m * P:(m + 1) * P],
                                         xT[:, k, half * 512:(half + 1) * 512], start=(k == 0), stop=(k == KT - 1))
                    last.then_inc(s_qx, 1)
            pe.wait_ge(s_qxl, 4)

            def first_pass(g, par, turn, i):
                h, qt, kb = product_of(i)
                if i == 0:
                    pe.wait_ge(s_qa[par], turn * 64)
                if i % (S1N // 2) == 0:
                    pe.wait_ge(s_kh[par][i // (S1N // 2)], turn * 16 * (2 * GH + 1))
                if not (isinstance(g, int) and g == 0 and i < 2):
                    pe.wait_ge(s_mx, g * S1N + (i - 1))
                pe.matmul(bank[i % 2], qa[par][:, h, qt * P:(qt + 1) * P],
                          kst[par][:, h, kb * 512:(kb + 1) * 512], start=True, stop=True).then_inc(s_s1, 1)

            def turn_maxima(g, first):
                pe.wait_ge(s_mxa, g + 1)
                if not first:
                    pe.wait_ge(s_on, g - 1)
                pe.transpose(bank[3][0:2 * GH, 0:P], mx[:, 0:2 * GH], ident[:, :]).then_inc(s_mT, 1)

            def weigh(g, par, c, turn, first):
                pe.wait_ge(s_exp, g * CH + (c + 1))
                if c == 0:
                    pe.wait_ge(s_vl[par], turn * 16)
                    if not first:
                        pe.wait_ge(s_oc, g)
                slot = (par * CH + c) % NP_
                for h in range(GH):
                    last = pe.matmul(bank[2][32 * h:32 * h + HV, 0:S], vst[par][:, c, h * HV:(h + 1) * HV],
                                     pexp[slot][:, h, :], start=(c == 0), stop=(c == CH - 1))
                last.then_inc(s_pv, 1)

            def turn_out(g, par, first):
                pe.wait_ge(s_oc, g + 1)
                if not first:
                    pe.wait_ge(s_on, g)
                for qt in range(2):
                    last = pe.transpose(bank[3][:, 256 + qt * P:256 + (qt + 1) * P], oT[par][:, qt * P:(qt + 1) * P],
                                        ident[:, :])
                last.then_inc(s_oT, 1)

            def weigh_group(g, par, turn, first, last_group):
                pe.wait_ge(s_mrow, g * 48 + 48)
                pe.wait_ge(s_qb[par], turn * 64)
                for c in range(CH):
                    beside = first_pass_at(g, par, turn, c)
                    if not (first and c < 2):
                        pe.wait_ge(s_exp, g * CH + (c - 1))
                    for h in range(GH):
                        last = pe.matmul(pair[c % 2][:, h * S:(h + 1) * S], kst[par][:, h, c * P:(c + 1) * P],
                                         qb[par][:, h, :], start=True, stop=True)
                        if h == GH - 1:
                            last.then_inc(s_s2, 1)
                        if h == 1 and not last_group and c == MAX_STEP + 1:
                            turn_maxima(g + 1, first)
                        if h % 2 and beside:
                            first_pass(*beside.pop(0))
                    if c >= 2:
                        weigh(g, par, c - 2, turn, first)
                    elif not first:
                        weigh(g - 1, 1 - par, CH - 2 + c, None, False)
                    if c == NORM_STEP - 1 and not first:
                        turn_out(g - 1, 1 - par, isinstance(g, int) and g == 1)
                if last_group:
                    weigh(g, par, CH - 2, turn, first)
                    weigh(g, par, CH - 1, turn, first)

            for i in range(S1N):
                first_pass(0, 0, 1, i)
            turn_maxima(0, True)
            for i in range(AHEAD):
                first_pass(1, 1, 1, i)
            each_group(pe, weigh_group)
            turn_out(NG - 1, 1, False)
            pe_turn(pe, turn3o, lambda half: pe.wait_ge(s_tok3, B))
            pe_gemm(pe, gemm3, turn3o)
            if stop <= 4:
                return

            def self_proj(sa, ws, nprod):
                for n in range(2):
                    for m in range(KT):
                        for half in range(2):
                            job = 4 * n + 2 * m + half
                            if job >= 1:
                                sa.wait(pe, "flo", job)
                            for w in range(nprod):
                                for k in range(KT):
                                    last = pe.matmul(bank[4 + w], ws[n * nprod + w][:, k, m * P:(m + 1) * P],
                                                     xT[:, k, half * 512:(half + 1) * 512], start=(k == 0),
                                                     stop=(k == KT - 1))
                            last.then_inc(signals["fproj"].s, 1)

            def self_values(sa, w):
                for t in range(T):
                    if t >= 2:
                        sa.wait(pe, "vtaken", t - 1)
                    for k in range(KT):
                        last = pe.matmul(bank[2 + t % 2][:, 0:D], xT[:, k, t * P:(t + 1) * P], w[:, k, :],
                                         start=(k == 0), stop=(k == KT - 1))
                    last.then_inc(signals["vproj"].s, 1)

            def self_attention(sa):
                sa.wait(pe, "qk_loaded", 16 * 32)
                sa.wait(pe, "rows_set", 3)
                for n in range(B * H):
                    hp, qt = divmod(n, 2)
                    if n >= 4:
                        sa.wait(pe, "mx", n - 3)
                    for i in range(2):
                        h = 2 * hp + i
                        last = pe.matmul(bank[4 + n % 4][:, i * S:(i + 1) * S], sa.q[:, h, qt * P:(qt + 1) * P],
                                         sa.k[:, h, :], start=True, stop=True)
                    last.then_inc(signals["s1"].s, 1)
                sa.wait(pe, "mx", B * H)
                pe.transpose(bank[3][:, 0:P], mx[:, :], ident[:, :]).then_inc(signals["mT"].s, 1)
                sa.wait(pe, "mrow", 48)

                def weigh(n):
                    g, c = divmod(n, 2)
                    sa.wait(pe, "exp", n + 1)
                    if c == 0 and g >= 1:
                        sa.wait(pe, "oc", g)
                    if n == 0:
                        sa.wait(pe, "vtaken", T)
                    b, g4 = divmod(g, H // GH)
                    for h in range(GH):
                        last = pe.matmul(bank[2][32 * h:32 * h + HV, 0:S], sa.v[:, 2 * b + c, g4 * GH + h, :],
                                         pexp[n % NP_][:, h, :], start=(c == 0), stop=(c == 1))
                    last.then_inc(signals["pv"].s, 1)

                def turn_out(g):
                    sa.wait(pe, "oc", g + 1)
                    if g >= 1:
                        sa.wait(pe, "on", g)
                    for qt in range(2):
                        last = pe.transpose(bank[3][:, 256 + qt * P:256 + (qt + 1) * P],
                                            oT[g % 2][:, qt * P:(qt + 1) * P], ident[:, :])
                    last.then_inc(signals["oT"].s, 1)

                for n in range(2 * NG):
                    g, c = divmod(n, 2)
                    if n >= 2:
                        sa.wait(pe, "exp", n - 1)
                    for h in range(GH):
                        last = pe.matmul(pair[n % 2][:, h * S:(h + 1) * S], sa.k[:, g * GH + h, c * P:(c + 1) * P],
                                         sa.q[:, g * GH + h, :], start=True, stop=True)
                    last.then_inc(signals["s2"].s, 1)
                    if n >= 1:
                        weigh(n - 1)
                    if c == 1 and g >= 1:
                        turn_out(g - 1)
                weigh(2 * NG - 1)
                turn_out(NG - 1)

            pe_turn(pe, turn4, tiles_ready(norm4b))
            turned(pe, turn4)
            pe.wait_ge(s_wb, 16 * 7)
            self_proj(sa5, [r_w[:, i] for i in range(4)], 2)
            self_values(sa5, r_w[:, 4])
            self_attention(sa5)
            pe_turn(pe, turn4o, lambda half: pe.wait_ge(s_tok4, B))
            pe_gemm(pe, gemm4, turn4o)
            pe_turn(pe, turn5, tiles_ready(norm5))
            pe.wait_ge(s_wa, 16 * 4)
            job = 0
            for half in range(2):
                turned(pe, turn5, half)
                for m in range(HM):
                    if job >= 4:
                        pe.wait_ge(s_h5e, job - 3)
                    for k in range(KT):
                        last = pe.matmul(bank[4 + job % 4], r_w1[:, k, m * P:(m + 1) * P],
                                         xT[:, k, half * 512:(half + 1) * 512], start=(k == 0), stop=(k == KT - 1))
                    last.then_inc(s_h5, 1)
                    job += 1
            for t in range(T):
                pe.wait_ge(s_h5e, HM * (t // 4 + 1))
                if t >= 2:
                    pe.wait_ge(s_x, 4 * T + t - 1)
                for m in range(HM):
                    last = pe.matmul(bank[2 + t % 2][:, 0:D], hid5[:, m, t * P:(t + 1) * P], r_w2[:, m, :],
                                     start=(m == 0), stop=(m == HM - 1))
                last.then_inc(s_m2, 1)
            if stop <= 5:
                return

            pe_turn(pe, turn6, tiles_ready(norm6))
            turned(pe, turn6)
            pe.wait_ge(s_wb, 16 * 8)
            self_proj(sa6, [l_w[:, 0], l_w[:, 1]], 1)
            self_values(sa6, l_w[:, 2])
            self_attention(sa6)
            pe_turn(pe, turn6o, lambda half: pe.wait_ge(s_tok6, B))
            pe_gemm(pe, gemm6, turn6o)
            pe_turn(pe, turn7, lambda half: pe.wait_ge(s_y6, T))
            turned(pe, turn7)
            pe.wait_ge(s_w6, 32)
            for t in range(T):
                for k in range(KT):
                    last = pe.matmul(bank[2][:, t * ER:(t + 1) * ER], xT[:, k, t * P:(t + 1) * P], wg_l[:, k, :],
                                     start=(k == 0), stop=(k == KT - 1), skip_group_check=True)
            last.then_inc(s_log6, 1)
            pe.wait_ge(s_gate6, 1)
            for j in range(2):
                for i in range(4):
                    last = pe.transpose(bank[j][0:ER, i * P:(i + 1) * P], gate_t[:, 4 * j + i, 0:ER], ident[:, :])
                last.then_inc(s_gT6, 1)
            pe.wait_ge(s_gTe6, 2)
            for t in range(T):
                if t >= 2:
                    pe.wait_ge(s_b2e6, t - 1)
                pe.matmul(bank[2 + t % 2][:, 0:D], gateT[0:ER, t * P:(t + 1) * P], b2_l[:, :], start=True, stop=True)\
                    .then_inc(s_b26, 1)
            pe.wait_ge(s_wa, 16 * 5)
            n = 0
            for e in range(ER // 2):
                for t in range(T):
                    if n >= 4:
                        pe.wait_ge(s_wee, 2 * (n - 3))
                    for k in range(KT):
                        last = pe.matmul(bank[4 + n % 4], xT[:, k, t * P:(t + 1) * P],
                                         l_we[:, e, k, :], start=(k == 0), stop=(k == KT - 1))
                    last.then_inc(s_we, 1)
                    n += 1

        @block.scalar
        def _(act):
            act.wait_ge(s_start, 16 * N_START)
            act_dev(act, norm0)
            act_turn(act, turn0)
            for job in range(2 * W0 // P):
                half, m = divmod(job, W0 // P)
                act.wait_ge(s_q0, job + 1)
                act.activation(q0T[:, m, half * 512:(half + 1) * 512], bank[2 + job % 2], ACT.Identity,
                               bias=col("L0_xattn_Wq_b", m)).then_inc(s_q0e, 1)
            for b in range(B):
                for hf in range(2):
                    t = 2 * b + hf
                    act.wait_ge(s_lgs, t + 1)
                    act.activation(lin[hf][:, :, :], lin[hf][:, :, :], ACT.Exp).then_inc(s_lge, 1)
                for hf in range(2):
                    t = 2 * b + hf
                    for j in range(2):
                        n = 2 * t + j
                        act.wait_ge(s_lt, n + 1)
                        if j == 0 and t >= 1:
                            act.wait_ge(s_lo, t)
                        act.activation(linT[:, 4 * j:4 * j + 4, :].rearrange("p m q -> p (m q)"), bank[3], ACT.Copy)\
                            .then_inc(s_lte, 1)
            if stop <= 1:
                return
            act_dev(act, norm1)
            act_turn(act, turn1)
            act.wait_ge(s_vones, 2)
            for n, (b, c) in enumerate(proj_blocks):
                if n in (6, 12):
                    i = n // 6 - 1
                    act.wait_ge(s_at0, i + 1)
                    act.activation(sc0[:, :, :, :], sc0[:, :, :, :], ACT.Exp, scale=SCALE).then_inc(s_at0e, 1)
                for m in range(KT):
                    job = 2 * n + m
                    act.wait_ge(s_kp, job + 1)
                    if job >= 2:
                        act.wait_ge(s_klo, job - 1)
                    if job >= 3:
                        act.wait_ge(s_kst[job % 3], 64 * (job // 3))
                    act.activation(k_f[job % 2][:, :], bank[4 + job % 2], ACT.Identity, bias=col("bk_x", m))\
                        .then_inc(s_kf, 1)
                    act.activation(k_hi[job % 3][:, :], bank[4 + job % 2], ACT.Identity, bias=col("bk_x", m))\
                        .then_inc(s_kf, 1)
                for j in range(4):
                    job = 4 * n + j
                    vb, cc = divmod(job, VC)
                    act.wait_ge(s_vp, job + 1)
                    if cc == 0 and vb >= 2:
                        act.wait_ge(s_vst[vb % 2], 64 * (vb // 2))
                    dst = v_st[vb % 2][:, :, cc, :].rearrange("p g (h d) -> p g h d", d=HV)[:, :, :, 0:HD]
                    act.activation(dst, bank[6 + job % 2][:, 0:D].rearrange("p (g h d) -> p g h d", h=GH, d=HD),
                                   ACT.Copy).then_inc(s_ve, 1)
            act_turn(act, turn1o)
            if stop <= 2:
                return
            act_dev(act, norm2)
            context_stored(act)
            for t in range(T):
                norm2.wait(act, t + 1)
                if t:
                    act.wait_ge(s_sq, t)
                act.activation(junk3[:, :], u[:, t, :], ACT.Square, accum_out=var_eps[:, t:t + 1]).then_inc(s_sq, 1)
            act_dev(act, rms)
            act_turn(act, turn2)

            def weights_high(n, par):
                act.wait_ge(s_wexp, n * 48 + 48)
                if not (isinstance(n, int) and n < 2):
                    act.wait_ge(s_w2, (n - 1) * T)
                for i in range(WPIECES):
                    act.activation(w_part[0][par][:, i, :], w_f[:, i, :], ACT.Copy, scale=W_SCALE).then_inc(s_whi, 1)

            def turn_gates():
                for j in range(2):
                    act.wait_ge(s_gT, j + 1)
                    act.activation(gateT[:, j * 512:(j + 1) * 512], bank[j][0:ER + ES, :], ACT.Copy).then_inc(s_gTe, 1)

            def expert(n, par, first=False, last=False, between=None):
                for job in range(2 * HM):
                    act.wait_ge(s_w1, n * 2 * HM + job + 1)
                    if not (first and job < 4):
                        act.wait_ge(s_hlo, n * 2 * HM + job - 3)
                    act.activation(hid_f[:, job % 4, :], bank[job % 4], ACT.Gelu, bias=b_1[par][:, job % HM:job % HM + 1],
                                   scale=1.0 / W_SCALE).then_inc(s_gelu, 1)
                if between:
                    between()
                if not last:
                    weights_high(n + 1, 1 - par)

            weights_high(0, 0)
            act.wait_ge(s_logs, 1)
            act.activation(logit[:, :, :], logit[:, :, :], ACT.Exp, scale=-1.0).then_inc(s_loge, 1)
            act.wait_ge(s_log, 1)
            expert(0, 0, first=True)
            expert(1, 1, between=turn_gates)
            with act.Fori(0, (ER - 2) // 2) as i:
                for par in range(2):
                    expert(2 * i + (2 + par), par)
            for par in range(2):
                expert(ER + par, par, last=par == 1)
            if stop <= 3:
                return
            act_dev(act, norm3)
            act_turn(act, turn3)
            for m in range(KT):
                for half in range(2):
                    job = 2 * m + half
                    act.wait_ge(s_qx, job + 1)
                    act.activation(q_hi[:, m, half * 512:(half + 1) * 512], bank[2 + job % 2], ACT.Identity,
                                   bias=col("L1_xattn_bq", m)).then_inc(s_qxh, 1)

            def copy_out(g, par):
                act.wait_ge(s_pv, g * CH + CH)
                act.activation(oT[par][:, :], bank[2][:, 0:S], ACT.Copy).then_inc(s_oc, 1)

            def exp_group(g, par, turn, first, last):
                for c in range(CH):
                    if c == COPY_STEP and not first:
                        copy_out(g - 1, 1 - par)
                    act.wait_ge(s_s2, g * CH + (c + 1))
                    if not (first and c < NP_):
                        act.wait_ge(s_pv, g * CH + (c - NP_ + 1))
                    slot = (par * CH + c) % NP_
                    act.activation(pexp[slot][:, :, :].rearrange("p h q -> p (h q)"), pair[c % 2][:, :], ACT.Exp,
                                   scale=SCALE).then_inc(s_exp, 1)

            each_group(act, exp_group)
            copy_out(NG - 1, 1)
            act_turn(act, turn3o)
            if stop <= 4:
                return

            def self_exp(sa):
                for n in range(2 * NG):
                    sa.wait(act, "s2", n + 1)
                    if n >= NP_:
                        sa.wait(act, "pv", n - NP_ + 1)
                    act.activation(pexp[n % NP_][:, :, :].rearrange("p h q -> p (h q)"), pair[n % 2][:, :], ACT.Exp,
                                   scale=SCALE).then_inc(signals["exp"].s, 1)

            act_dev(act, norm4a)
            act_dev(act, norm4b)
            act_turn(act, turn4)
            self_exp(sa5)
            act_turn(act, turn4o)
            act_dev(act, norm5)
            act_turn(act, turn5)
            for job in range(2 * HM):
                half, m = divmod(job, HM)
                act.wait_ge(s_h5, job + 1)
                act.activation(hid5[:, m, half * 512:(half + 1) * 512], bank[4 + job % 4], ACT.Relu,
                               bias=col("L1_attn_b1", m)).then_inc(s_h5e, 1)
            if stop <= 5:
                return
            act_dev(act, norm6)
            act_turn(act, turn6)
            for job in range(8):
                n, m, half = job // 4, (job // 2) % 2, job % 2
                sa6.wait(act, "fproj", job + 1)
                if job == 4:
                    sa6.wait(act, "fst", 32)
                act.activation(sa6.hi[:, m, half * 512:(half + 1) * 512], bank[4], ACT.Identity,
                               bias=col(("L1_ffn_bq", "L1_ffn_bk")[n], m)).then_inc(signals["fhi"].s, 1)
            self_exp(sa6)
            act_turn(act, turn6o)
            act_dev(act, norm6a)
            act_turn(act, turn7)
            act.wait_ge(s_logs6, 1)
            act.activation(logit[:, :, :], logit[:, :, :], ACT.Exp).then_inc(s_loge6, 1)
            for j in range(2):
                act.wait_ge(s_gT6, j + 1)
                act.activation(gateT[0:ER, j * 512:(j + 1) * 512], bank[j][0:ER, :], ACT.Copy).then_inc(s_gTe6, 1)
            act_dev(act, norm6m)

        @block.vector
        def _(dve):
            st = Steps(dve, s_dve)
            for i in range(NBUF):
                dve.memset(ctx_sb[i][:, :, D:D + 1], 1.0).then_inc(s_ones, 1)
            st.link(dve.memset(kv0[:, :, :], 0.0))
            dve.wait_ge(s_start, 16 * N_START)
            dve_norm(dve, st, norm0, x, u)

            def bcast(ap, n):
                return ap.to_broadcast(list(ap.shape[:-1]) + [n])

            def per_tile_rows(name, n=T):
                at = ROW_AT[name][0]
                return rows[:, at:at + D].rearrange("p (o d) -> p o d", o=1).to_broadcast([P, n, D])

            st.link(dve.tensor_tensor(x[:, :, :], x[:, :, :], per_tile_rows("L0_xattn_out_b"), ALU.add))
            st.settle()
            for b in range(B):
                dve.wait_ge(s_gram_blk, NCB * (b + 1))
                if b >= 1:
                    dve.wait_ge(s_gw, 6 * b)
                for m in range(KT):
                    dve.tensor_copy(gram[:, m, :], bank[m][:, 0:D + 1]).then_inc(s_grame, 1)
                dve.wait_ge(s_grame, 2 * (b + 1))
                if b >= 1:
                    for hf in range(2):
                        t = 2 * (b - 1) + hf
                        dve.wait_ge(s_lo, t + 1)
                        dve.tensor_tensor(x[:, t, :], x[:, t, :], bank[2][:, 0:D], ALU.add).then_inc(s_x, 1)
                n = 6 * b
                if b >= 1:
                    dve.wait_ge(s_kv0, 2 * b)
                for m in range(KT + 1):
                    for h in range(2):
                        hc = slice(h * 512, (h + 1) * 512)
                        dve.wait_ge(s_gw, n + 1)
                        if m < KT:
                            ins = dve.scalar_tensor_tensor(out=gw[:, m, hc], in0=row0[:, h * 512:(h + 1) * 512],
                                                           scalar=gram[:, m, D:D + 1], in1=bank[2 + n % 2],
                                                           op0=ALU.mult, op1=ALU.add)
                        else:
                            ins = dve.scalar_tensor_tensor(out=gw_row[:, hc],
                                                           in0=row0[0:1, h * 512:(h + 1) * 512],
                                                           scalar=float(S2), in1=bank[2 + n % 2][0:1, :],
                                                           op0=ALU.mult, op1=ALU.add)
                        ins.then_inc(s_gwe, 1)
                        n += 1
                if b == 0:
                    st.settle()
                if b >= 1:
                    dve.wait_ge(s_lg, 2 * b)
                for j in range(2):
                    dve.wait_ge(s_kv0, 2 * b + j + 1)
                    for i in range(2):
                        r = slice(64 * i, 64 * i + 64)
                        src = bank[2 + j][r, :].rearrange("p (m c) -> p m c", c=P)[:, :, r]
                        dve.tensor_scalar(kv0[r, 4 * j:4 * j + 4, r], src, float(DH0) ** -0.5, None, ALU.mult)\
                            .then_inc(s_kv0e, 1)
                for hf in range(2):
                    t = 2 * b + hf
                    dve.wait_ge(s_lg, t + 1)
                    lg = pair[hf][:, :].rearrange("p (h d) -> p h d", d=DH0)
                    st.link(dve.tensor_reduce(lin_max[:, hf, :], lg, X_AXIS, ALU.max))
                    st.settle()
                    if b >= 1:
                        dve.wait_ge(s_lt, 2 * t - 2)
                    dve.tensor_tensor(lin[hf][:, :, :], lg, bcast(lin_max[:, hf, :].rearrange("p (h o) -> p h o", o=1), DH0),
                                      ALU.subtract).then_inc(s_lgs, 1)
                for hf in range(2):
                    t = 2 * b + hf
                    dve.wait_ge(s_lge, t + 1)
                    st.link(dve.tensor_reduce(lin_sum[:, hf, :], lin[hf][:, :, :], X_AXIS, ALU.add))
                    st.settle()
                    st.link(dve.reciprocal(lin_sum[:, hf, :], lin_sum[:, hf, :]))
                    st.settle()
                    dve.tensor_tensor(lin[hf][:, :, :], lin[hf][:, :, :],
                                      bcast(lin_sum[:, hf, :].rearrange("p (h o) -> p h o", o=1), DH0), ALU.mult)\
                        .then_inc(s_lgn, 1)
            for t in (T - 2, T - 1):
                dve.wait_ge(s_lo, t + 1)
                dve.tensor_tensor(x[:, t, :], x[:, t, :], bank[2][:, 0:D], ALU.add).then_inc(s_x, 1)

            if stop <= 1:
                return
            dve.wait_ge(s_x, T)

            dve_norm(dve, st, norm1, x, u)
            dve.wait_ge(s_posT, 1)
            for m in range(KT):
                st.link(dve.tensor_scalar(posT[:, m, :], bank[4 + m][:, 0:R0], col("L0_attn_pos_proj_bias", m), None, ALU.add))
                st.link(dve.tensor_tensor(bqrr[:, m:m + 1], col("bq0", m), col("L0_attn_r_r_bias", m), ALU.add))
            st.settle()
            for m in range(KT):
                st.link(dve.tensor_tensor(pos_blk[:, m], bcast(posT[:, m, :].rearrange("p (j o) -> p j o", o=1), H),
                                          b_mask[:, m, :].rearrange("p (o h) -> p o h", o=1).to_broadcast([P, R0, H]), ALU.mult))
                st.link(dve.tensor_copy(bqrr_rep[:, m, :], bcast(bqrr[:, m:m + 1], P)))
            dve.wait_ge(s_rin, 16)
            st.settle()
            dve.tensor_tensor(row_in[:, 0:D], row_in[:, 0:D], row("L0_attn_r_w_bias"), ALU.add).then_inc(s_posb, 1)
            dve.wait_ge(s_relw, 1)
            for m in range(KT):
                dve.tensor_copy(rel_w[:, m, :], bank[4 + m][:, 0:R0 * H]).then_inc(s_relwe, 1)
            dve.tensor_copy(rel_bias[:, :], bank[6][:, 0:R0 * H]).then_inc(s_relwe, 1)
            dve.wait_ge(s_relwe, 3)
            dve.wait_ge(s_posb, 1)
            for t in range(T):
                dve.wait_ge(s_qkv, t + 1)
                dve.tensor_tensor(qkv[:, t, 0:512], bank[2], row_in[:, 0:512], ALU.add).then_inc(s_qkve, 1)
                dve.tensor_tensor(qkv[:, t, 512:768], bank[3][:, 0:256], row_in[:, 512:768], ALU.add).then_inc(s_qkve, 1)
                dve.tensor_tensor(rel[:, t, :], bank[7][:, 0:R0 * H], rel_bias[:, :], ALU.add).then_inc(s_qkve, 1)
            dve.wait_ge(s_qkve, 3 * T)
            for hf in range(2):
                for t in range(B):
                    tile = 2 * t + hf
                    q_b = qkv[:, tile, 0:D].rearrange("p (o d) -> p o d", o=1).to_broadcast([P, B, D])
                    k_all = qkv[:, hf:T:2, D:2 * D]
                    st.link(dve.tensor_tensor(prod[t % 2][:, :, :], q_b, k_all, ALU.mult))
                    st.settle()
                    st.link(dve.tensor_reduce(sc0[:, t].rearrange("p s h -> p (s h)"),
                                              prod[t % 2][:, :, :].rearrange("p s (h d) -> p (s h) d", d=HD), X_AXIS, ALU.add))
                    st.settle()
                    lo = (B - 1 - t) * H
                    st.link(dve.tensor_tensor(sc0[:, t].rearrange("p s h -> p (s h)"), sc0[:, t].rearrange("p s h -> p (s h)"),
                                              rel[:, tile, lo:lo + B * H], ALU.add))
                st.settle()
                by_key = sc0[:, :, :, :].rearrange("p t s h -> p t h s")
                st.link(dve.tensor_reduce(sc0_max[:, :, :], by_key, X_AXIS, ALU.max))
                st.settle()
                max_b = sc0_max[:, :, :].rearrange("p t (o h) -> p t o h", o=1).to_broadcast([P, B, B, H])
                dve.tensor_tensor(sc0[:, :, :, :], sc0[:, :, :, :], max_b, ALU.subtract).then_inc(s_at0, 1)
                dve.wait_ge(s_at0e, hf + 1)
                st.link(dve.tensor_reduce(sc0_max[:, :, :], by_key, X_AXIS, ALU.add))
                st.settle()
                st.link(dve.reciprocal(sc0_max[:, :, :], sc0_max[:, :, :]))
                st.settle()
                st.link(dve.tensor_tensor(sc0[:, :, :, :], sc0[:, :, :, :], max_b, ALU.mult))
                st.settle()
                for t in range(B):
                    tile = 2 * t + hf
                    w_b = bcast(sc0[:, t].rearrange("p s (h o) -> p s h o", o=1), HD)
                    v_all = qkv[:, hf:T:2, 2 * D:3 * D].rearrange("p s (h d) -> p s h d", d=HD)
                    st.link(dve.tensor_tensor(prod[t % 2][:, :, :].rearrange("p s (h d) -> p s h d", d=HD), v_all, w_b, ALU.mult))
                    st.settle()
                    dve.tensor_reduce(tok[:, tile, :], prod[t % 2][:, :, :].rearrange("p s f -> p f s"), X_AXIS, ALU.add)\
                        .then_inc(s_tok1, 1)
            dve.wait_ge(s_tok1, T)

            def add_out(g, dst, src):
                for t in range(T):
                    dve.wait_ge(g.mm, t + 1)
                    dve.tensor_tensor(dst[:, t, :], src[:, t, :], gemm_out(g, t), ALU.add).then_inc(g.ev, 1)

            st.link(dve.tensor_tensor(x[:, :, :], x[:, :, :], per_tile_rows("L0_attn_out_proj_bias"), ALU.add))
            st.settle()
            add_out(gemm1, x, x)
            st.link(dve.memset(score[:, :, ER:2 * ER], SENTINEL))
            if stop <= 2:
                return
            dve.wait_ge(s_x, 2 * T)

            dve_norm(dve, st, norm2, x, u)
            dve.wait_ge(s_sq, T)
            st.link(dve.tensor_scalar(var_eps[:, :], var_eps[:, :], 1.0 / D, RMS_EPS, ALU.mult, ALU.add))
            st.settle()
            dve.tensor_copy(esum[:, :], var_eps[:, :]).then_inc(s_var, 1)
            dve_rstd(dve, st, rms)
            for t in range(T):
                dve.tensor_scalar(tok[:, t, :], u[:, t, :], rstd[:, t:t + 1], None, ALU.mult).then_inc(s_un, 1)
            def top_two():
                for t in range(T):
                    st.link(dve.max(top8[:, t, :], score[:, t, 0:ER]))
                st.settle()
                st.link(dve.memset(top8[:, :, 2:8], SENTINEL))
                st.settle()
                for t in range(T):
                    st.link(dve.match_replace(rest[:, t, :], top8[:, t, :], score[:, t, :], 0.0))
                st.settle()

            context_stored(dve)
            st.link(dve.tensor_tensor(rinv[:, :], rstd[:, :], var_eps[:, :], ALU.mult))
            st.settle()

            def weights_low(n, par, i):
                dve.wait_ge(s_whi, n * WPIECES + i + 1)
                dve.scalar_tensor_tensor(out=w_part[1][par][:, i, :], in0=w_f[:, i, :], scalar=W_SCALE,
                                         in1=w_part[0][par][:, i, :], op0=ALU.mult, op1=ALU.subtract).then_inc(s_wlo, 1)

            def router_gates():
                dve.wait_ge(s_loge, 1)
                st.link(dve.tensor_scalar(logit[:, :, :], logit[:, :, :], 1.0, None, ALU.add))
                st.settle()
                st.link(dve.reciprocal(score[:, :, 0:ER], logit[:, :, :]))
                st.settle()
                st.link(dve.tensor_reduce(esum[:, :], score[:, :, 0:ER], X_AXIS, ALU.add))
                st.settle()
                st.link(dve.reciprocal(esum[:, :], esum[:, :]))
                st.settle()
                top_two()
                st.link(dve.tensor_tensor(gate[:, :, :].rearrange("p e t -> p t e"), score[:, :, 0:ER], rest[:, :, 0:ER],
                                          ALU.subtract))
                st.settle()
                st.link(dve.tensor_tensor(gate[:, :, :], gate[:, :, :],
                                          esum[:, :].rearrange("p (o t) -> p o t", o=1).to_broadcast([P, ER, T]), ALU.mult))
                st.link(dve.memset(gate_t[:, :, ER:ER + ES], 1.0))
                st.settle()
                dve.tensor_copy(gate_t[:, :, 0:ER], gate[:, :, :].rearrange("p e t -> p t e")).then_inc(s_gate, 1)

            def expert(n, par, take, last=False, between=None):
                for job in range(2 * HM):
                    half, m = divmod(job, HM)
                    hc = slice(half * 512, (half + 1) * 512)
                    dve.wait_ge(s_gelu, n * 2 * HM + job + 1)
                    if m == 0 and not (isinstance(n, int) and n == 0):
                        dve.wait_ge(s_w2, (n - 1) * T + 4 * (half + 1))
                    dve.tensor_copy(hid_part[0][:, m, hc], hid_f[:, job % 4, :]).then_inc(s_hhi, 1)
                    dve.wait_ge(s_hhi, n * 2 * HM + job + 1)
                    dve.tensor_tensor(hid_part[1][:, m, hc], hid_f[:, job % 4, :], hid_part[0][:, m, hc], ALU.subtract)\
                        .then_inc(s_hlo, 1)
                if between:
                    between()
                for t in range(T):
                    if not last:
                        if t == 0 and not (isinstance(n, int) and n == 0):
                            dve.wait_ge(s_w2, n * T)
                        weights_low(n + 1, 1 - par, t)
                    dve.wait_ge(s_w2, n * T + t + 1)
                    if not (isinstance(n, int) and n == 0):
                        dve.wait_ge(s_acc, (n - 1) * T + t + 1)
                    take(n, par, t)

            def take_shared(n, par, t):
                src = u if n == 0 else tok
                dve.scalar_tensor_tensor(out=tok[:, t, :], in0=bank[4 + t % 4][:, 0:D], scalar=1.0 / W_SCALE,
                                         in1=src[:, t, :], op0=ALU.mult, op1=ALU.add).then_inc(s_acc, 1)

            def take_routed(n, par, t):
                dve.scalar_tensor_tensor(out=tok[:, t, :], in0=bank[4 + t % 4][:, 0:D], scalar=g_now[par][:, t:t + 1],
                                         in1=tok[:, t, :], op0=ALU.mult, op1=ALU.add).then_inc(s_acc, 1)

            for i in range(WPIECES):
                weights_low(0, 0, i)
            for half in range(2):
                turned(dve, turn2, half)
            for src, parts in ((xTs, x_part[0]), (xT, x_part[1])):
                for k in range(KT):
                    st.link(dve.tensor_copy(parts[0][:, k, :], src[:, k, :]))
                st.settle()
                for k in range(KT):
                    dve.tensor_tensor(parts[1][:, k, :], src[:, k, :], parts[0][:, k, :], ALU.subtract).then_inc(s_xlo, 1)
            dve.wait_ge(s_log, 1)
            dve.tensor_tensor(logit[:, :, :], bank[4][:, 0:T * ER].rearrange("p (t e) -> p t e", e=ER),
                              bcast(rinv[:, :].rearrange("p (t o) -> p t o", o=1), ER), ALU.mult).then_inc(s_logs, 1)
            expert(0, 0, take_shared, between=router_gates)
            expert(1, 1, take_shared)
            for t in range(T):
                dve.wait_ge(s_b2, t + 1)
                dve.wait_ge(s_acc, T + t + 1)
                dve.tensor_tensor(tok[:, t, :], tok[:, t, :], bank[2 + t % 2][:, 0:D], ALU.add).then_inc(s_b2e, 1)
            dve.wait_ge(s_b2e, T)
            st.settle()
            base = st.n

            def gates_of(e, par, steps):
                dve.tensor_scalar(g_now[par][:, :], gate[:, bass.ds(e, 1), :].rearrange("p o t -> p (o t)"),
                                  1.0 / W_SCALE, None, ALU.mult).then_inc(s_dve, 1)
                dve.wait_ge(s_dve, steps)

            with dve.Fori(0, (ER - 2) // 2) as i:
                for par in range(2):
                    gates_of(2 * i + par, par, 2 * i + (base + par + 1))
                    expert(2 * i + (2 + par), par, take_routed)
            for par in range(2):
                gates_of(ER - 2 + par, par, base + ER - 1 + par)
                expert(ER + par, par, take_routed, last=par == 1)
            st.n = base + ER
            dve.wait_ge(s_acc, (ER + ES) * T)
            for t in range(T):
                dve.tensor_tensor(x[:, t, :], x[:, t, :], tok[:, t, :], ALU.add).then_inc(s_x, 1)
            if stop <= 3:
                return
            dve.wait_ge(s_x, 3 * T)

            dve_norm(dve, st, norm3, x, u)
            for m in range(KT):
                for half in range(2):
                    job = 2 * m + half
                    dve.wait_ge(s_qxh, job + 1)
                    dve.scalar_tensor_tensor(out=q_lo[:, m, half * 512:(half + 1) * 512], in0=bank[2 + job % 2],
                                             scalar=col("L1_xattn_bq", m), in1=q_hi[:, m, half * 512:(half + 1) * 512],
                                             op0=ALU.add, op1=ALU.subtract).then_inc(s_qxl, 1)
            def group_max(g, i):
                dve.wait_ge(s_s1, g * S1N + (i + 1))
                if i == 0 and not (isinstance(g, int) and g == 0):
                    dve.wait_ge(s_mxa, g)
                h, qt, kb = product_of(i)
                at = (2 * h + qt) * 8 + kb
                dve.tensor_reduce(mx_part[:, at:at + 1], bank[i % 2], X_AXIS, ALU.max).then_inc(s_mx, 1)

            def split_max(st, src, rws, s_out):
                st.link(dve.tensor_scalar(m_neg[rws, :], src, -1.0, None, ALU.mult))
                st.settle()
                st.link(dve.tensor_copy(m_prt[rws, 0, :], m_neg[rws, :]))
                st.settle()
                st.link(dve.tensor_tensor(m_res[rws, :], m_neg[rws, :], m_prt[rws, 0, :], ALU.subtract))
                st.settle()
                st.link(dve.tensor_copy(m_prt[rws, 1, :], m_res[rws, :]))
                st.settle()
                dve.tensor_tensor(m_prt[rws, 2, :], m_res[rws, :], m_prt[rws, 1, :], ALU.subtract).then_inc(s_out, 1)

            def group_maxima(g):
                dve.wait_ge(s_mx, g * S1N + S1N)
                dve.tensor_reduce(mx[:, 0:2 * GH], mx_part[:, :].rearrange("p (j k) -> p j k", k=8), X_AXIS, ALU.max)\
                    .then_inc(s_mxa, 1)

            def group_parts(st, g, first):
                dve.wait_ge(s_mT, g + 1)
                if not first:
                    dve.wait_ge(s_mrow, g * 48)
                split_max(st, bank[3][0:2 * GH, 0:P], slice(0, 2 * GH), s_mp)

            def normalise(st, g, s_out):
                o = bank[3][:, 256:512].rearrange("p (q h d) -> p q h d", q=2, h=GH)
                st.link(dve.reciprocal(den[:, :, :], o[:, :, :, HD]))
                st.settle()
                dst = o_grp[:, g] if isinstance(g, int) else o_grp[:, bass.ds(g, 1)].rearrange("p o q h d -> p (o q) h d")
                dve.tensor_tensor(dst, o[:, :, :, 0:HD], bcast(den[:, :, :].rearrange("p q (h o) -> p q h o", o=1), HD),
                                  ALU.mult).then_inc(s_out, 1)

            def gather(s_out, bias):
                for b in range(B):
                    src = o_grp[:, 4 * b:4 * b + 4].rearrange("p g q h d -> p q g (h d)")
                    bias_b = row(bias).rearrange("p (o g c) -> p o g c", o=1, c=GH * HD).to_broadcast([P, 2, 4, GH * HD])
                    dst = tok[:, 2 * b:2 * b + 2, :].rearrange("p q (g c) -> p q g c", c=GH * HD)
                    dve.tensor_tensor(dst, src, bias_b, ALU.add).then_inc(s_out, 1)

            for i in range(S1N):
                group_max(0, i)
            group_maxima(0)
            group_parts(st, 0, True)
            for i in range(AHEAD):
                group_max(1, i)
            grp = Steps(dve, s_grp)
            STEPS = 5

            def group_vector(g, par, turn, first, last):
                grp.base, grp.n = g * STEPS, 0
                for c in range(CH):
                    if c == NORM_STEP and first:
                        grp.link(dve.memset(den[:, :, :], 1.0))
                    elif c == NORM_STEP:
                        dve.wait_ge(s_oT, g)
                        normalise(grp, g - 1, s_on)
                    beside = first_pass_at(g, par, turn, c)
                    for n, (other, _, _, i) in enumerate(beside):
                        group_max(other, i)
                        if i == S1N - 1:
                            group_maxima(other)
                        if c == MAX_STEP + 1 and n == 0:
                            group_parts(grp, g + 1, False)
                    if not last and not beside and c == MAX_STEP + 1:
                        group_parts(grp, g + 1, False)
                assert last or grp.n == STEPS

            each_group(dve, group_vector)
            dve.wait_ge(s_oT, NG)
            normalise(st, NG - 1, s_on)
            dve.wait_ge(s_on, NG)
            gather(s_tok3, "bv_x")
            dve.wait_ge(s_tok3, B)
            st.link(dve.tensor_tensor(x[:, :, :], x[:, :, :], per_tile_rows("L1_xattn_bo"), ALU.add))
            st.settle()
            add_out(gemm3, x, x)
            if stop <= 4:
                return
            dve.wait_ge(s_x, 4 * T)

            def self_take_values(sa):
                for t in range(T):
                    sa.wait(dve, "vproj", t + 1)
                    dve.tensor_copy(sa.v[:, t, :, 0:HD], bank[2 + t % 2][:, 0:D].rearrange("p (h d) -> p h d", d=HD))\
                        .then_inc(signals["vtaken"].s, 1)

            def self_attention(sa):
                for n in range(B * H):
                    hp, qt = divmod(n, 2)
                    sa.wait(dve, "s1", n + 1)
                    dst = mx[:, 4 * hp + qt:4 * hp + qt + 3:2]
                    dve.tensor_reduce(dst, bank[4 + n % 4].rearrange("p (i k) -> p i k", i=2), X_AXIS, ALU.max)\
                        .then_inc(signals["mx"].s, 1)
                sa.wait(dve, "mT", 1)
                split_max(st, bank[3][:, 0:P], slice(0, P), signals["mp"].s)
                for g in range(NG):
                    sa.wait(dve, "pv", 2 * (g + 1))
                    dve.tensor_copy(oT[g % 2][:, :], bank[2][:, 0:S]).then_inc(signals["oc"].s, 1)
                    if g >= 1:
                        sa.wait(dve, "oT", g)
                        normalise(st, g - 1, signals["on"].s)
                sa.wait(dve, "oT", NG)
                normalise(st, NG - 1, signals["on"].s)
                sa.wait(dve, "on", NG)

            dve_norm(dve, st, norm4a, x, u)
            dve_norm(dve, st, norm4b, u, tok)
            dve.wait_ge(s_rope, 32)
            for job in range(8):
                n, m, half = job // 4, (job // 2) % 2, job % 2
                i = job % 2
                sa5.wait(dve, "fproj", job + 1)
                if job >= 1:
                    sa5.wait(dve, "flo", job)
                if job == 4:
                    sa5.wait(dve, "fst", 32)
                tb = lambda ap: ap[:, :].rearrange("p (o q) -> p o q", o=1).to_broadcast([P, 2, S])
                v2 = lambda ap: ap.rearrange("p (b q) -> p b q", b=2)
                st.link(dve.scalar_tensor_tensor(out=v2(rot_a[i][:, :]), in0=v2(bank[4]), scalar=col(("L1_attn_bq", "L1_attn_bk")[n], m),
                                                 in1=tb(cosT), op0=ALU.add, op1=ALU.mult))
                st.link(dve.scalar_tensor_tensor(out=v2(rot_b[i][:, :]), in0=v2(bank[5]), scalar=col(("bq_swapped", "bk_swapped")[n], m),
                                                 in1=tb(sinT), op0=ALU.add, op1=ALU.mult))
                st.settle()
                st.link(dve.tensor_tensor(rot_a[i][:, :], rot_a[i][:, :], rot_b[i][:, :], ALU.add))
                st.settle()
                hc = slice(half * 512, (half + 1) * 512)
                st.link(dve.tensor_copy(sa5.hi[:, m, hc], rot_a[i][:, :]))
                st.settle()
                dve.tensor_tensor(sa5.lo[:, m, hc], rot_a[i][:, :], sa5.hi[:, m, hc], ALU.subtract).then_inc(signals["flo"].s, 1)
            self_take_values(sa5)
            self_attention(sa5)
            gather(s_tok4, "L1_attn_bv")
            dve.wait_ge(s_tok4, B)
            st.link(dve.tensor_tensor(u[:, :, :], u[:, :, :], per_tile_rows("L1_attn_bo"), ALU.add))
            st.settle()
            add_out(gemm4, u, u)
            dve.wait_ge(gemm4.ev, T)
            dve_norm(dve, st, norm5, u, tok)
            st.link(dve.tensor_tensor(x[:, :, :], x[:, :, :], u[:, :, :], ALU.add))
            st.settle()
            st.link(dve.tensor_tensor(x[:, :, :], x[:, :, :], per_tile_rows("L1_attn_b2"), ALU.add))
            st.settle()
            for t in range(T):
                dve.wait_ge(s_m2, t + 1)
                dve.tensor_tensor(x[:, t, :], x[:, t, :], bank[2 + t % 2][:, 0:D], ALU.add).then_inc(s_x, 1)
            if stop <= 5:
                return
            dve.wait_ge(s_x, 5 * T)

            dve_norm(dve, st, norm6, x, u)
            for job in range(8):
                n, m, half = job // 4, (job // 2) % 2, job % 2
                hc = slice(half * 512, (half + 1) * 512)
                sa6.wait(dve, "fhi", job + 1)
                dve.scalar_tensor_tensor(out=sa6.lo[:, m, hc], in0=bank[4], scalar=col(("L1_ffn_bq", "L1_ffn_bk")[n], m),
                                         in1=sa6.hi[:, m, hc], op0=ALU.add, op1=ALU.subtract).then_inc(signals["flo"].s, 1)
            self_take_values(sa6)
            self_attention(sa6)
            gather(s_tok6, "L1_ffn_bv")
            for t in range(T):
                dve.wait_ge(gemm6.mm, t + 1)
                dve.tensor_tensor(tok[:, t, :], gemm_out(gemm6, t), row("L1_ffn_bo"), ALU.add).then_inc(gemm6.ev, 1)
            dve.wait_ge(gemm6.ev, T)
            dve_norm(dve, st, norm6a, tok, tok)
            st.link(dve.tensor_tensor(tok[:, :, :], tok[:, :, :], per_tile_rows("L1_ffn_g1"), ALU.mult))
            st.settle()
            st.link(dve.tensor_tensor(tok[:, :, :], tok[:, :, :], per_tile_rows("L1_ffn_be1"), ALU.add))
            st.settle()
            for t in range(T):
                dve.tensor_tensor(u[:, t, :], u[:, t, :], tok[:, t, :], ALU.add).then_inc(s_y6, 1)
            dve.wait_ge(s_y6, T)
            st.link(dve.tensor_tensor(x[:, :, :], x[:, :, :], u[:, :, :], ALU.add))
            st.settle()
            st.link(dve.tensor_tensor(x[:, :, :], x[:, :, :], per_tile_rows("L1_ffn_be2"), ALU.add))
            st.settle()
            dve.wait_ge(s_log6, 1)
            st.link(dve.tensor_tensor(logit[:, :, :], bank[2][:, 0:T * ER].rearrange("p (t e) -> p t e", e=ER),
                                      row("L1_ffn_bg").rearrange("p (o e) -> p o e", o=1).to_broadcast([P, T, ER]), ALU.add))
            st.settle()
            st.link(dve.tensor_reduce(esum[:, :], logit[:, :, :], X_AXIS, ALU.max))
            st.settle()
            esum_b = bcast(esum[:, :].rearrange("p (t o) -> p t o", o=1), ER)
            dve.tensor_tensor(logit[:, :, :], logit[:, :, :], esum_b, ALU.subtract).then_inc(s_logs6, 1)
            dve.wait_ge(s_loge6, 1)
            st.link(dve.tensor_reduce(esum[:, :], logit[:, :, :], X_AXIS, ALU.add))
            st.settle()
            st.link(dve.reciprocal(esum[:, :], esum[:, :]))
            st.settle()
            st.link(dve.tensor_tensor(score[:, :, 0:ER], logit[:, :, :], esum_b, ALU.mult))
            st.settle()
            top_two()
            dve.tensor_tensor(gate_t[:, :, 0:ER], score[:, :, 0:ER], rest[:, :, 0:ER], ALU.subtract).then_inc(s_gate6, 1)
            for t in range(T):
                dve.wait_ge(s_b26, t + 1)
                dve.tensor_copy(tok[:, t, :], bank[2 + t % 2][:, 0:D]).then_inc(s_b2e6, 1)
            dve.wait_ge(s_b2e6, T)
            dve.wait_ge(s_gate6, 1)
            n = 0
            for e in range(ER // 2):
                for t in range(T):
                    dve.wait_ge(s_we, n + 1)
                    for j in range(2):
                        if e or j:
                            dve.wait_ge(s_wee, 2 * n + 1 if j else 2 * (n - T) + 2)
                        dve.scalar_tensor_tensor(out=tok[:, t, :], in0=bank[4 + n % 4][:, j * D:(j + 1) * D],
                                                 scalar=gate_t[:, t, 2 * e + j:2 * e + j + 1], in1=tok[:, t, :],
                                                 op0=ALU.mult, op1=ALU.add).then_inc(s_wee, 1)
                    n += 1
            dve.wait_ge(s_wee, ER * T)
            dve_norm(dve, st, norm6m, tok, tok)
            st.link(dve.tensor_tensor(tok[:, :, :], tok[:, :, :], per_tile_rows("L1_ffn_g2"), ALU.mult))
            st.settle()
            for t in range(T):
                dve.tensor_tensor(x[:, t, :], x[:, t, :], tok[:, t, :], ALU.add).then_inc(s_x, 1)
            dve.wait_ge(s_x, 6 * T)

        @block.gpsimd
        def _(pool):
            if stop <= 1:
                return
            pool.wait_ge(s_x, T)
            for i in range(2):
                pool.memset(v_st[i][:, :, :, :], 1.0).then_inc(s_vones, 1)
            pool.wait_ge(s_m8, 16)
            pool.tensor_scalar(m_16[:, :], m_u32[:, :].bitcast(U8), MASKED, None, ALU.mult).then_inc(s_m16, 1)
            pool.wait_ge(s_m16, 1)
            for j in range(H // GH):
                pool.dma_start(mask_scr.rearrange("(b j) n -> j b n", b=B)[j], m_16[:, :]).then_inc(s_mst, 16)
            for n, (b, c) in enumerate(proj_blocks):
                for m in range(KT):
                    job = 2 * n + m
                    i = job % 3
                    pool.wait_ge(s_kf, 2 * (job + 1))
                    if job >= 3:
                        pool.wait_ge(s_kst[i], 64 * (job // 3))
                    pool.tensor_tensor(k_lo[i][:, :], k_f[job % 2][:, :], k_hi[i][:, :], ALU.subtract).then_inc(s_klo, 1)
            if stop <= 3:
                return
            pool.wait_ge(s_x, 3 * T)
            for n, q_ in enumerate((*qa, *qb)):
                pool.memset(q_[64:128, :, :], 0.0).then_inc(s_qz, 1)
                pool.wait_ge(s_qz, n + 1)
                pool.memset(q_[R_MASK:R_MASK + 1, :, :], UNMASK_ROW).then_inc(s_init4, 1)
            for n, k_ in enumerate(kst):
                pool.wait_ge(s_init4, 4 + n)
                pool.memset(k_[64:128, :, :], 1.0).then_inc(s_init4, 1)
            if stop <= 4:
                return
            for n, sa in ((4, sa5), (5, sa6)):
                pool.wait_ge(s_x, n * T)
                pool.memset(sa.v[:, :, :, HD:HV], 1.0).then_inc(signals["rows_set"].s, 1)
                sa.wait(pool, "rows_set", 1)
                pool.memset(sa.k[64:128, :, :], 1.0).then_inc(signals["rows_set"].s, 1)
                sa.wait(pool, "rows_set", 2)
                pool.memset(sa.q[64:128, :, :], 0.0).then_inc(signals["rows_set"].s, 1)
                if stop <= 5:
                    return


def kernel(**inputs):
    import concourse.bacc as bacc
    from concourse.bass_utils import run_bass_kernel_spmd as run

    i = {n: np.asarray(v) for n, v in inputs.items()}

    def t(name):
        return i[name].T

    pos_in_head = np.arange(P) % HD
    inv_freq = np.float32(1.0) / np.float32(10000.0) ** (np.arange(0, HD, 2, dtype=np.float32) / np.float32(HD))
    angles = np.arange(S, dtype=np.float32)[None, :] * inv_freq[pos_in_head // 2][:, None]
    signs = np.where(pos_in_head % 2 == 0, -1.0, 1.0)[:, None]
    swap = np.arange(D) ^ 1
    named = {
        **{n: i[n] for n in ("L0_xattn_Wq_b", "L0_attn_pos_proj_bias", "L0_ffn_g_shared", "L0_ffn_g_routed",
                             "L1_xattn_bq", "L1_attn_g1", "L1_attn_beta1", "L1_attn_g2", "L1_attn_beta2",
                             "L1_attn_bq", "L1_attn_bk", "L1_attn_b1", "L1_ffn_bq", "L1_ffn_bk", "L0_xattn_out_b",
                             "L0_attn_in_proj_bias", "L0_attn_out_proj_bias", "L1_xattn_bo", "L1_attn_bv",
                             "L1_attn_bo", "L1_attn_b2", "L1_ffn_bv", "L1_ffn_bo", "L1_ffn_g1", "L1_ffn_be1",
                             "L1_ffn_g2", "L1_ffn_be2", "L1_ffn_bg")},
        "bq0": i["L0_attn_in_proj_bias"][0:D],
        "L0_attn_r_r_bias": i["L0_attn_r_r_bias"].reshape(-1),
        "L0_attn_r_w_bias": i["L0_attn_r_w_bias"].reshape(-1),
        "bk_x": i["L1_xattn_bkv"][0:D],
        "bv_x": i["L1_xattn_bkv"][D:2 * D],
        "bq_swapped": i["L1_attn_bq"][swap],
        "bk_swapped": i["L1_attn_bk"][swap],
    }
    arrays = {
        "x": i["x"], "ctx": i["ctx_1024"], "ctxT": i["ctx_1024"].transpose(0, 2, 1),
        "mask": i["mask_BxS2_bk0"].view(np.uint32),
        "ident": np.eye(P, dtype=np.float32),
        "cols": np.concatenate([named[n.split(":")[0]].reshape(-1, P).T for n in COLS], axis=1),
        "rows": np.concatenate([named[n.split(":")[0]] for n in ROWS])[None, :],
        "row0": i["L0_xattn_Wq_b"][None, :], "row_in": i["L0_attn_in_proj_bias"][None, :],
        "w0qT": t("L0_xattn_Wq_w"), "w0oT": t("L0_xattn_out_w"),
        "w1inT": t("L0_attn_in_proj_weight"), "w1q": i["L0_attn_in_proj_weight"][0:D],
        "w1oT": t("L0_attn_out_proj_weight"), "w1pT": t("L0_attn_pos_proj_weight"),
        "posT": i["L0_attn_pos"][0:R0, 0, :].T,
        "head_mask": (np.arange(D)[:, None] // HD == np.arange(H)[None, :]).astype(np.float32),
        "wkv": i["L1_xattn_Wkv"], "wq_x": i["L1_xattn_Wq"], "wo_x": i["L1_xattn_Wo"],
        "cent": i["L0_ffn_centroids"],
        "b2_all": np.concatenate([i["L0_ffn_b2_r"], i["L0_ffn_b2_s"]]),
        "w1_all": np.concatenate([i["L0_ffn_W1_r"], i["L0_ffn_W1_s"]]),
        "w2_all": np.concatenate([i["L0_ffn_W2_r"], i["L0_ffn_W2_s"]]),
        "b1_all": np.concatenate([i["L0_ffn_b1_r"], i["L0_ffn_b1_s"]]).reshape(ER + ES, HM, P).transpose(0, 2, 1),
        "r_w": np.stack([i["L1_attn_Wq"], i["L1_attn_Wq"][:, swap], i["L1_attn_Wk"], i["L1_attn_Wk"][:, swap],
                         i["L1_attn_Wv"], i["L1_attn_Wo"]]),
        "r_w1": i["L1_attn_W1"], "r_w2": i["L1_attn_W2"],
        "cosT": np.cos(angles).astype(np.float32), "sinT": (np.sin(angles) * signs).astype(np.float32),
        "l_w": np.stack([i["L1_ffn_Wq"], i["L1_ffn_Wk"], i["L1_ffn_Wv"], i["L1_ffn_Wo"]]),
        "l_we": i["L1_ffn_We"].reshape(ER // 2, 2, D, D).transpose(0, 2, 1, 3).reshape(ER // 2, D, 2 * D),
        "wg": i["L1_ffn_Wg"], "bexp": i["L1_ffn_bexp"],
    }
    nc = bacc.Bacc("TRN2", target_bir_lowering=False, num_devices=1)
    held, aps = {}, {}
    for name, v in arrays.items():
        v = np.ascontiguousarray(v)
        held[f"in_{name}"] = v
        aps[name] = nc.dram_tensor(f"in_{name}", v.shape, mybir.dt.from_np(v.dtype), kind="ExternalInput").ap()
    out = nc.dram_tensor("out", (B, S, D), F32, kind="ExternalOutput").ap()
    build(nc, aps, out)
    r = run(nc, [held], core_ids=[0])
    return r.results[0]["out"]
```

```python
from contextlib import ExitStack

import numpy as np

import concourse.bass as bass
from concourse import mybir

F32 = mybir.dt.float32
F16 = mybir.dt.float16
U8 = mybir.dt.uint8
U32 = mybir.dt.uint32
ALU = mybir.AluOpType
ACT = mybir.ActivationFunctionType
X_AXIS = mybir.AxisListType.X

P = 128
B, S, D, S2 = 4, 256, 256, 4096
T = B * S // P
KT = D // P
NTOK = B * S
H, HD = 16, 16
H0, DH0 = 16, 64
W0 = H0 * DH0
R0 = 2 * B - 1
HID = 1024
HM = HID // P
WPIECES = 2 * KT * HID // 512
W_SCALE = 1024.0
ER, ES = 8, 2
LN_EPS = 1e-5
RMS_EPS = float(np.finfo(np.float32).eps)
SCALE = float(HD) ** -0.5
GH = 4
NG = B * H // GH
CH = S2 // P
KB = 1024
NKB = S2 // KB
MASKED, UNMASK_ROW = -60000.0, 16384.0
R_MASK, R_MAX = 64, 65
SENTINEL = -5.0
TWO_ONES = float(np.array([1.0, 1.0], dtype=np.float16).view(np.float32)[0])
HV = HD + 1

COLS = ["L0_xattn_Wq_b:8", "L0_attn_pos_proj_bias:2", "bq0:2", "L0_attn_r_r_bias:2", "L0_ffn_g_shared:2",
        "L0_ffn_g_routed:2", "L1_xattn_bq:2", "bk_x:2", "L1_attn_g1:2", "L1_attn_beta1:2", "L1_attn_g2:2",
        "L1_attn_beta2:2", "L1_attn_bq:2", "L1_attn_bk:2", "bq_swapped:2", "bk_swapped:2", "L1_attn_b1:8",
        "L1_ffn_bq:2", "L1_ffn_bk:2"]
ROWS = ["L0_xattn_out_b:256", "L0_attn_r_w_bias:256",
        "L0_attn_out_proj_bias:256", "bv_x:256", "L1_xattn_bo:256", "L1_attn_bv:256", "L1_attn_bo:256",
        "L1_attn_b2:256", "L1_ffn_bv:256", "L1_ffn_bo:256", "L1_ffn_g1:256", "L1_ffn_be1:256",
        "L1_ffn_g2:256", "L1_ffn_be2:256", "L1_ffn_bg:8"]


def offsets(names):
    at, out = 0, {}
    for n in names:
        name, width = n.split(":")
        out[name] = (at, int(width))
        at += int(width)
    return out, at


COL_AT, NCOLS = offsets(COLS)
ROW_AT, NROWS = offsets(ROWS)


def build(nc, a, out):
    with ExitStack() as top:
        def sem(name):
            return top.enter_context(nc.semaphore(name))

        def sb(name, shape, dt=F32, scope=top):
            return scope.enter_context(nc.sbuf_tensor(name, shape, dt))

        def dram(name, shape, dt):
            return nc.dram_tensor(name, shape, dt, kind="Internal").ap()

        k_scr = dram("k_scr", [B, H // GH, 2, GH * HD, S2], F16)
        q_scr = dram("q_scr", [B, H // GH, 2, GH * HD, S], F16)
        v_scr = dram("v_scr", [NG, P, CH, GH * HV], F32)
        mask_scr = dram("mask_scr", [NG, S2], F16)
        self_scr = [dram(f"self_scr{i}", [2, 2, D, NTOK], F16) for i in range(2)]

        x = sb("x", [P, T, D])
        u = sb("u", [P, T, D])
        tok = sb("tok", [P, T, D])
        xT = sb("xT", [P, KT, NTOK])
        ident = sb("ident", [P, P])
        cols = sb("cols", [P, NCOLS])
        rows = sb("rows", [P, NROWS])
        stats = sb("stats", [P, T, 6])
        meanvar = sb("meanvar", [P, T, 2])
        var_eps = sb("var_eps", [P, T])
        deviation = sb("deviation", [P, T])
        rstd = sb("rstd", [P, T])
        rtmp = sb("rtmp", [P, T])
        logit = sb("logit", [P, T, ER])
        score = sb("score", [P, T, 2 * ER])
        top8 = sb("top8", [P, T, 8])
        rest = sb("rest", [P, T, 2 * ER])
        esum = sb("esum", [P, T])
        gate = sb("gate", [P, ER, T])
        gate_t = sb("gate_t", [P, T, ER + ES])
        gateT = sb("gateT", [ER + ES, NTOK])
        wkv = sb("wkv", [P, KT, 2 * D])
        wqo_x = sb("wqo_x", [P, 2, KT, D])
        wb = sb("wb", [P, 4096])

        def col(name, i):
            at = COL_AT[name][0] + i
            return cols[:, at:at + 1]

        def row(name, lo=0, hi=None, parts=slice(0, P)):
            at, n = ROW_AT[name]
            return rows[parts, at + lo:at + (n if hi is None else hi)]

        psum = [top.enter_context(nc.psum_tensor(f"bank{i}", [P, 512], F32)) for i in range(4)]
        pair = [top.enter_context(nc.psum_tensor(f"pair{i}", [P, 1024], F32)) for i in range(2)]
        bank = psum + [pair[0][:, 0:512], pair[0][:, 512:1024], pair[1][:, 0:512], pair[1][:, 512:1024]]
        bank = [b_[:, :] for b_ in bank]

        b_in = wb[:, 0:1536].rearrange("p (k n) -> p k n", k=KT)
        b_q = wb[:, 1536:2048].rearrange("p (k n) -> p k n", k=KT)
        b_o = wb[:, 2048:2560].rearrange("p (k n) -> p k n", k=KT)
        b_p = wb[:, 2560:3072].rearrange("p (k n) -> p k n", k=KT)
        b_pos = wb[:, 3072:3072 + KT * R0].rearrange("p (k n) -> p k n", k=KT)
        b_mask = wb[:, 3100:3100 + KT * H].rearrange("p (k n) -> p k n", k=KT)
        r_w = wb[:, 0:3072].rearrange("p (w k n) -> p w k n", w=6, k=KT)
        l_w = wb[:, 0:2048].rearrange("p (w k n) -> p w k n", w=4, k=KT)

        s_tokens = sem("tokens_loaded")
        s_start = sem("constants_loaded")
        s_wa = sem("large_weights_loaded")
        s_wb = sem("weight_area_loaded")
        s_wkv = sem("cross_weights_loaded")
        s_dve = sem("vector_steps")
        s_x = sem("residual_updated")
        s_store = sem("output_stored")

        s_var = sem("norm_variance")
        s_dev = sem("norm_deviation")
        s_nt = sem("norm_tiles")
        s_tmm = sem("tiles_transposed")
        s_tev = sem("transposes_copied")
        counted = {"norms": 0, "normed": 0, "turned": 0, "copied": 0}

        class Norm:

            def __init__(self, tiles=T):
                self.root, self.tiles = counted["norms"], counted["normed"]
                counted["norms"] += 1
                counted["normed"] += tiles

            def wait(self, eng, n):
                eng.wait_ge(s_nt, self.tiles + n)

        class Turn:

            def __init__(self, src, dests):
                self.src, self.dests = src, dests
                self.mm, self.ev = counted["turned"], counted["copied"]
                counted["turned"] += 4
                counted["copied"] += 4 * len(dests)

        class Steps:

            def __init__(self, eng, s):
                self.eng, self.s, self.n, self.base = eng, s, 0, 0

            def link(self, ins):
                ins.then_inc(self.s, 1)
                self.n += 1

            def settle(self):
                self.eng.wait_ge(self.s, self.base + self.n)

        def dve_rstd(dve, st, nm):
            dve.wait_ge(s_dev, nm.root + 1)
            st.link(dve.reciprocal(rstd[:, :], deviation[:, :]))
            st.settle()
            st.link(dve.tensor_tensor(rtmp[:, :], rstd[:, :], rstd[:, :], ALU.mult))
            st.settle()
            st.link(dve.tensor_tensor(rtmp[:, :], rtmp[:, :], var_eps[:, :], ALU.mult))
            st.settle()
            st.link(dve.tensor_scalar(rtmp[:, :], rtmp[:, :], -0.5, 1.5, ALU.mult, ALU.add))
            st.settle()
            st.link(dve.tensor_tensor(rstd[:, :], rstd[:, :], rtmp[:, :], ALU.mult))
            st.settle()

        def tile_stats(dve, st, src, t):
            st.link(dve.bn_stats(stats[:, t, :], src[:, t, :]))

        def dve_norm(dve, st, nm, src, dst, measured=False):
            for t in range(0 if measured else T):
                tile_stats(dve, st, src, t)
            st.settle()
            for t in range(T):
                st.link(dve.bn_aggr(meanvar[:, t, :], stats[:, t, :]))
            st.settle()
            dve.tensor_scalar(var_eps[:, :], meanvar[:, :, 1], LN_EPS, None, ALU.add).then_inc(s_var, 1)
            dve.wait_ge(s_var, nm.root + 1)
            dve_rstd(dve, st, nm)
            for t in range(T):
                dve.tensor_scalar(dst[:, t, :], src[:, t, :], meanvar[:, t, 0:1], rstd[:, t:t + 1],
                                  ALU.subtract, ALU.mult).then_inc(s_nt, 1)
            nm.wait(dve, T)

        def act_dev(act, nm):
            act.wait_ge(s_var, nm.root + 1)
            act.activation(deviation[:, :], var_eps[:, :], ACT.Sqrt).then_inc(s_dev, 1)

        def pe_turn(pe, tr, ready):
            for half in range(2):
                ready(half)
                for k in range(KT):
                    job = 2 * half + k
                    if job >= 2:
                        pe.wait_ge(s_tev, tr.ev + len(tr.dests) * (job - 1))
                    for j in range(4):
                        last = pe.transpose(bank[job % 2][:, j * P:(j + 1) * P],
                                            tr.src[:, 4 * half + j, k * P:(k + 1) * P], ident[:, :])
                    last.then_inc(s_tmm, 1)

        def act_turn(act, tr):
            for half in range(2):
                for k in range(KT):
                    job = 2 * half + k
                    act.wait_ge(s_tmm, tr.mm + job + 1)
                    for dst, scale, bias in tr.dests:
                        o = dst[:, k, half * 512:(half + 1) * 512]
                        if scale is None:
                            act.activation(o, bank[job % 2], ACT.Copy).then_inc(s_tev, 1)
                        elif bias is None:
                            act.activation(o, bank[job % 2], ACT.Copy, scale=col(scale, k)).then_inc(s_tev, 1)
                        else:
                            act.activation(o, bank[job % 2], ACT.Identity, scale=col(scale, k),
                                           bias=col(bias, k)).then_inc(s_tev, 1)

        def turned(eng, tr, half=1):
            eng.wait_ge(s_tev, tr.ev + len(tr.dests) * 2 * (half + 1))

        class Gemm:

            def __init__(self, name, lhs, w, residual=None):
                self.lhs, self.w, self.kt, self.banks = lhs, w, KT, (2, 3)
                self.mm = sem(f"{name}_product")
                self.ev = sem(f"{name}_taken") if residual is None else s_x
                self.base = 0 if residual is None else residual * T

        def pe_gemm(pe, g, tr):
            n = g.w.shape[2]
            for t in range(T):
                if t % 4 == 0:
                    turned(pe, tr, t // 4)
                if t >= len(g.banks):
                    pe.wait_ge(g.ev, g.base + t - len(g.banks) + 1)
                for k in range(g.kt):
                    last = pe.matmul(bank[g.banks[t % len(g.banks)]][:, 0:n], g.lhs[:, k, t * P:(t + 1) * P],
                                     g.w[:, k, :], start=(k == 0), stop=(k == g.kt - 1))
                last.then_inc(g.mm, 1)

        def gemm_out(g, t):
            return bank[g.banks[t % len(g.banks)]][:, 0:g.w.shape[2]]

        with ExitStack() as sc:
            CB = 8
            NCB = S2 // P // CB
            NBUF = 3
            w0q = sb("w0q", [P, KT, W0], F32, sc)
            w0o = sb("w0o", [P, W0 // P, D], F32, sc)
            row0 = sb("row0", [P, W0], F32, sc)
            ctx_sb = [sb(f"ctx_sb{i}", [P, CB, D], F32, sc) for i in range(NBUF)]
            ctx_hi = [sb(f"ctx_hi{i}", [P, CB, D + 1], F16, sc) for i in range(2)]
            ctx_lo = [sb(f"ctx_lo{i}", [P, CB, D], F16, sc) for i in range(2)]
            q0T = sb("q0T", [P, W0 // P, NTOK], F32, sc)
            gram = sb("gram", [P, KT, D + 1], F32, sc)
            gw = sb("gw", [P, KT, W0], F32, sc)
            gw_row = sb("gw_row", [1, W0], F32, sc)
            kv0 = sb("kv0", [P, H0 // 2, P], F32, sc)
            lin = [sb(f"lin{i}", [P, H0, DH0], F32, sc) for i in range(2)]
            lin_max = sb("lin_max", [P, 2, H0], F32, sc)
            lin_sum = sb("lin_sum", [P, 2, H0], F32, sc)
            linT = sb("linT", [P, W0 // P, P], F32, sc)
        norm0 = Norm()
        turn0 = Turn(u, [(xT, None, None)])
        s_ctx = [sem(f"ctx_loaded{i}") for i in range(NBUF)]
        s_ones = sem("ctx_ones_set")
        s_ghi = sem("ctx_block_high")
        s_glo = sem("ctx_block_low")
        s_gram_blk = sem("ctx_block_used")
        s_q0 = sem("q0_product")
        s_q0e = sem("q0_copied")
        s_grame = sem("gram_copied")
        s_gw = sem("gram_w_product")
        s_gwe = sem("gram_w_copied")
        s_kv0 = sem("kv0_product")
        s_kv0e = sem("kv0_copied")
        s_lg = sem("linear_logits")
        s_lgs = sem("linear_logits_shifted")
        s_lge = sem("linear_exp")
        s_lgn = sem("linear_weights")
        s_lt = sem("linear_transposed")
        s_lte = sem("linear_transposes_copied")
        s_lo = sem("linear_out")

        with ExitStack() as sc:
            qkv = sb("qkv", [P, T, 3 * D], F32, sc)
            rel = sb("rel", [P, T, R0 * H], F32, sc)
            posT = sb("posT", [P, KT, R0], F32, sc)
            pos_blk = sb("pos_blk", [P, KT, R0, H], F32, sc)
            rel_w = sb("rel_w", [P, KT, R0 * H], F32, sc)
            rel_bias = sb("rel_bias", [P, R0 * H], F32, sc)
            bqrr = sb("bqrr", [P, KT], F32, sc)
            bqrr_rep = sb("bqrr_rep", [P, KT, P], F32, sc)
            row_in = sb("row_in", [P, 3 * D], F32, sc)
            prod = [sb(f"prod{i}", [P, B, D], F32, sc) for i in range(2)]
            sc0 = sb("sc0", [P, B, B, H], F32, sc)
            sc0_max = sb("sc0_max", [P, B, H], F32, sc)
            cT = [sb(f"cT{i}", [P, KT, 512], F32, sc) for i in range(3)]
            c_part = [[sb(f"c_{part}{i}", [P, KT, 512], F16, sc) for part in ("hi", "lo")] for i in range(2)]
            wkv_part = [sb(f"wkv_{part}", [P, KT, 2 * D], F16, sc) for part in ("hi", "lo")]
            k_f = [sb(f"k_f{i}", [P, 512], F32, sc) for i in range(3)]
            k_hi = [sb(f"k_hi{i}", [P, 512], F16, sc) for i in range(3)]
            k_lo = [sb(f"k_lo{i}", [P, 512], F16, sc) for i in range(3)]
            VC = CH // 4
            v_st = [sb(f"v_st{i}", [P, H // GH, VC, GH * HV], F32, sc) for i in range(2)]
            m_u32 = sb("m_u32", [B, S2 // 4], U32, sc)
            m_16 = sb("m_16", [B, S2], F16, sc)
        norm1 = Norm()
        turn1 = Turn(u, [(xT, None, None)])
        s_rin = sem("in_proj_bias_loaded")
        s_posT = sem("pos_product")
        s_posb = sem("pos_blocks")
        s_relw = sem("rel_w_product")
        s_relwe = sem("rel_w_copied")
        s_qkv = sem("qkv_product")
        s_qkve = sem("qkv_taken")
        s_at0 = sem("batch_scores_shifted")
        s_at0e = sem("batch_exp")
        s_tok1 = sem("batch_context_tiles")
        turn1o = Turn(tok, [(xT, None, None)])
        gemm1 = Gemm("out1", xT, b_o, residual=1)
        s_cT = [sem(f"ctxT_loaded{i}") for i in range(3)]
        s_wkvp = sem("cross_weights_parts")
        s_chi = sem("ctxT_high")
        s_clo = sem("ctxT_low")
        s_kp = sem("k_product")
        s_kf = sem("k_copied")
        s_klo = sem("k_low_part")
        s_kst = [sem(f"k_stored{i}") for i in range(3)]
        s_vp = sem("v_product")
        s_ve = sem("v_copied")
        s_vst = [sem(f"v_stored{i}") for i in range(2)]
        s_vones = sem("v_ones_set")
        s_m8 = sem("mask_loaded")
        s_m16 = sem("mask_row")
        s_mst = sem("mask_stored")

        with ExitStack() as sc:
            xTs = sb("xTs", [P, KT, NTOK], F32, sc)
            junk3 = sb("junk3", [P, D], F32, sc)
            w_f = sb("w_f", [P, WPIECES, 512], F32, sc)
            w_part = [[sb(f"w_{part}{i}", [P, WPIECES, 512], F16, sc) for i in range(2)] for part in ("hi", "lo")]
            b_1 = [sb(f"b_1{i}", [P, HM], F32, sc) for i in range(2)]
            x_part = [[sb(f"x_{src}_{part}", [P, KT, NTOK], F16, sc) for part in ("hi", "lo")] for src in ("s", "r")]
            hid_f = sb("hid_f", [P, 4, 512], F32, sc)
            hid_part = [sb(f"hid_{part}", [P, HM, NTOK], F16, sc) for part in ("hi", "lo")]
            xTr = hid_f[:, :, :].rearrange("p (k a) n -> p k (a n)", k=KT)
            cent = sb("cent", [P, KT, ER], F32, sc)
            b2_all = sb("b2_all", [ER + ES, D], F32, sc)
            rinv = sb("rinv", [P, T], F32, sc)
            g_now = [sb(f"g_now{i}", [P, T], F32, sc) for i in range(2)]
        norm2 = Norm()
        rms = Norm(tiles=0)
        s_sq = sem("squares_summed")
        s_un = sem("rms_tiles")
        turn2 = Turn(tok, [(xTs, "L0_ffn_g_shared", None), (xT, "L0_ffn_g_routed", None), (xTr, None, None)])
        s_w3 = sem("router_weights_loaded")
        s_wexp = sem("expert_loaded")
        s_whi = sem("expert_weights_high")
        s_wlo = sem("expert_weights_low")
        s_xlo = sem("expert_inputs_parts")
        s_hhi = sem("expert_hidden_high")
        s_hlo = sem("expert_hidden_low")
        s_log = sem("router_logits")
        s_logs = sem("router_logits_scaled")
        s_loge = sem("router_exp")
        s_gate = sem("gates_ready")
        s_gT = sem("gates_transposed")
        s_gTe = sem("gates_copied")
        s_b2 = sem("b2_product")
        s_b2e = sem("b2_taken")
        s_w1 = sem("expert_hidden_product")
        s_gelu = sem("expert_hidden")
        s_w2 = sem("expert_out_product")
        s_acc = sem("expert_accumulated")

        attention_scope = ExitStack()
        NP_ = 4
        pexp = [sb(f"pexp{i}", [P, GH, S], F32, attention_scope) for i in range(NP_)]
        mx_part = sb("mx_part", [P, GH * 2 * (S2 // 512)], F32, attention_scope)
        mx = sb("mx", [P, 128], F32, attention_scope)
        m_neg = sb("m_neg", [P, P], F32, attention_scope)
        m_res = sb("m_res", [P, P], F32, attention_scope)
        m_prt = sb("m_prt", [P, 3, P], F16, attention_scope)
        oT = [sb(f"oT{i}", [P, S], F32, attention_scope) for i in range(2)]
        o_grp = sb("o_grp", [P, NG, 2, GH, HD], F32, attention_scope)
        den = sb("den", [P, 2, GH], F32, attention_scope)
        with ExitStack() as sc:
            q_hi = sb("q_hi", [P, KT, NTOK], F16, sc)
            q_lo = sb("q_lo", [P, KT, NTOK], F16, sc)
            kst = [sb(f"kst{i}", [P, GH, S2], F16, sc) for i in range(2)]
            qa = [sb(f"qa{i}", [P, GH, S], F16, sc) for i in range(2)]
            qb = [sb(f"qb{i}", [P, GH, S], F16, sc) for i in range(2)]
            vst = [sb(f"vst{i}", [P, CH, GH * HV], F32, sc) for i in range(2)]
        norm3 = Norm()
        turn3 = Turn(u, [(xT, None, None)])
        s_qx = sem("cross_q_product")
        s_qxh = sem("cross_q_high")
        s_qxl = sem("cross_q_low")
        s_qst = sem("cross_q_stored")
        s_init4 = sem("stack_rows_set")
        s_qz = sem("query_rows_zeroed")
        s_qa = [sem(f"group_queries_loaded{i}") for i in range(2)]
        s_qb = [sem(f"group_queries_again_loaded{i}") for i in range(2)]
        s_kh = [[sem(f"group_keys{f}_loaded{i}") for f in range(2)] for i in range(2)]
        s_vl = [sem(f"group_values_loaded{i}") for i in range(2)]
        s_s1 = sem("scores_first_pass")
        s_mx = sem("partial_maxima")
        s_mxa = sem("group_maxima")
        s_mT = sem("maxima_transposed")
        s_mp = sem("maxima_parts")
        s_mrow = sem("maxima_rows_stored")
        s_s2 = sem("scores_second_pass")
        s_exp = sem("weights")
        s_pv = sem("weighted_values")
        s_oc = sem("weighted_values_copied")
        s_oT = sem("weighted_values_transposed")
        s_on = sem("group_normalised")
        s_grp = sem("group_vector_steps")
        turn3o = Turn(tok, [(xT, None, None)])
        gemm3 = Gemm("out3", xT, wqo_x[:, 1], residual=3)
        s_tok3 = sem("cross_context_tiles")

        class Counted:

            def __init__(self, name, each):
                self.s, self.each = sem("self_" + name), each

        SELF_LOADS = 16
        SELF_JOBS = [(half, n, m) for half in range(2) for n in range(2) for m in range(KT)]
        SELF_ITEMS = B * H // 2
        ITEMS_AFTER = {5: range(0, 10), 6: range(10, 21), 7: range(21, SELF_ITEMS)}

        def items_beside(n):
            return range(SELF_ITEMS + min(3 * n, SELF_ITEMS), SELF_ITEMS + min(3 * n + 3, SELF_ITEMS))

        SELF_MAX_STEP = -(-SELF_ITEMS // 3)

        signals = {
            "fproj": Counted("qk_product", 8), "fhi": Counted("high_parts", 0),
            "flo": Counted("low_parts", 8),
            "fst": Counted("parts_stored", 128), "qk0_loaded": Counted("first_stacks_loaded", 16 * SELF_LOADS),
            "qk1_loaded": Counted("second_stacks_loaded", 16 * SELF_LOADS),
            "rows_set": Counted("constant_rows_set", 3), "vproj": Counted("v_product", T),
            "vtaken": Counted("v_copied", T), "s1": Counted("scores_first_pass", B * H),
            "mx": Counted("maxima", B * H), "mT": Counted("maxima_transposed", 2),
            "mp": Counted("maxima_parts", 2), "mrow": Counted("maxima_rows_stored", 96),
            "s2": Counted("scores_second_pass", 2 * NG), "exp": Counted("weights", 2 * NG),
            "pv": Counted("weighted_values", 2 * NG), "oc": Counted("weighted_values_copied", NG),
            "oT": Counted("weighted_values_transposed", NG), "on": Counted("group_normalised", NG),
        }

        class SelfAttention:

            def __init__(self, turn, scope):
                i = f"self{turn}_"
                self.turn = turn
                self.hi = sb(i + "hi", [P, KT, NTOK], F16, scope)
                self.lo = sb(i + "lo", [P, KT, NTOK], F16, scope)
                self.k = sb(i + "k", [P, B * H, S], F16, scope)
                self.q = sb(i + "q", [P, B * H, S], F16, scope)
                self.v = sb(i + "v", [P, T, H, HV], F32, scope)

            def wait(self, eng, what, n):
                eng.wait_ge(signals[what].s, self.turn * signals[what].each + n)

        with ExitStack() as sc:
            sa5 = SelfAttention(0, sc)
            cosT = sb("cosT", [P, S], F32, sc)
            sinT = sb("sinT", [P, S], F32, sc)
            rot_a = [sb(f"rot_a{i}", [P, 512], F32, sc) for i in range(2)]
            rot_b = [sb(f"rot_b{i}", [P, 512], F32, sc) for i in range(2)]
        with ExitStack() as sc:
            hid5 = sb("hid5", [P, HM, NTOK], F32, sc)
            r_w1 = sb("r_w1", [P, KT, HID], F32, sc)
            r_w2 = sb("r_w2", [P, HM, D], F32, sc)
        norm4a, norm4b, norm5 = Norm(), Norm(), Norm()
        turn4 = Turn(tok, [(xT, "L1_attn_g1", "L1_attn_beta1")])
        turn4o = Turn(tok, [(xT, None, None)])
        gemm4 = Gemm("out4", xT, r_w[:, 5])
        turn5 = Turn(tok, [(xT, "L1_attn_g2", "L1_attn_beta2")])
        s_rope = sem("rotary_tables_loaded")
        s_tok4 = sem("self5_context_tiles")
        s_h5 = sem("mlp_hidden_product")
        s_h5e = sem("mlp_hidden")
        s_m2 = sem("mlp_out_product")

        with ExitStack() as sc:
            sa6 = SelfAttention(1, sc)
            b2_l = sb("b2_l", [ER, D], F32, sc)
            wg_l = sb("wg_l", [P, KT, ER], F32, sc)
        with ExitStack() as sc:
            l_we = sb("l_we", [P, ER // 2, KT, 2 * D], F32, sc)
        attention_scope.close()
        norm6, norm6a, norm6m = Norm(), Norm(), Norm()
        turn6 = Turn(u, [(xT, None, None)])
        turn6o = Turn(tok, [(xT, None, None)])
        gemm6 = Gemm("out6", xT, l_w[:, 3])
        turn7 = Turn(u, [(xT, None, None)])
        s_w6 = sem("last_weights_loaded")
        s_tok6 = sem("self6_context_tiles")
        s_y6 = sem("last_residual_tiles")
        s_log6 = sem("router6_logits")
        s_logs6 = sem("router6_logits_shifted")
        s_loge6 = sem("router6_exp")
        s_gate6 = sem("gates6_ready")
        s_b26 = sem("bexp_product")
        s_b2e6 = sem("bexp_taken")
        s_we = sem("expert6_product")
        s_wee = sem("expert6_accumulated")

        block = top.enter_context(nc.Block())

        N_START = 4
        ctx_blocks = [(b, c) for b in range(B) for c in range(NCB)]
        NPB = S2 // 512
        proj_blocks = [(b, c) for b in range(B) for c in range(NPB)]
        EXP_BLOCKS = (8, 16)
        S1N = GH * 2 * (S2 // 512)
        COPY_STEP = 2
        NORM_STEP = 4
        MAX_STEP = 27
        PER_STEP = S1N // CH
        AHEAD = PER_STEP * (CH - 1 - MAX_STEP)

        def first_pass_at(g, par, turn, c):
            if isinstance(g, int) and (g == NG - 1 or (g == NG - 2 and c > MAX_STEP)):
                return []
            if c <= MAX_STEP:
                return [(g + 1, 1 - par, turn + par, AHEAD + PER_STEP * c + i) for i in range(PER_STEP)]
            return [(g + 2, par, turn + 1, PER_STEP * (c - 1 - MAX_STEP) + i) for i in range(PER_STEP)]

        def product_of(i):
            f, h, qt, kb = i // 32, i // 8 % 4, i // 4 % 2, i % 4
            return h, qt, 4 * f + kb

        def each_group(eng, body):
            body(0, 0, 1, True, False)
            body(1, 1, 1, False, False)
            with eng.Fori(0, (NG - 4) // 2) as i:
                for par in range(2):
                    body(2 * i + (2 + par), par, i + 2, False, False)
            body(NG - 2, 0, NG // 2, False, False)
            body(NG - 1, 1, NG // 2, False, True)

        def context_stored(eng):
            for i in range(3):
                eng.wait_ge(s_kst[i], 64 * len(range(i, 2 * len(proj_blocks), 3)))
            for i in range(2):
                eng.wait_ge(s_vst[i], 64 * 8)
            eng.wait_ge(s_mst, 16 * (H // GH))

        @block.sync
        def _(sp):
            def store():
                sp.wait_ge(s_x, 6 * T)
                sp.dma_start(out.rearrange("b (h p) d -> p (b h) d", p=P), x[:, :, :]).then_inc(s_store, 16)
                sp.wait_ge(s_store, 16)

            def load_context(n):
                b, c = ctx_blocks[n]
                if n >= NBUF:
                    sp.wait_ge(s_glo, n - NBUF + 1)
                src = a["ctx"][b].rearrange("(n p c) d -> n p c d", p=P, c=CB)[c]
                sp.dma_start(ctx_sb[n % NBUF][:, :, :], src).then_inc(s_ctx[n % NBUF], 16)

            load_context(0)
            sp.dma_start(x[:, :, :], a["x"].rearrange("b (h p) d -> p (b h) d", p=P)).then_inc(s_tokens, 16)
            load_context(1)
            sp.dma_start(ident[:, :], a["ident"]).then_inc(s_start, 16)
            sp.dma_start(cols[:, :], a["cols"]).then_inc(s_start, 16)
            for n in range(2, len(ctx_blocks)):
                load_context(n)
                if n == 3:
                    sp.dma_start(w0q[:, :, :], a["w0qT"].rearrange("(k p) n -> p k n", p=P)).then_inc(s_wa, 16)
                    sp.dma_start(rows[:, :], a["rows"].to_broadcast([P, NROWS])).then_inc(s_start, 16)
                    sp.dma_start(row0[:, :], a["row0"].to_broadcast([P, W0])).then_inc(s_start, 16)
                    sp.dma_start(w0o[:, :, :], a["w0oT"].rearrange("(k p) n -> p k n", p=P)).then_inc(s_wa, 16)
                if n == 5:
                    for dst, name in ((b_in, "w1inT"), (b_q, "w1q"), (b_o, "w1oT"), (b_p, "w1pT"), (b_pos, "posT"),
                                      (b_mask, "head_mask")):
                        sp.dma_start(dst, a[name].rearrange("(k p) n -> p k n", p=P)).then_inc(s_wb, 16)
                    sp.dma_start(wkv[:, :, :], a["wkv"].rearrange("(k p) n -> p k n", p=P)).then_inc(s_wkv, 16)
                    sp.dma_start(wqo_x[:, 0], a["wq_x"].rearrange("(k p) n -> p k n", p=P)).then_inc(s_wkv, 16)
                    sp.dma_start(wqo_x[:, 1], a["wo_x"].rearrange("(k p) n -> p k n", p=P)).then_inc(s_wkv, 16)
            sp.wait_ge(s_x, T)
            sp.dma_start(row_in[:, :], a["row_in"].to_broadcast([P, 3 * D])).then_inc(s_rin, 16)
            sp.dma_start(m_u32[:, :], a["mask"]).then_inc(s_m8, 16)
            def store_projection(n):
                b, c = proj_blocks[n]
                for m in range(KT):
                    job = 2 * n + m
                    sp.wait_ge(s_klo, job + 1)
                    for part, src in enumerate((k_hi[job % 3], k_lo[job % 3])):
                        for g in range(2):
                            sp.dma_start(k_scr[b, 2 * m + g, part, :, c * 512:(c + 1) * 512],
                                         src[64 * g:64 * g + 64, :]).then_inc(s_kst[job % 3], 16)
                if n % 2 == 1:
                    vb = n // 2
                    sp.wait_ge(s_ve, 2 * (n + 1))
                    cb = (vb % 4) * VC
                    for g in range(H // GH):
                        sp.dma_start(v_scr[b * 4 + g, :, cb:cb + VC, :], v_st[vb % 2][:, g]).then_inc(s_vst[vb % 2], 16)

            for n, (b, c) in enumerate(proj_blocks):
                if n >= 3:
                    sp.wait_ge(s_clo, n - 2)
                sp.dma_start(cT[n % 3][:, :, :], a["ctxT"][b].rearrange("(k p) n -> p k n", p=P)[:, :, c * 512:(c + 1) * 512])\
                    .then_inc(s_cT[n % 3], 16)
                if n >= 3:
                    store_projection(n - 3)
            for n in range(len(proj_blocks) - 3, len(proj_blocks)):
                store_projection(n)
            sp.wait_ge(s_x, 2 * T)
            sp.dma_start(r_w, a["r_w"].rearrange("w (k p) n -> p w k n", p=P)).then_inc(s_wb, 16)
            sp.wait_ge(s_x, 2 * T)
            context_stored(sp)
            sp.dma_start(cent[:, :, :], a["cent"].rearrange("(k p) n -> p k n", p=P)).then_inc(s_w3, 16)
            sp.dma_start(b2_all[:, :], a["b2_all"]).then_inc(s_w3, 16)

            def expert(e, par):
                one = bass.ds(e, 1)
                sp.dma_start(w_f[:, 0:WPIECES // 2, :].rearrange("p (k a) n -> p k (a n)", k=KT),
                             a["w1_all"][one].rearrange("o (k p) n -> (o p) k n", p=P)).then_inc(s_wexp, 16)
                sp.dma_start(w_f[:, WPIECES // 2:WPIECES, :].rearrange("p b (a n) -> p (b a) n", n=D),
                             a["w2_all"][one].rearrange("o (k p) n -> (o p) k n", p=P)).then_inc(s_wexp, 16)
                sp.dma_start(b_1[par][:, :], a["b1_all"][one].rearrange("o p n -> (o p) n")).then_inc(s_wexp, 16)

            expert(ER, 0)
            sp.wait_ge(s_wlo, WPIECES)
            expert(ER + 1, 1)
            with sp.Fori(0, ER // 2) as i:
                for par in range(2):
                    sp.wait_ge(s_wlo, (2 * i + par) * WPIECES + 2 * WPIECES)
                    expert(2 * i + par, par)
            k_g = k_scr.rearrange("b g s f n -> (b g) s f n")

            def key_rows(g, par, f):
                one = bass.ds(g, 1)
                kc = slice(f * S2 // 2, (f + 1) * S2 // 2)
                for h in range(GH):
                    for part in range(2):
                        src = k_g[one, part, h * HD:(h + 1) * HD, kc].to_broadcast([2, HD, S2 // 2])
                        sp.dma_start(kst[par][32 * part:32 * part + 32, h, kc], src).then_inc(s_kh[par][f], 16)

            def mask_row(g, par, f):
                kc = slice(f * S2 // 2, (f + 1) * S2 // 2)
                src = mask_scr[bass.ds(g, 1), kc].rearrange("g (o n) -> g o n", o=1).to_broadcast([1, GH, S2 // 2])
                sp.dma_start(kst[par][R_MASK:R_MASK + 1, :, kc], src).then_inc(s_kh[par][f], 16)

            def load_keys(g, par, f):
                key_rows(g, par, f)
                mask_row(g, par, f)

            sp.wait_ge(s_x, 3 * T)
            key_rows(0, 0, 0)
            key_rows(0, 0, 1)
            for k in range(KT):
                sp.wait_ge(s_qxl, 2 * (k + 1))
                for part, src in enumerate((q_hi, q_lo)):
                    for g in range(2):
                        sp.dma_start(q_scr[:, 2 * k + g, part].rearrange("b f q -> f b q"),
                                     src[64 * g:64 * g + 64, k, :].rearrange("f (b q) -> f b q", b=B)).then_inc(s_qst, 16)
            sp.wait_ge(s_qst, 16 * 8)
            sp.wait_ge(s_init4, 5)

            q_g = q_scr.rearrange("b g s f n -> (b g) s f n")

            def q_parts(dst, g, s_):
                one = bass.ds(g, 1)
                for r, part in enumerate((0, 1, 0, 1)):
                    sp.dma_start(dst[16 * r:16 * r + 16, :, :],
                                 q_g[one, part].rearrange("o (h d) n -> (o d) h n", d=HD)).then_inc(s_, 16)

            def load_values(g, par):
                sp.dma_start(vst[par][:, :, :], v_scr[bass.ds(g, 1)].rearrange("o p c n -> (o p) c n")).then_inc(s_vl[par], 16)

            def max_rows(par):
                for i in range(3):
                    sp.dma_start(qb[par][R_MAX + i:R_MAX + i + 1, :, :], m_prt[0:2 * GH, i, :]).then_inc(s_mrow, 16)

            q_parts(qa[0], 0, s_qa[0])
            mask_row(0, 0, 0)
            mask_row(0, 0, 1)
            q_parts(qb[0], 0, s_qb[0])
            load_values(0, 0)
            q_parts(qa[1], 1, s_qa[1])
            sp.wait_ge(s_init4, 6)
            load_keys(1, 1, 0)
            sp.wait_ge(s_mp, 1)
            max_rows(0)

            def next_group(g, par, turn, first, last):
                if last:
                    return
                if not first:
                    sp.wait_ge(s_s2, g * CH)
                load_keys(g + 1, 1 - par, 1)
                q_parts(qb[1 - par], g + 1, s_qb[1 - par])
                if not first:
                    sp.wait_ge(s_pv, g * CH)
                load_values(g + 1, 1 - par)
                if not (isinstance(g, int) and g == NG - 2):
                    sp.wait_ge(s_s1, g * S1N + S1N)
                    q_parts(qa[par], g + 2, s_qa[par])
                    sp.wait_ge(s_s2, g * CH + CH // 2)
                    load_keys(g + 2, par, 0)
                sp.wait_ge(s_mp, g + 2)
                max_rows(1 - par)

            each_group(sp, next_group)

            def self_io(sa, scr):
                def max_rows(half):
                    sa.wait(sp, "rows_set", 3)
                    sa.wait(sp, "mp", half + 1)
                    for i in range(3):
                        sp.dma_start(sa.q[R_MAX + i:R_MAX + i + 1, 32 * half:32 * half + 32, :], m_prt[0:64, i, :])\
                            .then_inc(signals["mrow"].s, 16)

                for half in range(2):
                    for n in range(2):
                        sa.wait(sp, "flo", 4 * half + 2 * n + 2)
                        for part, src in enumerate((sa.hi, sa.lo)):
                            sp.dma_start(scr[n, part].rearrange("(k p) q -> p k q", p=P)[:, :, half * 512:(half + 1) * 512],
                                         src[:, :, n * 512:(n + 1) * 512]).then_inc(signals["fst"].s, 16)
                        sa.wait(sp, "fst", 64 * half + 32 * (n + 1))
                        order, dst = (((0, 1, 0, 1), sa.q), ((0, 0, 1, 1), sa.k))[n]
                        for r, part in enumerate(order):
                            for b in (2 * half, 2 * half + 1):
                                sp.dma_start(dst[16 * r:16 * r + 16, b * H:(b + 1) * H, :],
                                             scr[n, part].rearrange("(h d) (b q) -> b d h q", d=HD, b=B)[b])\
                                    .then_inc(signals[f"qk{half}_loaded"].s, 16)
                max_rows(0)
                max_rows(1)

            sp.wait_ge(s_x, 4 * T)
            sp.dma_start(cosT[:, :], a["cosT"]).then_inc(s_rope, 16)
            sp.dma_start(sinT[:, :], a["sinT"]).then_inc(s_rope, 16)
            self_io(sa5, self_scr[0])
            sa5.wait(sp, "on", NG)
            sp.dma_start(r_w1[:, :, :], a["r_w1"].rearrange("(k p) n -> p k n", p=P)).then_inc(s_wa, 16)
            sp.dma_start(r_w2[:, :, :], a["r_w2"].rearrange("(k p) n -> p k n", p=P)).then_inc(s_wa, 16)
            sp.wait_ge(s_x, 5 * T)
            sp.dma_start(l_w, a["l_w"].rearrange("w (k p) n -> p w k n", p=P)).then_inc(s_wb, 16)
            sp.dma_start(b2_l[:, :], a["bexp"]).then_inc(s_w6, 16)
            sp.dma_start(wg_l[:, :, :], a["wg"].rearrange("(k p) n -> p k n", p=P)).then_inc(s_w6, 16)
            self_io(sa6, self_scr[1])
            sa6.wait(sp, "on", NG)
            sp.dma_start(l_we[:, :, :, :], a["l_we"].rearrange("e (k p) n -> p e k n", p=P)).then_inc(s_wa, 16)
            store()

        @block.tensor
        def _(pe):
            def tiles_ready(nm):
                return lambda half: nm.wait(pe, 4 * (half + 1))

            def gram_of(b):
                if b >= 1:
                    pe.wait_ge(s_grame, 2 * b)
                if b == 0:
                    pe.wait_ge(s_ones, 2)
                for c in range(NCB):
                    n = b * NCB + c
                    pe.wait_ge(s_glo, n + 1)
                    hi, lo = ctx_hi[n % 2], ctx_lo[n % 2]
                    for j in range(CB):
                        for m in range(KT):
                            mc = slice(m * P, (m + 1) * P)
                            pe.matmul(bank[m][:, 0:D + 1], hi[:, j, mc], hi[:, j, :], start=(c == 0 and j == 0), stop=False)
                            pe.matmul(bank[m][:, 0:D], hi[:, j, mc], lo[:, j, :], start=False, stop=False)
                            last = pe.matmul(bank[m][:, 0:D + 1], lo[:, j, mc], hi[:, j, :], start=False,
                                             stop=(c == NCB - 1 and j == CB - 1))
                    last.then_inc(s_gram_blk, 1)

            gram_of(0)
            pe.wait_ge(s_grame, 2)
            pe.wait_ge(s_start, 16 * N_START)
            pe_turn(pe, turn0, tiles_ready(norm0))
            pe.wait_ge(s_wa, 32)
            job = 0
            for half in range(2):
                turned(pe, turn0, half)
                for m in range(W0 // P):
                    if job >= 2:
                        pe.wait_ge(s_q0e, job - 1)
                    for k in range(KT):
                        last = pe.matmul(bank[2 + job % 2], w0q[:, k, m * P:(m + 1) * P],
                                         xT[:, k, half * 512:(half + 1) * 512], start=(k == 0), stop=(k == KT - 1))
                    last.then_inc(s_q0, 1)
                    job += 1

            def kv_of(b):
                pe.wait_ge(s_grame, 2 * (b + 1))
                if b == 0:
                    pe.wait_ge(s_q0e, W0 // P * 2)
                else:
                    pe.wait_ge(s_x, 2 * b)
                    pe.wait_ge(s_lte, 4 * b)
                n = 6 * b
                for m in range(KT + 1):
                    cs, rws = (slice(m * P, (m + 1) * P), slice(0, P)) if m < KT else (slice(D, D + 1), slice(0, 1))
                    for h in range(2):
                        if n >= 6 * b + 2:
                            pe.wait_ge(s_gwe, n - 1)
                        for k in range(KT):
                            last = pe.matmul(bank[2 + n % 2][rws, :], gram[:, k, cs],
                                             w0q[:, k, h * 512:(h + 1) * 512], start=(k == 0), stop=(k == KT - 1))
                        last.then_inc(s_gw, 1)
                        n += 1
                pe.wait_ge(s_gwe, 6 * (b + 1))
                for j in range(2):
                    for i in range(4):
                        h = 4 * j + i
                        hc = slice(h * P, (h + 1) * P)
                        o = bank[2 + j][:, i * P:(i + 1) * P]
                        for k in range(KT):
                            pe.matmul(o, w0q[:, k, hc], gw[:, k, hc], start=(k == 0), stop=False)
                        last = pe.matmul(o, row0[0:1, h * P:(h + 1) * P], gw_row[:, hc],
                                         start=False, stop=True)
                    last.then_inc(s_kv0, 1)

            def logits_of(b):
                pe.wait_ge(s_kv0e, 4 * (b + 1))
                for hf in range(2):
                    t = 2 * b + hf
                    if b >= 1:
                        pe.wait_ge(s_lgs, t - 1)
                    for m in range(W0 // P):
                        last = pe.matmul(pair[hf][:, m * P:(m + 1) * P], q0T[:, m, t * P:(t + 1) * P], kv0[:, m, :],
                                         start=(m % 4 == 0), stop=(m % 4 == 3), skip_group_check=True)
                    last.then_inc(s_lg, 1)

            def out_of(b):
                for hf in range(2):
                    t = 2 * b + hf
                    pe.wait_ge(s_lgn, t + 1)
                    for j in range(2):
                        n = 2 * t + j
                        if n >= 1:
                            pe.wait_ge(s_lte, n)
                        for i in range(4):
                            m = 4 * j + i
                            last = pe.transpose(bank[3][:, i * P:(i + 1) * P],
                                                lin[hf][:, 2 * m:2 * m + 2, :].rearrange("p h d -> p (h d)"), ident[:, :])
                        last.then_inc(s_lt, 1)
                    pe.wait_ge(s_lte, 2 * t + 2)
                    if t >= 1:
                        pe.wait_ge(s_x, t)
                    for m in range(W0 // P):
                        last = pe.matmul(bank[2][:, 0:D], linT[:, m, :], w0o[:, m, :], start=(m == 0),
                                         stop=(m == W0 // P - 1))
                    last.then_inc(s_lo, 1)

            turned(pe, turn0)
            for b in range(B + 1):
                if 0 < b < B:
                    gram_of(b)
                if b > 0:
                    out_of(b - 1)
                if b < B:
                    kv_of(b)
                    logits_of(b)

            pe.wait_ge(s_wb, 16 * 6)
            for m in range(KT):
                for k in range(KT):
                    last = pe.matmul(bank[4 + m][:, 0:R0], b_p[:, k, m * P:(m + 1) * P], b_pos[:, k, :],
                                     start=(k == 0), stop=(k == KT - 1))
            last.then_inc(s_posT, 1)
            pe.wait_ge(s_posb, 1)
            for m in range(KT):
                for k in range(KT):
                    last = pe.matmul(bank[4 + m][:, 0:R0 * H], b_q[:, k, m * P:(m + 1) * P],
                                     pos_blk[:, k].rearrange("p j h -> p (j h)"), start=(k == 0), stop=(k == KT - 1))
            for k in range(KT):
                last = pe.matmul(bank[6][:, 0:R0 * H], bqrr_rep[:, k, :], pos_blk[:, k].rearrange("p j h -> p (j h)"),
                                 start=(k == 0), stop=(k == KT - 1))
            last.then_inc(s_relw, 1)
            pe_turn(pe, turn1, tiles_ready(norm1))
            pe.wait_ge(s_relwe, 3)
            for t in range(T):
                if t % 4 == 0:
                    turned(pe, turn1, t // 4)
                if t >= 1:
                    pe.wait_ge(s_qkve, 3 * t)
                for k in range(KT):
                    lhs = xT[:, k, t * P:(t + 1) * P]
                    pe.matmul(bank[2][:, :], lhs, b_in[:, k, 0:512], start=(k == 0), stop=(k == KT - 1))
                    pe.matmul(bank[3][:, 0:256], lhs, b_in[:, k, 512:768], start=(k == 0), stop=(k == KT - 1))
                    last = pe.matmul(bank[7][:, 0:R0 * H], lhs, rel_w[:, k, :], start=(k == 0), stop=(k == KT - 1))
                last.then_inc(s_qkv, 1)

            pe.wait_ge(s_wkvp, 2)
            for n in range(len(proj_blocks)):
                c_hi, c_lo = c_part[n % 2]
                pe.wait_ge(s_clo, n + 1)
                for m in range(KT):
                    job = 2 * n + m
                    if job >= 2:
                        pe.wait_ge(s_kf, 2 * (job - 1))
                    for k in range(KT):
                        for i, (w, c_) in enumerate(((wkv_part[0], c_hi), (wkv_part[0], c_lo), (wkv_part[1], c_hi))):
                            last = pe.matmul(bank[4 + job % 2], w[:, k, m * P:(m + 1) * P], c_[:, k, :],
                                             start=(k == 0 and i == 0), stop=(k == KT - 1 and i == 2))
                    last.then_inc(s_kp, 1)
                for job in (2 * n, 2 * n + 1):
                    if job == 1:
                        pe.wait_ge(s_qkve, 3 * T)
                    if job >= 2:
                        pe.wait_ge(s_ve, job - 1)
                    for cc in range(2):
                        j = 2 * (job % 2) + cc
                        o = bank[6 + job % 2].rearrange("p (g c f) -> p c g f", g=H // GH, c=2)[:, cc]
                        for k in range(KT):
                            for i, (c_, w) in enumerate(((c_hi, wkv_part[0]), (c_hi, wkv_part[1]), (c_lo, wkv_part[0]))):
                                last = pe.matmul(o, c_[:, k, j * P:(j + 1) * P], w[:, k, D:2 * D],
                                                 start=(k == 0 and i == 0), stop=(k == KT - 1 and i == 2),
                                                 skip_group_check=True)
                    last.then_inc(s_vp, 1)

            pe_turn(pe, turn1o, lambda half: pe.wait_ge(s_tok1, T))
            pe_gemm(pe, gemm1, turn1o)

            pe_turn(pe, turn2, lambda half: pe.wait_ge(s_un, 4 * (half + 1)))
            turned(pe, turn2)
            pe.wait_ge(s_w3, 32)
            for t in range(T):
                for k in range(KT):
                    last = pe.matmul(bank[4][:, t * ER:(t + 1) * ER], xTr[:, k, t * P:(t + 1) * P], cent[:, k, :],
                                     start=(k == 0), stop=(k == KT - 1), skip_group_check=True)
            last.then_inc(s_log, 1)

            def turn_gates():
                pe.wait_ge(s_gate, 1)
                pe.wait_ge(s_gelu, 4 * HM)
                for j in range(2):
                    for i in range(4):
                        last = pe.transpose(bank[j][0:ER + ES, i * P:(i + 1) * P], gate_t[:, 4 * j + i, :], ident[:, :])
                    last.then_inc(s_gT, 1)

            def expert(n, par, src, first=False, between=None):
                w_hi, w_lo = w_part[0][par], w_part[1][par]
                pe.wait_ge(s_wlo, n * WPIECES + WPIECES)
                for job in range(2 * HM):
                    half, m = divmod(job, HM)
                    if not (first and job < 4):
                        pe.wait_ge(s_gelu, n * 2 * HM + job - 3)
                    hc = slice(half * 512, (half + 1) * 512)
                    for k in range(KT):
                        piece, at = k * (HID // 512) + m // 4, m % 4 * P
                        for w, x_ in ((w_hi, 0), (w_hi, 1), (w_lo, 0)):
                            last = pe.matmul(bank[job % 4], w[:, piece, at:at + P], src[x_][:, k, hc],
                                             start=(k == 0 and x_ == 0 and w is w_hi),
                                             stop=(k == KT - 1 and w is w_lo))
                    last.then_inc(s_w1, 1)
                if between:
                    between()
                for t in range(T):
                    if t % 4 == 0:
                        pe.wait_ge(s_hlo, n * 2 * HM + (t // 4 + 1) * HM)
                    if not (first and t < 4):
                        pe.wait_ge(s_acc, n * T + t - 3)
                    elif t == 0:
                        pe.wait_ge(s_logs, 1)
                    for m in range(HM):
                        wc = slice(m % 2 * D, (m % 2 + 1) * D)
                        for h_, w in ((0, w_hi), (0, w_lo), (1, w_hi)):
                            last = pe.matmul(bank[4 + t % 4][:, 0:D], hid_part[h_][:, m, t * P:(t + 1) * P],
                                             w[:, WPIECES // 2 + m // 2, wc], start=(m == 0 and h_ == 0 and w is w_hi),
                                             stop=(m == HM - 1 and h_ == 1))
                    last.then_inc(s_w2, 1)

            pe.wait_ge(s_xlo, 2 * KT)
            expert(0, 0, x_part[0], first=True)
            expert(1, 1, x_part[0], between=turn_gates)
            pe.wait_ge(s_gTe, 2)
            for t in range(T):
                if t >= 2:
                    pe.wait_ge(s_b2e, t - 1)
                pe.matmul(bank[2 + t % 2][:, 0:D], gateT[:, t * P:(t + 1) * P], b2_all[:, :], start=True, stop=True)\
                    .then_inc(s_b2, 1)
            pe.wait_ge(s_b2e, T)
            with pe.Fori(0, (ER - 2) // 2) as i:
                for par in range(2):
                    expert(2 * i + (2 + par), par, x_part[1])
            for par in range(2):
                expert(ER + par, par, x_part[1])

            pe_turn(pe, turn3, tiles_ready(norm3))
            turned(pe, turn3)
            for m in range(KT):
                for half in range(2):
                    job = 2 * m + half
                    if job >= 2:
                        pe.wait_ge(s_qxl, job - 1)
                    for k in range(KT):
                        last = pe.matmul(bank[2 + job % 2], wqo_x[:, 0, k, m * P:(m + 1) * P],
                                         xT[:, k, half * 512:(half + 1) * 512], start=(k == 0), stop=(k == KT - 1))
                    last.then_inc(s_qx, 1)
            pe.wait_ge(s_qxl, 4)

            def first_pass(g, par, turn, i):
                h, qt, kb = product_of(i)
                if i == 0:
                    pe.wait_ge(s_qa[par], turn * 64)
                if i % (S1N // 2) == 0:
                    pe.wait_ge(s_kh[par][i // (S1N // 2)], turn * 16 * (2 * GH + 1))
                if not (isinstance(g, int) and g == 0 and i < 2):
                    pe.wait_ge(s_mx, g * S1N + (i - 1))
                pe.matmul(bank[i % 2], qa[par][:, h, qt * P:(qt + 1) * P],
                          kst[par][:, h, kb * 512:(kb + 1) * 512], start=True, stop=True).then_inc(s_s1, 1)

            def turn_maxima(g, first):
                pe.wait_ge(s_mxa, g + 1)
                if not first:
                    pe.wait_ge(s_on, g - 1)
                pe.transpose(bank[3][0:2 * GH, 0:P], mx[:, 0:2 * GH], ident[:, :]).then_inc(s_mT, 1)

            def weigh(g, par, c, turn, first):
                pe.wait_ge(s_exp, g * CH + (c + 1))
                if c == 0:
                    pe.wait_ge(s_vl[par], turn * 16)
                    if not first:
                        pe.wait_ge(s_oc, g)
                slot = (par * CH + c) % NP_
                for h in range(GH):
                    last = pe.matmul(bank[2][32 * h:32 * h + HV, 0:S], vst[par][:, c, h * HV:(h + 1) * HV],
                                     pexp[slot][:, h, :], start=(c == 0), stop=(c == CH - 1))
                last.then_inc(s_pv, 1)

            def turn_out(g, par, first):
                pe.wait_ge(s_oc, g + 1)
                if not first:
                    pe.wait_ge(s_on, g)
                for qt in range(2):
                    last = pe.transpose(bank[3][:, 256 + qt * P:256 + (qt + 1) * P], oT[par][:, qt * P:(qt + 1) * P],
                                        ident[:, :])
                last.then_inc(s_oT, 1)

            def weigh_group(g, par, turn, first, last_group):
                pe.wait_ge(s_mrow, g * 48 + 48)
                pe.wait_ge(s_qb[par], turn * 64)
                for c in range(CH):
                    beside = first_pass_at(g, par, turn, c)
                    if not (first and c < 2):
                        pe.wait_ge(s_exp, g * CH + (c - 1))
                    for h in range(GH):
                        last = pe.matmul(pair[c % 2][:, h * S:(h + 1) * S], kst[par][:, h, c * P:(c + 1) * P],
                                         qb[par][:, h, :], start=True, stop=True)
                        if h == GH - 1:
                            last.then_inc(s_s2, 1)
                        if h == 1 and not last_group and c == MAX_STEP + 1:
                            turn_maxima(g + 1, first)
                        if h % 2 and beside:
                            first_pass(*beside.pop(0))
                    if c >= 2:
                        weigh(g, par, c - 2, turn, first)
                    elif not first:
                        weigh(g - 1, 1 - par, CH - 2 + c, None, False)
                    if c == NORM_STEP - 1 and not first:
                        turn_out(g - 1, 1 - par, isinstance(g, int) and g == 1)
                if last_group:
                    weigh(g, par, CH - 2, turn, first)
                    weigh(g, par, CH - 1, turn, first)

            for i in range(S1N):
                first_pass(0, 0, 1, i)
            turn_maxima(0, True)
            for i in range(AHEAD):
                first_pass(1, 1, 1, i)
            each_group(pe, weigh_group)
            turn_out(NG - 1, 1, False)
            pe_turn(pe, turn3o, lambda half: pe.wait_ge(s_tok3, B))
            pe_gemm(pe, gemm3, turn3o)

            def self_attention(sa, ws, w_v, nprod):
                def project(job):
                    half, n, m = SELF_JOBS[job]
                    if job >= 2:
                        sa.wait(pe, "flo", job - 1)
                    for w in range(nprod):
                        for k in range(KT):
                            last = pe.matmul(bank[4 + 2 * (job % 2) + w], ws[n * nprod + w][:, k, m * P:(m + 1) * P],
                                             xT[:, k, half * 512:(half + 1) * 512], start=(k == 0), stop=(k == KT - 1))
                    last.then_inc(signals["fproj"].s, 1)

                def values(tiles):
                    for t in tiles:
                        if t >= 2:
                            sa.wait(pe, "vtaken", t - 1)
                        for k in range(KT):
                            last = pe.matmul(bank[2 + t % 2][:, 0:D], xT[:, k, t * P:(t + 1) * P], w_v[:, k, :],
                                             start=(k == 0), stop=(k == KT - 1))
                        last.then_inc(signals["vproj"].s, 1)

                def first_pass(n):
                    hp, qt = divmod(n, 2)
                    if n % SELF_ITEMS == 0:
                        sa.wait(pe, f"qk{n // SELF_ITEMS}_loaded", 16 * SELF_LOADS)
                        sa.wait(pe, "rows_set", 3)
                    if n >= 2:
                        sa.wait(pe, "mx", n - 1)
                    for i in range(2):
                        h = 2 * hp + i
                        last = pe.matmul(bank[n % 2][:, i * S:(i + 1) * S], sa.q[:, h, qt * P:(qt + 1) * P],
                                         sa.k[:, h, :], start=True, stop=True)
                    last.then_inc(signals["s1"].s, 1)

                def turn_maxima(half):
                    sa.wait(pe, "mx", SELF_ITEMS * (half + 1))
                    pe.transpose(bank[1][0:64, 0:P], mx[:, 64 * half:64 * half + 64], ident[:, :])\
                        .then_inc(signals["mT"].s, 1)

                for job in range(len(SELF_JOBS)):
                    project(job)
                    if job == 5:
                        values(range(0, 4))
                    for i in ITEMS_AFTER.get(job, ()):
                        first_pass(i)
                turn_maxima(0)
                values(range(4, T))
                sa.wait(pe, "flo", len(SELF_JOBS))

                def weigh(n):
                    g, c = divmod(n, 2)
                    sa.wait(pe, "exp", n + 1)
                    if c == 0 and g >= 1:
                        sa.wait(pe, "oc", g)
                    if n == 0:
                        sa.wait(pe, "vtaken", T)
                    b, g4 = divmod(g, H // GH)
                    for h in range(GH):
                        last = pe.matmul(bank[2][32 * h:32 * h + HV, 0:S], sa.v[:, 2 * b + c, g4 * GH + h, :],
                                         pexp[n % NP_][:, h, :], start=(c == 0), stop=(c == 1))
                    last.then_inc(signals["pv"].s, 1)

                def turn_out(g):
                    sa.wait(pe, "oc", g + 1)
                    if g >= 1:
                        sa.wait(pe, "on", g)
                    for qt in range(2):
                        last = pe.transpose(bank[3][:, 256 + qt * P:256 + (qt + 1) * P],
                                            oT[g % 2][:, qt * P:(qt + 1) * P], ident[:, :])
                    last.then_inc(signals["oT"].s, 1)

                for n in range(2 * NG):
                    g, c = divmod(n, 2)
                    if n % NG == 0:
                        sa.wait(pe, "mrow", 48 * (n // NG + 1))
                    if n >= 2:
                        sa.wait(pe, "exp", n - 1)
                    for h in range(GH):
                        last = pe.matmul(pair[n % 2][:, h * S:(h + 1) * S], sa.k[:, g * GH + h, c * P:(c + 1) * P],
                                         sa.q[:, g * GH + h, :], start=True, stop=True)
                    last.then_inc(signals["s2"].s, 1)
                    if n == SELF_MAX_STEP:
                        turn_maxima(1)
                    for i in items_beside(n):
                        first_pass(i)
                    if n >= 1:
                        weigh(n - 1)
                    if c == 1 and g >= 1:
                        turn_out(g - 1)
                weigh(2 * NG - 1)
                turn_out(NG - 1)

            pe_turn(pe, turn4, tiles_ready(norm4b))
            turned(pe, turn4)
            pe.wait_ge(s_wb, 16 * 7)
            self_attention(sa5, [r_w[:, i] for i in range(4)], r_w[:, 4], 2)
            pe_turn(pe, turn4o, lambda half: pe.wait_ge(s_tok4, B))
            pe_gemm(pe, gemm4, turn4o)
            pe_turn(pe, turn5, tiles_ready(norm5))
            pe.wait_ge(s_wa, 16 * 4)
            job = 0
            for half in range(2):
                turned(pe, turn5, half)
                for m in range(HM):
                    if job >= 4:
                        pe.wait_ge(s_h5e, job - 3)
                    for k in range(KT):
                        last = pe.matmul(bank[4 + job % 4], r_w1[:, k, m * P:(m + 1) * P],
                                         xT[:, k, half * 512:(half + 1) * 512], start=(k == 0), stop=(k == KT - 1))
                    last.then_inc(s_h5, 1)
                    job += 1
            for t in range(T):
                pe.wait_ge(s_h5e, HM * (t // 4 + 1))
                if t >= 2:
                    pe.wait_ge(s_x, 4 * T + t - 1)
                for m in range(HM):
                    last = pe.matmul(bank[2 + t % 2][:, 0:D], hid5[:, m, t * P:(t + 1) * P], r_w2[:, m, :],
                                     start=(m == 0), stop=(m == HM - 1))
                last.then_inc(s_m2, 1)

            pe_turn(pe, turn6, tiles_ready(norm6))
            turned(pe, turn6)
            pe.wait_ge(s_wb, 16 * 8)
            self_attention(sa6, [l_w[:, 0], l_w[:, 1]], l_w[:, 2], 1)
            pe_turn(pe, turn6o, lambda half: pe.wait_ge(s_tok6, B))
            pe_gemm(pe, gemm6, turn6o)
            pe_turn(pe, turn7, lambda half: pe.wait_ge(s_y6, T))
            turned(pe, turn7)
            pe.wait_ge(s_w6, 32)
            for t in range(T):
                for k in range(KT):
                    last = pe.matmul(bank[2][:, t * ER:(t + 1) * ER], xT[:, k, t * P:(t + 1) * P], wg_l[:, k, :],
                                     start=(k == 0), stop=(k == KT - 1), skip_group_check=True)
            last.then_inc(s_log6, 1)
            pe.wait_ge(s_gate6, 1)
            for j in range(2):
                for i in range(4):
                    last = pe.transpose(bank[j][0:ER, i * P:(i + 1) * P], gate_t[:, 4 * j + i, 0:ER], ident[:, :])
                last.then_inc(s_gT, 1)
            pe.wait_ge(s_gTe, 4)
            for t in range(T):
                if t >= 2:
                    pe.wait_ge(s_b2e6, t - 1)
                pe.matmul(bank[2 + t % 2][:, 0:D], gateT[0:ER, t * P:(t + 1) * P], b2_l[:, :], start=True, stop=True)\
                    .then_inc(s_b26, 1)
            pe.wait_ge(s_wa, 16 * 5)
            n = 0
            for e in range(ER // 2):
                for t in range(T):
                    if n >= 4:
                        pe.wait_ge(s_wee, 2 * (n - 3))
                    for k in range(KT):
                        last = pe.matmul(bank[4 + n % 4], xT[:, k, t * P:(t + 1) * P],
                                         l_we[:, e, k, :], start=(k == 0), stop=(k == KT - 1))
                    last.then_inc(s_we, 1)
                    n += 1

        @block.scalar
        def _(act):

            def ctx_block_high(n):
                act.wait_ge(s_ctx[n % NBUF], 16 * (n // NBUF + 1))
                if n >= 2:
                    act.wait_ge(s_gram_blk, n - 1)
                act.activation(ctx_hi[n % 2][:, :, 0:D], ctx_sb[n % NBUF][:, :, :], ACT.Copy).then_inc(s_ghi, 1)

            ctx_block_high(0)
            ctx_block_high(1)
            act_dev(act, norm0)
            ctx_block_high(2)
            ctx_block_high(3)
            act.wait_ge(s_start, 16 * N_START)
            act_turn(act, turn0)
            for job in range(2 * W0 // P):
                half, m = divmod(job, W0 // P)
                act.wait_ge(s_q0, job + 1)
                act.activation(q0T[:, m, half * 512:(half + 1) * 512], bank[2 + job % 2], ACT.Identity,
                               bias=col("L0_xattn_Wq_b", m)).then_inc(s_q0e, 1)
            for b in range(B):
                if b + 1 < B:
                    ctx_block_high(NCB * (b + 1))
                    ctx_block_high(NCB * (b + 1) + 1)
                for hf in range(2):
                    t = 2 * b + hf
                    act.wait_ge(s_lgs, t + 1)
                    act.activation(lin[hf][:, :, :], lin[hf][:, :, :], ACT.Exp).then_inc(s_lge, 1)
                if b + 1 < B:
                    for c in range(2, NCB):
                        ctx_block_high(NCB * (b + 1) + c)
                for hf in range(2):
                    t = 2 * b + hf
                    for j in range(2):
                        n = 2 * t + j
                        act.wait_ge(s_lt, n + 1)
                        if j == 0 and t >= 1:
                            act.wait_ge(s_lo, t)
                        act.activation(linT[:, 4 * j:4 * j + 4, :].rearrange("p m q -> p (m q)"), bank[3], ACT.Copy)\
                            .then_inc(s_lte, 1)
            act_dev(act, norm1)
            act_turn(act, turn1)
            act.wait_ge(s_vones, 2)

            def ctx_high(n):
                act.wait_ge(s_cT[n % 3], 16 * (n // 3 + 1))
                if n >= 2:
                    act.wait_ge(s_vp, 2 * (n - 1))
                act.activation(c_part[n % 2][0][:, :, :], cT[n % 3][:, :, :], ACT.Copy).then_inc(s_chi, 1)

            ctx_high(0)
            for n in range(len(proj_blocks)):
                if n + 1 < len(proj_blocks):
                    ctx_high(n + 1)
                if n in EXP_BLOCKS:
                    act.wait_ge(s_at0, EXP_BLOCKS.index(n) + 1)
                    act.activation(sc0[:, :, :, :], sc0[:, :, :, :], ACT.Exp, scale=SCALE).then_inc(s_at0e, 1)
                for m in range(KT):
                    job = 2 * n + m
                    act.wait_ge(s_kp, job + 1)
                    if job >= 3:
                        act.wait_ge(s_klo, job - 2)
                    if job >= 3:
                        act.wait_ge(s_kst[job % 3], 64 * (job // 3))
                    act.activation(k_f[job % 3][:, :], bank[4 + job % 2], ACT.Identity, bias=col("bk_x", m),
                                   scale=1.0 / W_SCALE).then_inc(s_kf, 1)
                    act.activation(k_hi[job % 3][:, :], bank[4 + job % 2], ACT.Identity, bias=col("bk_x", m),
                                   scale=1.0 / W_SCALE).then_inc(s_kf, 1)
                for job in (2 * n, 2 * n + 1):
                    vb, cc = divmod(2 * job, VC)
                    act.wait_ge(s_vp, job + 1)
                    if cc == 0 and vb >= 2:
                        act.wait_ge(s_vst[vb % 2], 64 * (vb // 2))
                    dst = v_st[vb % 2][:, :, cc:cc + 2, :].rearrange("p g c (h d) -> p g (c h) d", d=HV)[:, :, :, 0:HD]
                    src = bank[6 + job % 2].rearrange("p (g c d) -> p g c d", g=H // GH, d=HD)
                    act.activation(dst, src, ACT.Copy, scale=1.0 / W_SCALE).then_inc(s_ve, 1)
            act_turn(act, turn1o)
            act_dev(act, norm2)
            context_stored(act)
            for t in range(T):
                norm2.wait(act, t + 1)
                if t:
                    act.wait_ge(s_sq, t)
                act.activation(junk3[:, :], u[:, t, :], ACT.Square, accum_out=var_eps[:, t:t + 1]).then_inc(s_sq, 1)
            act_dev(act, rms)
            act_turn(act, turn2)

            def weights_high(n, par):
                act.wait_ge(s_wexp, n * 48 + 48)
                if not (isinstance(n, int) and n < 2):
                    act.wait_ge(s_w2, (n - 1) * T)
                for i in range(WPIECES):
                    act.activation(w_part[0][par][:, i, :], w_f[:, i, :], ACT.Copy, scale=W_SCALE).then_inc(s_whi, 1)

            def turn_gates():
                for j in range(2):
                    act.wait_ge(s_gT, j + 1)
                    act.activation(gateT[:, j * 512:(j + 1) * 512], bank[j][0:ER + ES, :], ACT.Copy).then_inc(s_gTe, 1)

            def expert(n, par, first=False, last=False, between=None):
                for job in range(2 * HM):
                    act.wait_ge(s_w1, n * 2 * HM + job + 1)
                    if not (first and job < 4):
                        act.wait_ge(s_hlo, n * 2 * HM + job - 3)
                    act.activation(hid_f[:, job % 4, :], bank[job % 4], ACT.Gelu, bias=b_1[par][:, job % HM:job % HM + 1],
                                   scale=1.0 / W_SCALE).then_inc(s_gelu, 1)
                if between:
                    between()
                if not last:
                    weights_high(n + 1, 1 - par)

            weights_high(0, 0)
            act.wait_ge(s_logs, 1)
            act.activation(logit[:, :, :], logit[:, :, :], ACT.Exp, scale=-1.0).then_inc(s_loge, 1)
            act.wait_ge(s_log, 1)
            expert(0, 0, first=True)
            expert(1, 1, between=turn_gates)
            with act.Fori(0, (ER - 2) // 2) as i:
                for par in range(2):
                    expert(2 * i + (2 + par), par)
            for par in range(2):
                expert(ER + par, par, last=par == 1)
            act_dev(act, norm3)
            act_turn(act, turn3)
            for m in range(KT):
                for half in range(2):
                    job = 2 * m + half
                    act.wait_ge(s_qx, job + 1)
                    act.activation(q_hi[:, m, half * 512:(half + 1) * 512], bank[2 + job % 2], ACT.Identity,
                                   bias=col("L1_xattn_bq", m)).then_inc(s_qxh, 1)

            def copy_out(g, par):
                act.wait_ge(s_pv, g * CH + CH)
                act.activation(oT[par][:, :], bank[2][:, 0:S], ACT.Copy).then_inc(s_oc, 1)

            def exp_group(g, par, turn, first, last):
                for c in range(CH):
                    if c == COPY_STEP and not first:
                        copy_out(g - 1, 1 - par)
                    act.wait_ge(s_s2, g * CH + (c + 1))
                    if not (first and c < NP_):
                        act.wait_ge(s_pv, g * CH + (c - NP_ + 1))
                    slot = (par * CH + c) % NP_
                    act.activation(pexp[slot][:, :, :].rearrange("p h q -> p (h q)"), pair[c % 2][:, :], ACT.Exp,
                                   scale=SCALE).then_inc(s_exp, 1)

            each_group(act, exp_group)
            copy_out(NG - 1, 1)
            act_turn(act, turn3o)

            def self_exp(sa):
                for n in range(2 * NG):
                    sa.wait(act, "s2", n + 1)
                    if n >= NP_:
                        sa.wait(act, "pv", n - NP_ + 1)
                    act.activation(pexp[n % NP_][:, :, :].rearrange("p h q -> p (h q)"), pair[n % 2][:, :], ACT.Exp,
                                   scale=SCALE).then_inc(signals["exp"].s, 1)

            act_dev(act, norm4a)
            act_dev(act, norm4b)
            act_turn(act, turn4)
            self_exp(sa5)
            act_turn(act, turn4o)
            act_dev(act, norm5)
            act_turn(act, turn5)
            for job in range(2 * HM):
                half, m = divmod(job, HM)
                act.wait_ge(s_h5, job + 1)
                act.activation(hid5[:, m, half * 512:(half + 1) * 512], bank[4 + job % 4], ACT.Relu,
                               bias=col("L1_attn_b1", m)).then_inc(s_h5e, 1)
            act_dev(act, norm6)
            act_turn(act, turn6)
            for job, (half, n, m) in enumerate(SELF_JOBS):
                sa6.wait(act, "fproj", job + 1)
                if job == 4:
                    sa6.wait(act, "fst", 64)
                act.activation(sa6.hi[:, m, n * 512:(n + 1) * 512], bank[4 + 2 * (job % 2)], ACT.Identity,
                               bias=col(("L1_ffn_bq", "L1_ffn_bk")[n], m)).then_inc(signals["fhi"].s, 1)
            self_exp(sa6)
            act_turn(act, turn6o)
            act_dev(act, norm6a)
            act_turn(act, turn7)
            act.wait_ge(s_logs6, 1)
            act.activation(logit[:, :, :], logit[:, :, :], ACT.Exp).then_inc(s_loge6, 1)
            for j in range(2):
                act.wait_ge(s_gT, 2 + j + 1)
                act.activation(gateT[0:ER, j * 512:(j + 1) * 512], bank[j][0:ER, :], ACT.Copy).then_inc(s_gTe, 1)
            act_dev(act, norm6m)

        @block.vector
        def _(dve):
            st = Steps(dve, s_dve)
            for i in range(2):
                dve.memset(ctx_hi[i][:, :, D:D + 1], 1.0).then_inc(s_ones, 1)
            st.link(dve.memset(kv0[:, :, :], 0.0))
            dve.wait_ge(s_tokens, 16)
            dve_norm(dve, st, norm0, x, u)

            def bcast(ap, n):
                return ap.to_broadcast(list(ap.shape[:-1]) + [n])

            def per_tile_rows(name, n=T):
                at = ROW_AT[name][0]
                return rows[:, at:at + D].rearrange("p (o d) -> p o d", o=1).to_broadcast([P, n, D])

            for b in range(B):
                dve.wait_ge(s_gram_blk, NCB * (b + 1))
                if b >= 1:
                    dve.wait_ge(s_gw, 6 * b)
                for m in range(KT):
                    dve.tensor_copy(gram[:, m, :], bank[m][:, 0:D + 1]).then_inc(s_grame, 1)
                dve.wait_ge(s_grame, 2 * (b + 1))
                if b == 0:
                    dve.wait_ge(s_start, 16 * N_START)
                    st.link(dve.tensor_tensor(x[:, :, :], x[:, :, :], per_tile_rows("L0_xattn_out_b"), ALU.add))
                    st.settle()
                if b >= 1:
                    for hf in range(2):
                        t = 2 * (b - 1) + hf
                        dve.wait_ge(s_lo, t + 1)
                        dve.tensor_tensor(x[:, t, :], x[:, t, :], bank[2][:, 0:D], ALU.add).then_inc(s_x, 1)
                n = 6 * b
                if b >= 1:
                    dve.wait_ge(s_kv0, 2 * b)
                for m in range(KT + 1):
                    for h in range(2):
                        hc = slice(h * 512, (h + 1) * 512)
                        dve.wait_ge(s_gw, n + 1)
                        if m < KT:
                            ins = dve.scalar_tensor_tensor(out=gw[:, m, hc], in0=row0[:, h * 512:(h + 1) * 512],
                                                           scalar=gram[:, m, D:D + 1], in1=bank[2 + n % 2],
                                                           op0=ALU.mult, op1=ALU.add)
                        else:
                            ins = dve.scalar_tensor_tensor(out=gw_row[:, hc],
                                                           in0=row0[0:1, h * 512:(h + 1) * 512],
                                                           scalar=float(S2), in1=bank[2 + n % 2][0:1, :],
                                                           op0=ALU.mult, op1=ALU.add)
                        ins.then_inc(s_gwe, 1)
                        n += 1
                if b == 0:
                    st.settle()
                if b >= 1:
                    dve.wait_ge(s_lg, 2 * b)
                for j in range(2):
                    dve.wait_ge(s_kv0, 2 * b + j + 1)
                    for i in range(2):
                        r = slice(64 * i, 64 * i + 64)
                        src = bank[2 + j][r, :].rearrange("p (m c) -> p m c", c=P)[:, :, r]
                        dve.tensor_scalar(kv0[r, 4 * j:4 * j + 4, r], src, float(DH0) ** -0.5, None, ALU.mult)\
                            .then_inc(s_kv0e, 1)
                for hf in range(2):
                    t = 2 * b + hf
                    dve.wait_ge(s_lg, t + 1)
                    lg = pair[hf][:, :].rearrange("p (h d) -> p h d", d=DH0)
                    st.link(dve.tensor_reduce(lin_max[:, hf, :], lg, X_AXIS, ALU.max))
                    st.settle()
                    if b >= 1:
                        dve.wait_ge(s_lt, 2 * t - 2)
                    dve.tensor_tensor(lin[hf][:, :, :], lg, bcast(lin_max[:, hf, :].rearrange("p (h o) -> p h o", o=1), DH0),
                                      ALU.subtract).then_inc(s_lgs, 1)
                for hf in range(2):
                    t = 2 * b + hf
                    dve.wait_ge(s_lge, t + 1)
                    st.link(dve.tensor_reduce(lin_sum[:, hf, :], lin[hf][:, :, :], X_AXIS, ALU.add))
                    st.settle()
                    st.link(dve.reciprocal(lin_sum[:, hf, :], lin_sum[:, hf, :]))
                    st.settle()
                    dve.tensor_tensor(lin[hf][:, :, :], lin[hf][:, :, :],
                                      bcast(lin_sum[:, hf, :].rearrange("p (h o) -> p h o", o=1), DH0), ALU.mult)\
                        .then_inc(s_lgn, 1)
            dve.wait_ge(s_x, T - 2)
            for t in range(T - 2):
                tile_stats(dve, st, x, t)
            for t in (T - 2, T - 1):
                dve.wait_ge(s_lo, t + 1)
                dve.tensor_tensor(x[:, t, :], x[:, t, :], bank[2][:, 0:D], ALU.add).then_inc(s_x, 1)
            dve.wait_ge(s_x, T)
            for t in (T - 2, T - 1):
                tile_stats(dve, st, x, t)

            dve.wait_ge(s_x, T)

            dve_norm(dve, st, norm1, x, u, measured=True)
            dve.wait_ge(s_wkv, 48)
            dve.tensor_scalar(wkv_part[0][:, :, :], wkv[:, :, :], W_SCALE, None, ALU.mult).then_inc(s_wkvp, 1)
            dve.wait_ge(s_wkvp, 1)
            dve.scalar_tensor_tensor(out=wkv_part[1][:, :, :], in0=wkv[:, :, :], scalar=W_SCALE,
                                     in1=wkv_part[0][:, :, :], op0=ALU.mult, op1=ALU.subtract).then_inc(s_wkvp, 1)
            dve.wait_ge(s_posT, 1)
            for m in range(KT):
                st.link(dve.tensor_scalar(posT[:, m, :], bank[4 + m][:, 0:R0], col("L0_attn_pos_proj_bias", m), None, ALU.add))
                st.link(dve.tensor_tensor(bqrr[:, m:m + 1], col("bq0", m), col("L0_attn_r_r_bias", m), ALU.add))
            st.settle()
            for m in range(KT):
                st.link(dve.tensor_tensor(pos_blk[:, m], bcast(posT[:, m, :].rearrange("p (j o) -> p j o", o=1), H),
                                          b_mask[:, m, :].rearrange("p (o h) -> p o h", o=1).to_broadcast([P, R0, H]), ALU.mult))
                st.link(dve.tensor_copy(bqrr_rep[:, m, :], bcast(bqrr[:, m:m + 1], P)))
            dve.wait_ge(s_rin, 16)
            st.settle()
            dve.tensor_tensor(row_in[:, 0:D], row_in[:, 0:D], row("L0_attn_r_w_bias"), ALU.add).then_inc(s_posb, 1)
            dve.wait_ge(s_relw, 1)
            for m in range(KT):
                dve.tensor_copy(rel_w[:, m, :], bank[4 + m][:, 0:R0 * H]).then_inc(s_relwe, 1)
            dve.tensor_copy(rel_bias[:, :], bank[6][:, 0:R0 * H]).then_inc(s_relwe, 1)
            dve.wait_ge(s_relwe, 3)
            dve.wait_ge(s_posb, 1)
            for t in range(T):
                dve.wait_ge(s_qkv, t + 1)
                dve.tensor_tensor(qkv[:, t, 0:512], bank[2], row_in[:, 0:512], ALU.add).then_inc(s_qkve, 1)
                dve.tensor_tensor(qkv[:, t, 512:768], bank[3][:, 0:256], row_in[:, 512:768], ALU.add).then_inc(s_qkve, 1)
                dve.tensor_tensor(rel[:, t, :], bank[7][:, 0:R0 * H], rel_bias[:, :], ALU.add).then_inc(s_qkve, 1)
            dve.wait_ge(s_qkve, 3 * T)
            for hf in range(2):
                for t in range(B):
                    tile = 2 * t + hf
                    q_b = qkv[:, tile, 0:D].rearrange("p (o d) -> p o d", o=1).to_broadcast([P, B, D])
                    k_all = qkv[:, hf:T:2, D:2 * D]
                    st.link(dve.tensor_tensor(prod[t % 2][:, :, :], q_b, k_all, ALU.mult))
                    st.settle()
                    st.link(dve.tensor_reduce(sc0[:, t].rearrange("p s h -> p (s h)"),
                                              prod[t % 2][:, :, :].rearrange("p s (h d) -> p (s h) d", d=HD), X_AXIS, ALU.add))
                    st.settle()
                    lo = (B - 1 - t) * H
                    st.link(dve.tensor_tensor(sc0[:, t].rearrange("p s h -> p (s h)"), sc0[:, t].rearrange("p s h -> p (s h)"),
                                              rel[:, tile, lo:lo + B * H], ALU.add))
                st.settle()
                by_key = sc0[:, :, :, :].rearrange("p t s h -> p t h s")
                st.link(dve.tensor_reduce(sc0_max[:, :, :], by_key, X_AXIS, ALU.max))
                st.settle()
                max_b = sc0_max[:, :, :].rearrange("p t (o h) -> p t o h", o=1).to_broadcast([P, B, B, H])
                dve.tensor_tensor(sc0[:, :, :, :], sc0[:, :, :, :], max_b, ALU.subtract).then_inc(s_at0, 1)
                dve.wait_ge(s_at0e, hf + 1)
                st.link(dve.tensor_reduce(sc0_max[:, :, :], by_key, X_AXIS, ALU.add))
                st.settle()
                st.link(dve.reciprocal(sc0_max[:, :, :], sc0_max[:, :, :]))
                st.settle()
                st.link(dve.tensor_tensor(sc0[:, :, :, :], sc0[:, :, :, :], max_b, ALU.mult))
                st.settle()
                for t in range(B):
                    tile = 2 * t + hf
                    w_b = bcast(sc0[:, t].rearrange("p s (h o) -> p s h o", o=1), HD)
                    v_all = qkv[:, hf:T:2, 2 * D:3 * D].rearrange("p s (h d) -> p s h d", d=HD)
                    st.link(dve.tensor_tensor(prod[t % 2][:, :, :].rearrange("p s (h d) -> p s h d", d=HD), v_all, w_b, ALU.mult))
                    st.settle()
                    dve.tensor_reduce(tok[:, tile, :], prod[t % 2][:, :, :].rearrange("p s f -> p f s"), X_AXIS, ALU.add)\
                        .then_inc(s_tok1, 1)
            dve.wait_ge(s_tok1, T)

            def each_tile(add, s_added, base, src):
                for t in range(T):
                    add(t)
                    if t:
                        dve.wait_ge(s_added, base + t)
                        tile_stats(dve, st, src, t - 1)
                dve.wait_ge(s_added, base + T)
                tile_stats(dve, st, src, T - 1)

            def add_out(g, dst, src):
                def add(t):
                    dve.wait_ge(g.mm, t + 1)
                    dve.tensor_tensor(dst[:, t, :], src[:, t, :], gemm_out(g, t), ALU.add).then_inc(g.ev, 1)

                each_tile(add, g.ev, g.base, dst)

            st.link(dve.tensor_tensor(x[:, :, :], x[:, :, :], per_tile_rows("L0_attn_out_proj_bias"), ALU.add))
            st.settle()
            add_out(gemm1, x, x)
            st.link(dve.memset(score[:, :, ER:2 * ER], SENTINEL))
            dve.wait_ge(s_x, 2 * T)

            dve_norm(dve, st, norm2, x, u, measured=True)
            dve.wait_ge(s_sq, T)
            st.link(dve.tensor_scalar(var_eps[:, :], var_eps[:, :], 1.0 / D, RMS_EPS, ALU.mult, ALU.add))
            st.settle()
            dve.tensor_copy(esum[:, :], var_eps[:, :]).then_inc(s_var, 1)
            dve_rstd(dve, st, rms)
            for t in range(T):
                dve.tensor_scalar(tok[:, t, :], u[:, t, :], rstd[:, t:t + 1], None, ALU.mult).then_inc(s_un, 1)
            def top_two():
                for t in range(T):
                    st.link(dve.max(top8[:, t, :], score[:, t, 0:ER]))
                st.settle()
                st.link(dve.memset(top8[:, :, 2:8], SENTINEL))
                st.settle()
                for t in range(T):
                    st.link(dve.match_replace(rest[:, t, :], top8[:, t, :], score[:, t, :], 0.0))
                st.settle()

            context_stored(dve)
            st.link(dve.tensor_tensor(rinv[:, :], rstd[:, :], var_eps[:, :], ALU.mult))
            st.settle()

            def weights_low(n, par, i):
                dve.wait_ge(s_whi, n * WPIECES + i + 1)
                dve.scalar_tensor_tensor(out=w_part[1][par][:, i, :], in0=w_f[:, i, :], scalar=W_SCALE,
                                         in1=w_part[0][par][:, i, :], op0=ALU.mult, op1=ALU.subtract).then_inc(s_wlo, 1)

            def router_gates():
                dve.wait_ge(s_loge, 1)
                st.link(dve.tensor_scalar(logit[:, :, :], logit[:, :, :], 1.0, None, ALU.add))
                st.settle()
                st.link(dve.reciprocal(score[:, :, 0:ER], logit[:, :, :]))
                st.settle()
                st.link(dve.tensor_reduce(esum[:, :], score[:, :, 0:ER], X_AXIS, ALU.add))
                st.settle()
                st.link(dve.reciprocal(esum[:, :], esum[:, :]))
                st.settle()
                top_two()
                st.link(dve.tensor_tensor(gate[:, :, :].rearrange("p e t -> p t e"), score[:, :, 0:ER], rest[:, :, 0:ER],
                                          ALU.subtract))
                st.settle()
                st.link(dve.tensor_tensor(gate[:, :, :], gate[:, :, :],
                                          esum[:, :].rearrange("p (o t) -> p o t", o=1).to_broadcast([P, ER, T]), ALU.mult))
                st.link(dve.memset(gate_t[:, :, ER:ER + ES], 1.0))
                st.settle()
                dve.tensor_copy(gate_t[:, :, 0:ER], gate[:, :, :].rearrange("p e t -> p t e")).then_inc(s_gate, 1)

            def expert(n, par, take, last=False, between=None):
                for job in range(2 * HM):
                    half, m = divmod(job, HM)
                    hc = slice(half * 512, (half + 1) * 512)
                    dve.wait_ge(s_gelu, n * 2 * HM + job + 1)
                    if m == 0 and not (isinstance(n, int) and n == 0):
                        dve.wait_ge(s_w2, (n - 1) * T + 4 * (half + 1))
                    dve.tensor_copy(hid_part[0][:, m, hc], hid_f[:, job % 4, :]).then_inc(s_hhi, 1)
                    dve.wait_ge(s_hhi, n * 2 * HM + job + 1)
                    dve.tensor_tensor(hid_part[1][:, m, hc], hid_f[:, job % 4, :], hid_part[0][:, m, hc], ALU.subtract)\
                        .then_inc(s_hlo, 1)
                if between:
                    between()
                for t in range(T):
                    if not last:
                        if t == 0 and not (isinstance(n, int) and n == 0):
                            dve.wait_ge(s_w2, n * T)
                        weights_low(n + 1, 1 - par, t)
                    dve.wait_ge(s_w2, n * T + t + 1)
                    if not (isinstance(n, int) and n == 0):
                        dve.wait_ge(s_acc, (n - 1) * T + t + 1)
                    take(n, par, t)

            def take_shared(n, par, t):
                src = u if n == 0 else tok
                dve.scalar_tensor_tensor(out=tok[:, t, :], in0=bank[4 + t % 4][:, 0:D], scalar=1.0 / W_SCALE,
                                         in1=src[:, t, :], op0=ALU.mult, op1=ALU.add).then_inc(s_acc, 1)

            def take_routed(n, par, t):
                dve.scalar_tensor_tensor(out=tok[:, t, :], in0=bank[4 + t % 4][:, 0:D], scalar=g_now[par][:, t:t + 1],
                                         in1=tok[:, t, :], op0=ALU.mult, op1=ALU.add).then_inc(s_acc, 1)

            for i in range(WPIECES):
                weights_low(0, 0, i)
            for half in range(2):
                turned(dve, turn2, half)
            for src, parts in ((xTs, x_part[0]), (xT, x_part[1])):
                for k in range(KT):
                    st.link(dve.tensor_copy(parts[0][:, k, :], src[:, k, :]))
                st.settle()
                for k in range(KT):
                    dve.tensor_tensor(parts[1][:, k, :], src[:, k, :], parts[0][:, k, :], ALU.subtract).then_inc(s_xlo, 1)
            dve.wait_ge(s_log, 1)
            dve.tensor_tensor(logit[:, :, :], bank[4][:, 0:T * ER].rearrange("p (t e) -> p t e", e=ER),
                              bcast(rinv[:, :].rearrange("p (t o) -> p t o", o=1), ER), ALU.mult).then_inc(s_logs, 1)
            expert(0, 0, take_shared, between=router_gates)
            expert(1, 1, take_shared)
            for t in range(T):
                dve.wait_ge(s_b2, t + 1)
                dve.wait_ge(s_acc, T + t + 1)
                dve.tensor_tensor(tok[:, t, :], tok[:, t, :], bank[2 + t % 2][:, 0:D], ALU.add).then_inc(s_b2e, 1)
            dve.wait_ge(s_b2e, T)
            st.settle()
            base = st.n

            def gates_of(e, par, steps):
                dve.tensor_scalar(g_now[par][:, :], gate[:, bass.ds(e, 1), :].rearrange("p o t -> p (o t)"),
                                  1.0 / W_SCALE, None, ALU.mult).then_inc(s_dve, 1)
                dve.wait_ge(s_dve, steps)

            with dve.Fori(0, (ER - 2) // 2) as i:
                for par in range(2):
                    gates_of(2 * i + par, par, 2 * i + (base + par + 1))
                    expert(2 * i + (2 + par), par, take_routed)
            for par in range(2):
                gates_of(ER - 2 + par, par, base + ER - 1 + par)
                expert(ER + par, par, take_routed, last=par == 1)
            st.n = base + ER
            dve.wait_ge(s_acc, (ER + ES) * T)
            each_tile(lambda t: dve.tensor_tensor(x[:, t, :], x[:, t, :], tok[:, t, :], ALU.add).then_inc(s_x, 1),
                      s_x, 2 * T, x)
            dve.wait_ge(s_x, 3 * T)

            dve_norm(dve, st, norm3, x, u, measured=True)
            for m in range(KT):
                for half in range(2):
                    job = 2 * m + half
                    dve.wait_ge(s_qxh, job + 1)
                    dve.scalar_tensor_tensor(out=q_lo[:, m, half * 512:(half + 1) * 512], in0=bank[2 + job % 2],
                                             scalar=col("L1_xattn_bq", m), in1=q_hi[:, m, half * 512:(half + 1) * 512],
                                             op0=ALU.add, op1=ALU.subtract).then_inc(s_qxl, 1)
            def group_max(g, i):
                dve.wait_ge(s_s1, g * S1N + (i + 1))
                if i == 0 and not (isinstance(g, int) and g == 0):
                    dve.wait_ge(s_mxa, g)
                h, qt, kb = product_of(i)
                at = (2 * h + qt) * 8 + kb
                dve.tensor_reduce(mx_part[:, at:at + 1], bank[i % 2], X_AXIS, ALU.max).then_inc(s_mx, 1)

            def split_max(st, src, rws, s_out):
                st.link(dve.tensor_scalar(m_neg[rws, :], src, -1.0, None, ALU.mult))
                st.settle()
                st.link(dve.tensor_copy(m_prt[rws, 0, :], m_neg[rws, :]))
                st.settle()
                st.link(dve.tensor_tensor(m_res[rws, :], m_neg[rws, :], m_prt[rws, 0, :], ALU.subtract))
                st.settle()
                st.link(dve.tensor_copy(m_prt[rws, 1, :], m_res[rws, :]))
                st.settle()
                dve.tensor_tensor(m_prt[rws, 2, :], m_res[rws, :], m_prt[rws, 1, :], ALU.subtract).then_inc(s_out, 1)

            def group_maxima(g):
                dve.wait_ge(s_mx, g * S1N + S1N)
                dve.tensor_reduce(mx[:, 0:2 * GH], mx_part[:, :].rearrange("p (j k) -> p j k", k=8), X_AXIS, ALU.max)\
                    .then_inc(s_mxa, 1)

            def group_parts(st, g, first):
                dve.wait_ge(s_mT, g + 1)
                if not first:
                    dve.wait_ge(s_mrow, g * 48)
                split_max(st, bank[3][0:2 * GH, 0:P], slice(0, 2 * GH), s_mp)

            def normalise(st, g, s_out):
                o = bank[3][:, 256:512].rearrange("p (q h d) -> p q h d", q=2, h=GH)
                st.link(dve.reciprocal(den[:, :, :], o[:, :, :, HD]))
                st.settle()
                dst = o_grp[:, g] if isinstance(g, int) else o_grp[:, bass.ds(g, 1)].rearrange("p o q h d -> p (o q) h d")
                dve.tensor_tensor(dst, o[:, :, :, 0:HD], bcast(den[:, :, :].rearrange("p q (h o) -> p q h o", o=1), HD),
                                  ALU.mult).then_inc(s_out, 1)

            def gather(s_out, bias):
                for b in range(B):
                    src = o_grp[:, 4 * b:4 * b + 4].rearrange("p g q h d -> p q g (h d)")
                    bias_b = row(bias).rearrange("p (o g c) -> p o g c", o=1, c=GH * HD).to_broadcast([P, 2, 4, GH * HD])
                    dst = tok[:, 2 * b:2 * b + 2, :].rearrange("p q (g c) -> p q g c", c=GH * HD)
                    dve.tensor_tensor(dst, src, bias_b, ALU.add).then_inc(s_out, 1)

            for i in range(S1N):
                group_max(0, i)
            group_maxima(0)
            group_parts(st, 0, True)
            for i in range(AHEAD):
                group_max(1, i)
            grp = Steps(dve, s_grp)
            STEPS = 5

            def group_vector(g, par, turn, first, last):
                grp.base, grp.n = g * STEPS, 0
                for c in range(CH):
                    if c == NORM_STEP and first:
                        grp.link(dve.memset(den[:, :, :], 1.0))
                    elif c == NORM_STEP:
                        dve.wait_ge(s_oT, g)
                        normalise(grp, g - 1, s_on)
                    beside = first_pass_at(g, par, turn, c)
                    for n, (other, _, _, i) in enumerate(beside):
                        group_max(other, i)
                        if i == S1N - 1:
                            group_maxima(other)
                        if c == MAX_STEP + 1 and n == 0:
                            group_parts(grp, g + 1, False)
                    if not last and not beside and c == MAX_STEP + 1:
                        group_parts(grp, g + 1, False)
                assert last or grp.n == STEPS

            each_group(dve, group_vector)
            dve.wait_ge(s_oT, NG)
            normalise(st, NG - 1, s_on)
            dve.wait_ge(s_on, NG)
            gather(s_tok3, "bv_x")
            dve.wait_ge(s_tok3, B)
            st.link(dve.tensor_tensor(x[:, :, :], x[:, :, :], per_tile_rows("L1_xattn_bo"), ALU.add))
            st.settle()
            add_out(gemm3, x, x)
            dve.wait_ge(s_x, 4 * T)

            def self_attention(sa, take_projection):
                def take_values(tiles):
                    for t in tiles:
                        sa.wait(dve, "vproj", t + 1)
                        dve.tensor_copy(sa.v[:, t, :, 0:HD], bank[2 + t % 2][:, 0:D].rearrange("p (h d) -> p h d", d=HD))\
                            .then_inc(signals["vtaken"].s, 1)

                def maxima(n):
                    hp, qt = divmod(n, 2)
                    sa.wait(dve, "s1", n + 1)
                    dst = mx[:, 4 * hp + qt:4 * hp + qt + 3:2]
                    dve.tensor_reduce(dst, bank[n % 2].rearrange("p (i k) -> p i k", i=2), X_AXIS, ALU.max)\
                        .then_inc(signals["mx"].s, 1)

                def parts(half):
                    sa.wait(dve, "mT", half + 1)
                    if half:
                        sa.wait(dve, "mrow", 48)
                    split_max(st, bank[1][0:64, 0:P], slice(0, 64), signals["mp"].s)

                def copy_out(g):
                    sa.wait(dve, "pv", 2 * (g + 1))
                    dve.tensor_copy(oT[g % 2][:, :], bank[2][:, 0:S]).then_inc(signals["oc"].s, 1)
                    if g >= 1:
                        sa.wait(dve, "oT", g)
                        normalise(st, g - 1, signals["on"].s)

                for job in range(len(SELF_JOBS)):
                    take_projection(job)
                    if job == 5:
                        take_values(range(0, 4))
                    for i in ITEMS_AFTER.get(job, ()):
                        maxima(i)
                parts(0)
                take_values(range(4, T))
                for n in range(2 * NG):
                    if n == SELF_MAX_STEP:
                        parts(1)
                    for i in items_beside(n):
                        maxima(i)
                    if n % 2 == 0 and n:
                        copy_out(n // 2 - 1)
                copy_out(NG - 1)
                sa.wait(dve, "oT", NG)
                normalise(st, NG - 1, signals["on"].s)
                sa.wait(dve, "on", NG)

            dve_norm(dve, st, norm4a, x, u, measured=True)
            dve_norm(dve, st, norm4b, u, tok)
            dve.wait_ge(s_rope, 32)

            def rotate(job):
                half, n, m = SELF_JOBS[job]
                i = job % 2
                sa5.wait(dve, "fproj", job + 1)
                if job >= 1:
                    sa5.wait(dve, "flo", job)
                if job == 4:
                    sa5.wait(dve, "fst", 64)
                tb = lambda ap: ap[:, :].rearrange("p (o q) -> p o q", o=1).to_broadcast([P, 2, S])
                v2 = lambda ap: ap.rearrange("p (b q) -> p b q", b=2)
                st.link(dve.scalar_tensor_tensor(out=v2(rot_a[i][:, :]), in0=v2(bank[4 + 2 * i]),
                                                 scalar=col(("L1_attn_bq", "L1_attn_bk")[n], m),
                                                 in1=tb(cosT), op0=ALU.add, op1=ALU.mult))
                st.link(dve.scalar_tensor_tensor(out=v2(rot_b[i][:, :]), in0=v2(bank[5 + 2 * i]),
                                                 scalar=col(("bq_swapped", "bk_swapped")[n], m),
                                                 in1=tb(sinT), op0=ALU.add, op1=ALU.mult))
                st.settle()
                st.link(dve.tensor_tensor(rot_a[i][:, :], rot_a[i][:, :], rot_b[i][:, :], ALU.add))
                st.settle()
                nc_ = slice(n * 512, (n + 1) * 512)
                st.link(dve.tensor_copy(sa5.hi[:, m, nc_], rot_a[i][:, :]))
                st.settle()
                dve.tensor_tensor(sa5.lo[:, m, nc_], rot_a[i][:, :], sa5.hi[:, m, nc_], ALU.subtract)\
                    .then_inc(signals["flo"].s, 1)

            self_attention(sa5, rotate)
            gather(s_tok4, "L1_attn_bv")
            dve.wait_ge(s_tok4, B)
            st.link(dve.tensor_tensor(u[:, :, :], u[:, :, :], per_tile_rows("L1_attn_bo"), ALU.add))
            st.settle()
            add_out(gemm4, u, u)
            dve.wait_ge(gemm4.ev, T)
            dve_norm(dve, st, norm5, u, tok, measured=True)
            st.link(dve.tensor_tensor(x[:, :, :], x[:, :, :], u[:, :, :], ALU.add))
            st.settle()
            st.link(dve.tensor_tensor(x[:, :, :], x[:, :, :], per_tile_rows("L1_attn_b2"), ALU.add))
            st.settle()
            def add_mlp(t):
                dve.wait_ge(s_m2, t + 1)
                dve.tensor_tensor(x[:, t, :], x[:, t, :], bank[2 + t % 2][:, 0:D], ALU.add).then_inc(s_x, 1)

            each_tile(add_mlp, s_x, 4 * T, x)
            dve.wait_ge(s_x, 5 * T)

            dve_norm(dve, st, norm6, x, u, measured=True)

            def low_part(job):
                half, n, m = SELF_JOBS[job]
                nc_ = slice(n * 512, (n + 1) * 512)
                sa6.wait(dve, "fhi", job + 1)
                dve.scalar_tensor_tensor(out=sa6.lo[:, m, nc_], in0=bank[4 + 2 * (job % 2)],
                                         scalar=col(("L1_ffn_bq", "L1_ffn_bk")[n], m),
                                         in1=sa6.hi[:, m, nc_], op0=ALU.add, op1=ALU.subtract).then_inc(signals["flo"].s, 1)

            self_attention(sa6, low_part)
            gather(s_tok6, "L1_ffn_bv")
            def add_bias(t):
                dve.wait_ge(gemm6.mm, t + 1)
                dve.tensor_tensor(tok[:, t, :], gemm_out(gemm6, t), row("L1_ffn_bo"), ALU.add).then_inc(gemm6.ev, 1)

            each_tile(add_bias, gemm6.ev, 0, tok)
            dve_norm(dve, st, norm6a, tok, tok, measured=True)
            st.link(dve.tensor_tensor(tok[:, :, :], tok[:, :, :], per_tile_rows("L1_ffn_g1"), ALU.mult))
            st.settle()
            st.link(dve.tensor_tensor(tok[:, :, :], tok[:, :, :], per_tile_rows("L1_ffn_be1"), ALU.add))
            st.settle()
            for t in range(T):
                dve.tensor_tensor(u[:, t, :], u[:, t, :], tok[:, t, :], ALU.add).then_inc(s_y6, 1)
            dve.wait_ge(s_y6, T)
            st.link(dve.tensor_tensor(x[:, :, :], x[:, :, :], u[:, :, :], ALU.add))
            st.settle()
            st.link(dve.tensor_tensor(x[:, :, :], x[:, :, :], per_tile_rows("L1_ffn_be2"), ALU.add))
            st.settle()
            dve.wait_ge(s_log6, 1)
            st.link(dve.tensor_tensor(logit[:, :, :], bank[2][:, 0:T * ER].rearrange("p (t e) -> p t e", e=ER),
                                      row("L1_ffn_bg").rearrange("p (o e) -> p o e", o=1).to_broadcast([P, T, ER]), ALU.add))
            st.settle()
            st.link(dve.tensor_reduce(esum[:, :], logit[:, :, :], X_AXIS, ALU.max))
            st.settle()
            esum_b = bcast(esum[:, :].rearrange("p (t o) -> p t o", o=1), ER)
            dve.tensor_tensor(logit[:, :, :], logit[:, :, :], esum_b, ALU.subtract).then_inc(s_logs6, 1)
            dve.wait_ge(s_loge6, 1)
            st.link(dve.tensor_reduce(esum[:, :], logit[:, :, :], X_AXIS, ALU.add))
            st.settle()
            st.link(dve.reciprocal(esum[:, :], esum[:, :]))
            st.settle()
            st.link(dve.tensor_tensor(score[:, :, 0:ER], logit[:, :, :], esum_b, ALU.mult))
            st.settle()
            top_two()
            dve.tensor_tensor(gate_t[:, :, 0:ER], score[:, :, 0:ER], rest[:, :, 0:ER], ALU.subtract).then_inc(s_gate6, 1)
            for t in range(T):
                dve.wait_ge(s_b26, t + 1)
                dve.tensor_copy(tok[:, t, :], bank[2 + t % 2][:, 0:D]).then_inc(s_b2e6, 1)
            dve.wait_ge(s_b2e6, T)
            dve.wait_ge(s_gate6, 1)
            n = 0
            for e in range(ER // 2):
                for t in range(T):
                    dve.wait_ge(s_we, n + 1)
                    for j in range(2):
                        if e or j:
                            dve.wait_ge(s_wee, 2 * n + 1 if j else 2 * (n - T) + 2)
                        dve.scalar_tensor_tensor(out=tok[:, t, :], in0=bank[4 + n % 4][:, j * D:(j + 1) * D],
                                                 scalar=gate_t[:, t, 2 * e + j:2 * e + j + 1], in1=tok[:, t, :],
                                                 op0=ALU.mult, op1=ALU.add).then_inc(s_wee, 1)
                    if e == ER // 2 - 1 and t:
                        dve.wait_ge(s_wee, 2 * n)
                        tile_stats(dve, st, tok, t - 1)
                    n += 1
            dve.wait_ge(s_wee, ER * T)
            tile_stats(dve, st, tok, T - 1)
            dve_norm(dve, st, norm6m, tok, tok, measured=True)
            st.link(dve.tensor_tensor(tok[:, :, :], tok[:, :, :], per_tile_rows("L1_ffn_g2"), ALU.mult))
            st.settle()
            for t in range(T):
                dve.tensor_tensor(x[:, t, :], x[:, t, :], tok[:, t, :], ALU.add).then_inc(s_x, 1)
            dve.wait_ge(s_x, 6 * T)

        @block.gpsimd
        def _(pool):
            for n in range(len(ctx_blocks)):
                pool.wait_ge(s_ghi, n + 1)
                pool.tensor_tensor(ctx_lo[n % 2][:, :, :], ctx_sb[n % NBUF][:, :, :], ctx_hi[n % 2][:, :, 0:D],
                                   ALU.subtract).then_inc(s_glo, 1)
            pool.wait_ge(s_x, T)
            for i in range(2):
                pool.memset(v_st[i][:, :, :, :], 1.0).then_inc(s_vones, 1)
            pool.wait_ge(s_m8, 16)
            pool.tensor_scalar(m_16[:, :], m_u32[:, :].bitcast(U8), MASKED, None, ALU.mult).then_inc(s_m16, 1)
            pool.wait_ge(s_m16, 1)
            for j in range(H // GH):
                pool.dma_start(mask_scr.rearrange("(b j) n -> j b n", b=B)[j], m_16[:, :]).then_inc(s_mst, 16)

            def ctx_low(n):
                pool.wait_ge(s_chi, n + 1)
                pool.tensor_tensor(c_part[n % 2][1][:, :, :], cT[n % 3][:, :, :], c_part[n % 2][0][:, :, :],
                                   ALU.subtract).then_inc(s_clo, 1)

            ctx_low(0)
            for n in range(len(proj_blocks)):
                if n + 1 < len(proj_blocks):
                    ctx_low(n + 1)
                for m in range(KT):
                    job = 2 * n + m
                    i = job % 3
                    pool.wait_ge(s_kf, 2 * (job + 1))
                    if job >= 3:
                        pool.wait_ge(s_kst[i], 64 * (job // 3))
                    pool.tensor_tensor(k_lo[i][:, :], k_f[i][:, :], k_hi[i][:, :], ALU.subtract).then_inc(s_klo, 1)
            pool.wait_ge(s_x, 3 * T)

            def wide(ap):
                return ap.rearrange("p h n -> p (h n)").bitcast(F32)

            pool.memset(wide(kst[0][64:128, :, :]), TWO_ONES).then_inc(s_init4, 1)
            for n, q_ in enumerate((*qa, *qb)):
                pool.wait_ge(s_init4, n + 1)
                pool.memset(wide(q_[64:128, :, :]), 0.0).then_inc(s_qz, 1)
                pool.wait_ge(s_qz, n + 1)
                pool.memset(q_[R_MASK:R_MASK + 1, :, :], UNMASK_ROW).then_inc(s_init4, 1)
            pool.wait_ge(s_init4, 5)
            pool.memset(wide(kst[1][64:128, :, :]), TWO_ONES).then_inc(s_init4, 1)
            for n, sa in ((4, sa5), (5, sa6)):
                pool.wait_ge(s_x, n * T)
                pool.memset(sa.v[:, :, :, HD:HV], 1.0).then_inc(signals["rows_set"].s, 1)
                sa.wait(pool, "rows_set", 1)
                pool.memset(wide(sa.k[64:128, :, :]), TWO_ONES).then_inc(signals["rows_set"].s, 1)
                sa.wait(pool, "rows_set", 2)
                pool.memset(wide(sa.q[64:128, :, :]), 0.0).then_inc(signals["rows_set"].s, 1)


def kernel(**inputs):
    import concourse.bacc as bacc
    from concourse.bass_utils import run_bass_kernel_spmd as run

    i = {n: np.asarray(v) for n, v in inputs.items()}

    def t(name):
        return i[name].T

    pos_in_head = np.arange(P) % HD
    inv_freq = np.float32(1.0) / np.float32(10000.0) ** (np.arange(0, HD, 2, dtype=np.float32) / np.float32(HD))
    angles = np.arange(S, dtype=np.float32)[None, :] * inv_freq[pos_in_head // 2][:, None]
    signs = np.where(pos_in_head % 2 == 0, -1.0, 1.0)[:, None]
    swap = np.arange(D) ^ 1
    named = {
        **{n: i[n] for n in ("L0_xattn_Wq_b", "L0_attn_pos_proj_bias", "L0_ffn_g_shared", "L0_ffn_g_routed",
                             "L1_xattn_bq", "L1_attn_g1", "L1_attn_beta1", "L1_attn_g2", "L1_attn_beta2",
                             "L1_attn_bq", "L1_attn_bk", "L1_attn_b1", "L1_ffn_bq", "L1_ffn_bk", "L0_xattn_out_b",
                             "L0_attn_in_proj_bias", "L0_attn_out_proj_bias", "L1_xattn_bo", "L1_attn_bv",
                             "L1_attn_bo", "L1_attn_b2", "L1_ffn_bv", "L1_ffn_bo", "L1_ffn_g1", "L1_ffn_be1",
                             "L1_ffn_g2", "L1_ffn_be2", "L1_ffn_bg")},
        "bq0": i["L0_attn_in_proj_bias"][0:D],
        "L0_attn_r_r_bias": i["L0_attn_r_r_bias"].reshape(-1),
        "L0_attn_r_w_bias": i["L0_attn_r_w_bias"].reshape(-1),
        "bk_x": i["L1_xattn_bkv"][0:D],
        "bv_x": i["L1_xattn_bkv"][D:2 * D],
        "bq_swapped": i["L1_attn_bq"][swap],
        "bk_swapped": i["L1_attn_bk"][swap],
    }
    arrays = {
        "x": i["x"], "ctx": i["ctx_1024"], "ctxT": i["ctx_1024"].transpose(0, 2, 1),
        "mask": i["mask_BxS2_bk0"].view(np.uint32),
        "ident": np.eye(P, dtype=np.float32),
        "cols": np.concatenate([named[n.split(":")[0]].reshape(-1, P).T for n in COLS], axis=1),
        "rows": np.concatenate([named[n.split(":")[0]] for n in ROWS])[None, :],
        "row0": i["L0_xattn_Wq_b"][None, :], "row_in": i["L0_attn_in_proj_bias"][None, :],
        "w0qT": t("L0_xattn_Wq_w"), "w0oT": t("L0_xattn_out_w"),
        "w1inT": t("L0_attn_in_proj_weight"), "w1q": i["L0_attn_in_proj_weight"][0:D],
        "w1oT": t("L0_attn_out_proj_weight"), "w1pT": t("L0_attn_pos_proj_weight"),
        "posT": i["L0_attn_pos"][0:R0, 0, :].T,
        "head_mask": (np.arange(D)[:, None] // HD == np.arange(H)[None, :]).astype(np.float32),
        "wkv": i["L1_xattn_Wkv"], "wq_x": i["L1_xattn_Wq"], "wo_x": i["L1_xattn_Wo"],
        "cent": i["L0_ffn_centroids"],
        "b2_all": np.concatenate([i["L0_ffn_b2_r"], i["L0_ffn_b2_s"]]),
        "w1_all": np.concatenate([i["L0_ffn_W1_r"], i["L0_ffn_W1_s"]]),
        "w2_all": np.concatenate([i["L0_ffn_W2_r"], i["L0_ffn_W2_s"]]),
        "b1_all": np.concatenate([i["L0_ffn_b1_r"], i["L0_ffn_b1_s"]]).reshape(ER + ES, HM, P).transpose(0, 2, 1),
        "r_w": np.stack([i["L1_attn_Wq"], i["L1_attn_Wq"][:, swap], i["L1_attn_Wk"], i["L1_attn_Wk"][:, swap],
                         i["L1_attn_Wv"], i["L1_attn_Wo"]]),
        "r_w1": i["L1_attn_W1"], "r_w2": i["L1_attn_W2"],
        "cosT": np.cos(angles).astype(np.float32), "sinT": (np.sin(angles) * signs).astype(np.float32),
        "l_w": np.stack([i["L1_ffn_Wq"], i["L1_ffn_Wk"], i["L1_ffn_Wv"], i["L1_ffn_Wo"]]),
        "l_we": i["L1_ffn_We"].reshape(ER // 2, 2, D, D).transpose(0, 2, 1, 3).reshape(ER // 2, D, 2 * D),
        "wg": i["L1_ffn_Wg"], "bexp": i["L1_ffn_bexp"],
    }
    nc = bacc.Bacc("TRN2", target_bir_lowering=False, num_devices=1)
    held, aps = {}, {}
    for name, v in arrays.items():
        v = np.ascontiguousarray(v)
        held[f"in_{name}"] = v
        aps[name] = nc.dram_tensor(f"in_{name}", v.shape, mybir.dt.from_np(v.dtype), kind="ExternalInput").ap()
    out = nc.dram_tensor("out", (B, S, D), F32, kind="ExternalOutput").ap()
    build(nc, aps, out)
    r = run(nc, [held], core_ids=[0])
    return r.results[0]["out"]
```
